# Optimizing a Trainium2 kernel written in Bass

```python
import numpy as np
import jax
import jax.numpy as jnp

def _softmax(x, axis=-1):
    return jax.nn.softmax(x, axis=axis)

def _gelu(x):
    return jax.nn.gelu(x, approximate=True)

def _silu(x):
    return jax.nn.silu(x)

def _sigmoid(x):
    return jax.nn.sigmoid(x)

def _layernorm(x, axis=-1, eps=1e-05):
    m = jnp.mean(x, axis=axis, keepdims=True)
    v = jnp.var(x, axis=axis, keepdims=True)
    return (x - m) / jnp.sqrt(v + eps)

def _scatter_add(tgt, idx, src, axis=0):
    return tgt.at[idx].add(src)

def _segment_sum(src, seg, n):
    return jax.ops.segment_sum(src, seg, n)
kernel_name = 'mk_gps_d2_gnn_r32_f79c3d'

def setup_inputs(seed: int=0):
    np.random.seed(seed)
    _w = jnp.asarray

    def _rec_inputs():
        import jax
        import jax.numpy as jnp
        _gk = jax.random.key(seed)
        x = -8.776e-05 + 1 * jax.random.normal(jax.random.fold_in(_gk, 1), (625, 256), jnp.float32)
        src = jax.random.randint(jax.random.fold_in(_gk, 2), (20000,), 0, 625, jnp.int32)
        dst = jnp.minimum((625 * jax.random.uniform(jax.random.fold_in(_gk, 3), (20000,)) ** 2.0).astype(jnp.int32), 19999)
        _o = jnp.argsort(dst, stable=True)
        src = src[_o]
        dst = dst[_o]
        return (x, src, dst)
    x, src, dst = _rec_inputs()

    def _L0_gnn_setup():
        import jax, jax.numpy as jnp
        import numpy as np
        N = 625
        E = 20000
        F_IN = 256
        H = 4
        F_OUT = 64
        NEG_SLOPE = 0.2
        key = jax.random.key(seed)
        k = jax.random.split(key, 6)
        x = jax.random.normal(k[0], (N, F_IN), jnp.float32)
        edge_src = jax.random.randint(k[1], (E,), 0, N, jnp.int32)
        edge_dst = jax.random.randint(k[2], (E,), 0, N, jnp.int32)
        W = jax.random.normal(k[3], (H, F_IN, F_OUT), jnp.float32) * (1.0 / np.sqrt(F_IN))
        a_src = jax.random.normal(k[4], (H, F_OUT), jnp.float32) * 0.1
        a_dst = jax.random.normal(k[5], (H, F_OUT), jnp.float32) * 0.1
        return {'x': x, 'edge_src': edge_src, 'edge_dst': edge_dst, 'W': W, 'a_src': a_src, 'a_dst': a_dst}
    _L0_gnn_all = _L0_gnn_setup()
    _L0_gnn_in = {k: v for k, v in _L0_gnn_all.items() if k in ('W', 'a_src', 'a_dst')}
    del _L0_gnn_all

    def _L0_mix_setup():
        import jax, jax.numpy as jnp
        import numpy as np
        HEADS = 8
        EPS = 1e-05

        def _ln(t, w, b, headc):
            m = jnp.mean(t, axis=-1, keepdims=True)
            d = t - m
            std = jnp.sqrt(jnp.sum(d * d, axis=-1, keepdims=True) / (headc - 1))
            return w * (d / (std + EPS)) + b
        key = jax.random.key(seed)
        B, N, C = (32, 128, 256)
        headc = C // HEADS
        x = jax.random.normal(key, (B, N, C), dtype=jnp.float32)
        return {'x': x, 'kln_weight': jnp.ones((HEADS, 1, headc), dtype=jnp.float32), 'kln_bias': jnp.zeros((HEADS, 1, headc), dtype=jnp.float32), 'vln_weight': jnp.ones((HEADS, 1, headc), dtype=jnp.float32), 'vln_bias': jnp.zeros((HEADS, 1, headc), dtype=jnp.float32)}
    _L0_mix_all = _L0_mix_setup()
    _L0_mix_in = {k: v for k, v in _L0_mix_all.items() if k in ('kln_weight', 'kln_bias', 'vln_weight', 'vln_bias')}
    del _L0_mix_all

    def _L0_ffn_setup():
        import jax, jax.numpy as jnp
        import numpy as np
        BN_EPS = 0.001

        def _bn(h, g, b, m, v):
            return g * (h - m) * jax.lax.rsqrt(v + BN_EPS) + b
        key = jax.random.key(seed)
        ks = jax.random.split(key, 8)
        B, F, Df = (256, 64, 256)
        E, H, D = (8, 256, 256)
        s1 = 1.0 / np.sqrt(Df)
        s2 = 1.0 / np.sqrt(H)
        return {'x': jax.random.normal(ks[0], (B, F, Df), jnp.float32), 'Wr': jax.random.normal(ks[1], (Df, E), jnp.float32) * s1, 'br': jnp.zeros((E,), jnp.float32), 'W1': jax.random.normal(ks[2], (E, Df, H), jnp.float32) * s1, 'b1': jnp.zeros((E, H), jnp.float32), 'g1': jnp.ones((E, H), jnp.float32), 'be1': jnp.zeros((E, H), jnp.float32), 'm1': jnp.zeros((E, H), jnp.float32), 'v1': jnp.ones((E, H), jnp.float32), 'W2': jax.random.normal(ks[3], (E, H, H), jnp.float32) * s2, 'b2': jnp.zeros((E, H), jnp.float32), 'g2': jnp.ones((E, H), jnp.float32), 'be2': jnp.zeros((E, H), jnp.float32), 'm2': jnp.zeros((E, H), jnp.float32), 'v2': jnp.ones((E, H), jnp.float32), 'Wo': jax.random.normal(ks[4], (E, H, D), jnp.float32) * s2, 'bo': jnp.zeros((E, D), jnp.float32)}
    _L0_ffn_all = _L0_ffn_setup()
    _L0_ffn_in = {k: v for k, v in _L0_ffn_all.items() if k in ('Wr', 'br', 'W1', 'b1', 'g1', 'be1', 'm1', 'v1', 'W2', 'b2', 'g2', 'be2', 'm2', 'v2', 'Wo', 'bo')}
    del _L0_ffn_all

    def _L1_gnn_setup():
        import jax, jax.numpy as jnp
        import numpy as np
        N = 3125
        E = 25000
        D_IN = 256
        D_H = 512

        def _gcn_prep(edge_index, n_nodes):
            loop = jnp.arange(n_nodes, dtype=edge_index.dtype)
            row = jnp.concatenate([edge_index[0], loop])
            col = jnp.concatenate([edge_index[1], loop])
            deg = jax.ops.segment_sum(jnp.ones_like(row, dtype=jnp.float32), row, num_segments=n_nodes)
            dinv = jax.lax.rsqrt(deg)
            norm = dinv[row] * dinv[col]
            return (row, col, norm)

        def _gcn_conv(x, W, b, row, col, norm, n_nodes):
            h = x @ W
            msg = h[col] * norm[:, None]
            out = jax.ops.segment_sum(msg, row, num_segments=n_nodes)
            return out + b
        key = jax.random.key(seed)
        ks = jax.random.split(key, 8)
        s_in = 1.0 / np.sqrt(D_IN)
        s_h = 1.0 / np.sqrt(D_H)
        return {'x': jax.random.normal(ks[0], (N, D_IN), jnp.float32), 'edge_index': jax.random.randint(ks[1], (2, E), 0, N, dtype=jnp.int64), 'W1': jax.random.normal(ks[2], (D_IN, D_H), jnp.float32) * s_in, 'b1': jnp.zeros((D_H,), jnp.float32), 'W2': jax.random.normal(ks[3], (D_H, D_H), jnp.float32) * s_h, 'b2': jnp.zeros((D_H,), jnp.float32), 'W3': jax.random.normal(ks[4], (D_H, D_H), jnp.float32) * s_h, 'b3': jnp.zeros((D_H,), jnp.float32), 'Wfc': jax.random.normal(ks[5], (D_H, D_IN), jnp.float32) * s_h, 'bfc': jnp.zeros((D_IN,), jnp.float32)}
    _L1_gnn_all = _L1_gnn_setup()
    _L1_gnn_in = {k: v for k, v in _L1_gnn_all.items() if k in ('W1', 'b1', 'W2', 'b2', 'W3', 'b3', 'Wfc', 'bfc')}
    del _L1_gnn_all

    def _L1_mix_setup():
        import jax, jax.numpy as jnp
        import numpy as np
        B, S, D = (8, 64, 256)
        H, KD = (8, 256)
        M = 256
        EPS_LN = 1e-06
        EPS_ATT = 1e-06

        def _layernorm(x, g, b):
            mu = jnp.mean(x, axis=-1, keepdims=True)
            var = jnp.mean(jnp.square(x - mu), axis=-1, keepdims=True)
            return (x - mu) * jax.lax.rsqrt(var + EPS_LN) * g + b

        def _phi(x, proj):
            u = jnp.einsum('bshd,md->bshm', x, proj)
            sq = 0.5 * jnp.sum(jnp.square(x), axis=-1, keepdims=True)
            return jnp.exp(u - sq) * (1.0 / np.sqrt(M)) + EPS_ATT
        key = jax.random.key(seed)
        ks = jax.random.split(key, 16)
        sd = lambda *s: 1.0 / np.sqrt(s[0])
        return {'inputs': jax.random.normal(ks[0], (B, S, D), dtype=jnp.float32), 'Wq': jax.random.normal(ks[1], (D, H, KD), jnp.float32) * sd(D), 'bq': jnp.zeros((H, KD), jnp.float32), 'Wk': jax.random.normal(ks[2], (D, H, KD), jnp.float32) * sd(D), 'bk': jnp.zeros((H, KD), jnp.float32), 'Wv': jax.random.normal(ks[3], (D, H, KD), jnp.float32) * sd(D), 'bv': jnp.zeros((H, KD), jnp.float32), 'Wo': jax.random.normal(ks[4], (H, KD, D), jnp.float32) * sd(H * KD), 'bo': jnp.zeros((D,), jnp.float32), 'proj': jax.random.normal(ks[5], (M, KD), jnp.float32), 'W1': jax.random.normal(ks[6], (D, D), jnp.float32) * sd(D), 'bias1': jnp.zeros((D,), jnp.float32), 'W2': jax.random.normal(ks[7], (D, D), jnp.float32) * sd(D), 'bias2': jnp.zeros((D,), jnp.float32), 'g1': jnp.ones((D,), jnp.float32), 'beta1': jnp.zeros((D,), jnp.float32), 'g2': jnp.ones((D,), jnp.float32), 'beta2': jnp.zeros((D,), jnp.float32)}
    _L1_mix_all = _L1_mix_setup()
    _L1_mix_in = {k: v for k, v in _L1_mix_all.items() if k in ('Wq', 'bq', 'Wk', 'bk', 'Wv', 'bv', 'Wo', 'bo', 'proj', 'W1', 'bias1', 'W2', 'bias2', 'g1', 'beta1', 'g2', 'beta2')}
    del _L1_mix_all

    def _L1_ffn_setup():
        import jax, jax.numpy as jnp
        import numpy as np
        E, D, H, TOP_K = (6, 256, 256, 2)
        ROUTER_H = D // 2
        key = jax.random.key(seed)
        ks = jax.random.split(key, 12)
        s = 1.0 / np.sqrt(D)
        sh = 1.0 / np.sqrt(H)
        sr = 1.0 / np.sqrt(ROUTER_H)
        return {'features': jax.random.normal(ks[0], (8, 128, D), dtype=jnp.float32), 'router_w1': jax.random.uniform(ks[1], (D, ROUTER_H), jnp.float32, -s, s), 'router_b1': jnp.zeros((ROUTER_H,), jnp.float32), 'router_w2': jax.random.uniform(ks[2], (ROUTER_H, E), jnp.float32, -sr, sr), 'router_b2': jnp.zeros((E,), jnp.float32), 'expert_w1': jax.random.uniform(ks[3], (E, D, H), jnp.float32, -s, s), 'expert_b1': jnp.zeros((E, H), jnp.float32), 'expert_w2': jax.random.uniform(ks[4], (E, H, H), jnp.float32, -sh, sh), 'expert_b2': jnp.zeros((E, H), jnp.float32), 'expert_w3': jax.random.uniform(ks[5], (E, H, D), jnp.float32, -sh, sh), 'expert_b3': jnp.zeros((E, D), jnp.float32)}
    _L1_ffn_all = _L1_ffn_setup()
    _L1_ffn_in = {k: v for k, v in _L1_ffn_all.items() if k in ('router_w1', 'router_b1', 'router_w2', 'router_b2', 'expert_w1', 'expert_b1', 'expert_w2', 'expert_b2', 'expert_w3', 'expert_b3')}
    del _L1_ffn_all
    return {'x': x, 'src': src, 'dst': dst, 'L0_gnn_W': _L0_gnn_in['W'], 'L0_gnn_a_src': _L0_gnn_in['a_src'], 'L0_gnn_a_dst': _L0_gnn_in['a_dst'], 'L0_mix_kln_weight': _L0_mix_in['kln_weight'], 'L0_mix_kln_bias': _L0_mix_in['kln_bias'], 'L0_mix_vln_weight': _L0_mix_in['vln_weight'], 'L0_mix_vln_bias': _L0_mix_in['vln_bias'], 'L0_ffn_Wr': _L0_ffn_in['Wr'], 'L0_ffn_br': _L0_ffn_in['br'], 'L0_ffn_W1': _L0_ffn_in['W1'], 'L0_ffn_b1': _L0_ffn_in['b1'], 'L0_ffn_g1': _L0_ffn_in['g1'], 'L0_ffn_be1': _L0_ffn_in['be1'], 'L0_ffn_m1': _L0_ffn_in['m1'], 'L0_ffn_v1': _L0_ffn_in['v1'], 'L0_ffn_W2': _L0_ffn_in['W2'], 'L0_ffn_b2': _L0_ffn_in['b2'], 'L0_ffn_g2': _L0_ffn_in['g2'], 'L0_ffn_be2': _L0_ffn_in['be2'], 'L0_ffn_m2': _L0_ffn_in['m2'], 'L0_ffn_v2': _L0_ffn_in['v2'], 'L0_ffn_Wo': _L0_ffn_in['Wo'], 'L0_ffn_bo': _L0_ffn_in['bo'], 'L1_gnn_W1': _L1_gnn_in['W1'], 'L1_gnn_b1': _L1_gnn_in['b1'], 'L1_gnn_W2': _L1_gnn_in['W2'], 'L1_gnn_b2': _L1_gnn_in['b2'], 'L1_gnn_W3': _L1_gnn_in['W3'], 'L1_gnn_b3': _L1_gnn_in['b3'], 'L1_gnn_Wfc': _L1_gnn_in['Wfc'], 'L1_gnn_bfc': _L1_gnn_in['bfc'], 'L1_mix_Wq': _L1_mix_in['Wq'], 'L1_mix_bq': _L1_mix_in['bq'], 'L1_mix_Wk': _L1_mix_in['Wk'], 'L1_mix_bk': _L1_mix_in['bk'], 'L1_mix_Wv': _L1_mix_in['Wv'], 'L1_mix_bv': _L1_mix_in['bv'], 'L1_mix_Wo': _L1_mix_in['Wo'], 'L1_mix_bo': _L1_mix_in['bo'], 'L1_mix_proj': _L1_mix_in['proj'], 'L1_mix_W1': _L1_mix_in['W1'], 'L1_mix_bias1': _L1_mix_in['bias1'], 'L1_mix_W2': _L1_mix_in['W2'], 'L1_mix_bias2': _L1_mix_in['bias2'], 'L1_mix_g1': _L1_mix_in['g1'], 'L1_mix_beta1': _L1_mix_in['beta1'], 'L1_mix_g2': _L1_mix_in['g2'], 'L1_mix_beta2': _L1_mix_in['beta2'], 'L1_ffn_router_w1': _L1_ffn_in['router_w1'], 'L1_ffn_router_b1': _L1_ffn_in['router_b1'], 'L1_ffn_router_w2': _L1_ffn_in['router_w2'], 'L1_ffn_router_b2': _L1_ffn_in['router_b2'], 'L1_ffn_expert_w1': _L1_ffn_in['expert_w1'], 'L1_ffn_expert_b1': _L1_ffn_in['expert_b1'], 'L1_ffn_expert_w2': _L1_ffn_in['expert_w2'], 'L1_ffn_expert_b2': _L1_ffn_in['expert_b2'], 'L1_ffn_expert_w3': _L1_ffn_in['expert_w3'], 'L1_ffn_expert_b3': _L1_ffn_in['expert_b3']}

def reference(x, src, dst, L0_gnn_W, L0_gnn_a_src, L0_gnn_a_dst, L0_mix_kln_weight, L0_mix_kln_bias, L0_mix_vln_weight, L0_mix_vln_bias, L0_ffn_Wr, L0_ffn_br, L0_ffn_W1, L0_ffn_b1, L0_ffn_g1, L0_ffn_be1, L0_ffn_m1, L0_ffn_v1, L0_ffn_W2, L0_ffn_b2, L0_ffn_g2, L0_ffn_be2, L0_ffn_m2, L0_ffn_v2, L0_ffn_Wo, L0_ffn_bo, L1_gnn_W1, L1_gnn_b1, L1_gnn_W2, L1_gnn_b2, L1_gnn_W3, L1_gnn_b3, L1_gnn_Wfc, L1_gnn_bfc, L1_mix_Wq, L1_mix_bq, L1_mix_Wk, L1_mix_bk, L1_mix_Wv, L1_mix_bv, L1_mix_Wo, L1_mix_bo, L1_mix_proj, L1_mix_W1, L1_mix_bias1, L1_mix_W2, L1_mix_bias2, L1_mix_g1, L1_mix_beta1, L1_mix_g2, L1_mix_beta2, L1_ffn_router_w1, L1_ffn_router_b1, L1_ffn_router_w2, L1_ffn_router_b2, L1_ffn_expert_w1, L1_ffn_expert_b1, L1_ffn_expert_w2, L1_ffn_expert_b2, L1_ffn_expert_w3, L1_ffn_expert_b3):
    import jax
    import jax.numpy as jnp

    def _L0_gnn_ref(x, edge_src, edge_dst, W, a_src, a_dst):
        import jax, jax.numpy as jnp
        import numpy as np
        N = 625
        E = 20000
        F_IN = 256
        H = 4
        F_OUT = 64
        NEG_SLOPE = 0.2
        h = jnp.einsum('nf,hfo->nho', x, W)
        e_s = jnp.einsum('nho,ho->nh', h, a_src)
        e_d = jnp.einsum('nho,ho->nh', h, a_dst)
        scores = jax.nn.leaky_relu(e_s[edge_src] + e_d[edge_dst], NEG_SLOPE)
        m = jax.ops.segment_max(scores, edge_dst, num_segments=N)
        m = jnp.where(jnp.isfinite(m), m, 0.0)
        ex = jnp.exp(scores - m[edge_dst])
        denom = jax.ops.segment_sum(ex, edge_dst, num_segments=N)
        alpha = ex / jnp.maximum(denom[edge_dst], 1e-09)
        msg = alpha[:, :, None] * h[edge_src]
        agg = jax.ops.segment_sum(msg, edge_dst, num_segments=N)
        return jax.nn.relu(agg).reshape(N, H * F_OUT)

    def _L0_mix_ref(x, kln_weight, kln_bias, vln_weight, vln_bias):
        import jax, jax.numpy as jnp
        import numpy as np
        HEADS = 8
        EPS = 1e-05

        def _ln(t, w, b, headc):
            m = jnp.mean(t, axis=-1, keepdims=True)
            d = t - m
            std = jnp.sqrt(jnp.sum(d * d, axis=-1, keepdims=True) / (headc - 1))
            return w * (d / (std + EPS)) + b
        B, N, C = x.shape
        headc = C // HEADS
        qkv = x.reshape(B, N, HEADS, headc).transpose(0, 2, 1, 3)
        k = _ln(qkv, kln_weight, kln_bias, headc)
        v = _ln(qkv, vln_weight, vln_bias, headc)
        kv = jnp.einsum('bhnd,bhne->bhde', k, v) / N
        out = jnp.einsum('bhnd,bhde->bhne', qkv, kv)
        out = out.transpose(0, 2, 1, 3).reshape(B, N, C)
        return out + x

    def _L0_ffn_ref(x, Wr, br, W1, b1, g1, be1, m1, v1, W2, b2, g2, be2, m2, v2, Wo, bo):
        import jax, jax.numpy as jnp
        import numpy as np
        BN_EPS = 0.001

        def _bn(h, g, b, m, v):
            return g * (h - m) * jax.lax.rsqrt(v + BN_EPS) + b
        feat = jnp.mean(x, axis=0)
        w = jax.nn.softmax(feat @ Wr + br, axis=-1)
        h = jnp.einsum('bfd,edh->bfeh', x, W1) + b1
        h = jax.nn.relu(_bn(h, g1, be1, m1, v1))
        h = jnp.einsum('bfeh,ehk->bfek', h, W2) + b2
        h = jax.nn.relu(_bn(h, g2, be2, m2, v2))
        y = jnp.einsum('bfeh,ehd->bfed', h, Wo) + bo
        return jnp.einsum('bfed,fe->bfd', y, w)

    def _L1_gnn_ref(x, edge_index, W1, b1, W2, b2, W3, b3, Wfc, bfc):
        import jax, jax.numpy as jnp
        import numpy as np
        N = 3125
        E = 25000
        D_IN = 256
        D_H = 512

        def _gcn_prep(edge_index, n_nodes):
            loop = jnp.arange(n_nodes, dtype=edge_index.dtype)
            row = jnp.concatenate([edge_index[0], loop])
            col = jnp.concatenate([edge_index[1], loop])
            deg = jax.ops.segment_sum(jnp.ones_like(row, dtype=jnp.float32), row, num_segments=n_nodes)
            dinv = jax.lax.rsqrt(deg)
            norm = dinv[row] * dinv[col]
            return (row, col, norm)

        def _gcn_conv(x, W, b, row, col, norm, n_nodes):
            h = x @ W
            msg = h[col] * norm[:, None]
            out = jax.ops.segment_sum(msg, row, num_segments=n_nodes)
            return out + b
        n = x.shape[0]
        row, col, norm = _gcn_prep(edge_index, n)
        h = jax.nn.relu(_gcn_conv(x, W1, b1, row, col, norm, n))
        h = jax.nn.relu(_gcn_conv(h, W2, b2, row, col, norm, n))
        h = jax.nn.relu(_gcn_conv(h, W3, b3, row, col, norm, n))
        return h @ Wfc + bfc

    def _L1_mix_ref(inputs, Wq, bq, Wk, bk, Wv, bv, Wo, bo, proj, W1, bias1, W2, bias2, g1, beta1, g2, beta2):
        import jax, jax.numpy as jnp
        import numpy as np
        B, S, D = (8, 64, 256)
        H, KD = (8, 256)
        M = 256
        EPS_LN = 1e-06
        EPS_ATT = 1e-06

        def _layernorm(x, g, b):
            mu = jnp.mean(x, axis=-1, keepdims=True)
            var = jnp.mean(jnp.square(x - mu), axis=-1, keepdims=True)
            return (x - mu) * jax.lax.rsqrt(var + EPS_LN) * g + b

        def _phi(x, proj):
            u = jnp.einsum('bshd,md->bshm', x, proj)
            sq = 0.5 * jnp.sum(jnp.square(x), axis=-1, keepdims=True)
            return jnp.exp(u - sq) * (1.0 / np.sqrt(M)) + EPS_ATT
        scale = KD ** (-0.25)
        q = (jnp.einsum('bsd,dhk->bshk', inputs, Wq) + bq) * scale
        k = (jnp.einsum('bsd,dhk->bshk', inputs, Wk) + bk) * scale
        v = jnp.einsum('bsd,dhk->bshk', inputs, Wv) + bv
        phi_q = _phi(q, proj)
        phi_k = _phi(k, proj)
        kv = jnp.einsum('bshm,bshk->bhmk', phi_k, v)
        z = jnp.einsum('bshm,bhm->bsh', phi_q, phi_k.sum(axis=1))
        attn = jnp.einsum('bshm,bhmk->bshk', phi_q, kv) / z[..., None]
        attn_out = jnp.einsum('bshk,hkd->bsd', attn, Wo) + bo
        out1 = _layernorm(inputs + attn_out, g1, beta1)
        h = jax.nn.relu(out1 @ W1 + bias1)
        ffn_out = h @ W2 + bias2
        return _layernorm(out1 + ffn_out, g2, beta2)

    def _L1_ffn_ref(features, router_w1, router_b1, router_w2, router_b2, expert_w1, expert_b1, expert_w2, expert_b2, expert_w3, expert_b3):
        import jax, jax.numpy as jnp
        import numpy as np
        E, D, H, TOP_K = (6, 256, 256, 2)
        ROUTER_H = D // 2
        rh = jax.nn.relu(features @ router_w1 + router_b1)
        expert_logits = jax.nn.softmax(rh @ router_w2 + router_b2, axis=-1)
        top_w, top_i = jax.lax.top_k(expert_logits, TOP_K)
        routing_weights = jax.nn.softmax(top_w, axis=-1)
        h1 = jax.nn.relu(jnp.einsum('bsd,edh->bseh', features, expert_w1) + expert_b1)
        h2 = jax.nn.relu(jnp.einsum('bseh,ehf->bsef', h1, expert_w2) + expert_b2)
        expert_out = jnp.einsum('bsef,efo->bseo', h2, expert_w3) + expert_b3
        sel = jnp.take_along_axis(expert_out, top_i[:, :, :, None], axis=2)
        combined = jnp.sum(sel * routing_weights[..., None], axis=2)
        return combined
    edge_index = jnp.stack([src, dst])
    xn = _layernorm(x, axis=-1)
    x = x + _L0_gnn_ref(xn, src, dst, L0_gnn_W, L0_gnn_a_src, L0_gnn_a_dst) + _L0_mix_ref(xn[None], L0_mix_kln_weight, L0_mix_kln_bias, L0_mix_vln_weight, L0_mix_vln_bias)[0]
    x = x + _L0_ffn_ref(_layernorm(x, axis=-1)[None], L0_ffn_Wr, L0_ffn_br, L0_ffn_W1, L0_ffn_b1, L0_ffn_g1, L0_ffn_be1, L0_ffn_m1, L0_ffn_v1, L0_ffn_W2, L0_ffn_b2, L0_ffn_g2, L0_ffn_be2, L0_ffn_m2, L0_ffn_v2, L0_ffn_Wo, L0_ffn_bo)[0]
    xn = _layernorm(x, axis=-1)
    x = x + _L1_gnn_ref(xn, edge_index, L1_gnn_W1, L1_gnn_b1, L1_gnn_W2, L1_gnn_b2, L1_gnn_W3, L1_gnn_b3, L1_gnn_Wfc, L1_gnn_bfc) + _L1_mix_ref(xn[None], L1_mix_Wq, L1_mix_bq, L1_mix_Wk, L1_mix_bk, L1_mix_Wv, L1_mix_bv, L1_mix_Wo, L1_mix_bo, L1_mix_proj, L1_mix_W1, L1_mix_bias1, L1_mix_W2, L1_mix_bias2, L1_mix_g1, L1_mix_beta1, L1_mix_g2, L1_mix_beta2)[0]
    x = x + _L1_ffn_ref(_layernorm(x, axis=-1)[None], L1_ffn_router_w1, L1_ffn_router_b1, L1_ffn_router_w2, L1_ffn_router_b2, L1_ffn_expert_w1, L1_ffn_expert_b1, L1_ffn_expert_w2, L1_ffn_expert_b2, L1_ffn_expert_w3, L1_ffn_expert_b3)[0]
    return x

_drawn_inputs = setup_inputs


def setup_inputs(seed=0):
    import zlib

    import numpy as np

    out = dict(_drawn_inputs(seed))
    spreads = {'L0_mix_kln_weight': (1.0, 0.2),
     'L0_mix_kln_bias': (0.0, 0.416),
     'L0_mix_vln_weight': (1.0, 0.2),
     'L0_mix_vln_bias': (0.0, 0.404),
     'L0_ffn_br': (0.0, 0.654),
     'L0_ffn_b1': (0.0, 0.8),
     'L0_ffn_g1': (1.0, 0.6),
     'L0_ffn_be1': (0.0, 0.8),
     'L0_ffn_m1': (0.0, 0.8),
     'L0_ffn_v1': (1.0, 0.6),
     'L0_ffn_b2': (0.0, 0.624),
     'L0_ffn_g2': (1.0, 0.6),
     'L0_ffn_be2': (0.0, 0.642),
     'L0_ffn_m2': (0.0, 0.649),
     'L0_ffn_v2': (1.0, 0.6),
     'L0_ffn_bo': (0.0, 0.471),
     'L1_gnn_b1': (0.0, 0.8),
     'L1_gnn_b2': (0.0, 0.654),
     'L1_gnn_b3': (0.0, 0.483),
     'L1_gnn_bfc': (0.0, 0.28),
     'L1_mix_bq': (0.0, 0.407),
     'L1_mix_bk': (0.0, 1.221),
     'L1_mix_bv': (0.0, 0.319),
     'L1_mix_bo': (0.0, 0.322),
     'L1_mix_bias1': (0.0, 0.55),
     'L1_mix_bias2': (0.0, 0.387),
     'L1_mix_g1': (1.0, 0.558),
     'L1_mix_beta1': (0.0, 0.837),
     'L1_mix_g2': (1.0, 0.548),
     'L1_mix_beta2': (0.0, 0.317),
     'L1_ffn_router_b1': (0.0, 0.599),
     'L1_ffn_router_b2': (0.0, 0.674),
     'L1_ffn_expert_b1': (0.0, 0.8),
     'L1_ffn_expert_b2': (0.0, 0.8),
     'L1_ffn_expert_b3': (0.0, 1.942)}
    factors = {'L0_gnn_a_dst': 63.643,
     'L1_gnn_W1': 8.0,
     'L1_gnn_W2': 4.898,
     'L1_gnn_W3': 3.458,
     'L1_ffn_expert_w1': 4.322,
     'L1_ffn_expert_w2': 3.675,
     'L1_ffn_expert_w3': 2.82}
    for name, (base, spread) in spreads.items():
        noise = np.random.default_rng([zlib.crc32(name.encode()), seed]).standard_normal(out[name].shape)
        drawn = base * np.exp(spread * noise) if base else spread * noise
        out[name] = jnp.asarray(drawn.astype(out[name].dtype))
    for name, factor in factors.items():
        out[name] = (out[name] * factor).astype(out[name].dtype)
    return out
```

```python
from contextlib import ExitStack

import numpy as np

import concourse.bass as bass
from concourse import mybir

F32 = mybir.dt.float32
F16 = mybir.dt.float16
F32R = mybir.dt.float32r
BF16 = mybir.dt.bfloat16
I32 = mybir.dt.int32
ALU = mybir.AluOpType
ACT = mybir.ActivationFunctionType
AX = mybir.AxisListType

N = 625
R = 125
T = N // R
D = 256
P = 128
KB = D // P
NF = 628
CH = NF // 2
NE = 20000
EP = 125
CHUNKS = NE // EP
BANK = 512

LO = 313
HI = N - LO
FIELD = 12
GROUP = 32
GROUPS = CHUNKS // GROUP
UNROLL = 5
assert GROUP * EP < 2 ** FIELD and (GROUP - 2) % UNROLL == 0 and GROUPS * GROUP == CHUNKS

PASSES = ((0, 0), (1, 0), (0, 1))

GH, GO = 4, 64
LEAK = 0.2
NONE = -1e30
MH, MO = 8, 32


class Own:

    def __init__(self, eng, sem):
        self.eng, self.sem, self.count = eng, sem, 0

    def add(self, instruction):
        self.count += 1
        instruction.then_inc(self.sem, 1)

    def settle(self):
        self.eng.wait_ge(self.sem, self.count)


class Scope:

    def __init__(self, nc, ctx, part):
        self.nc, self.ctx, self.part = nc, ctx, part

    def sb(self, name, shape, dt=F32):
        return self.ctx.enter_context(self.nc.sbuf_tensor(f"{self.part}_{name}", shape, dt))

    def parts(self, name, shape):
        return self.sb(name + "_hi", shape, F32R), self.sb(name + "_lo", shape, F32R)

    def ps(self, name, shape):
        return self.ctx.enter_context(self.nc.psum_tensor(f"{self.part}_{name}", shape, F32))

    def sem(self, name):
        return self.ctx.enter_context(self.nc.semaphore(f"{self.part}_{name}"))


def rows(ap):
    return ap.rearrange("(t p) d -> p t d", p=R)


def spread(ap, n):
    return ap.rearrange("(a d) -> a d", a=1).to_broadcast([n, ap.shape[0]])


def halves(ap):
    return ap.rearrange("p (c n) -> p c n", c=2)


def rest(engine, parts, whole, at=()):
    hi, lo = parts
    at = at or slice(None)
    return engine.tensor_tensor(lo[at], whole[at], hi[at].bitcast(F32), ALU.subtract)


def normalize(nc, own, w, nth, src, dst, done):
    for t in range(T):
        own.add(nc.vector.bn_stats(w.stats[:, t, :], src[:, t, :]))
    own.settle()
    for t in range(T):
        ins = nc.vector.bn_aggr(w.mv[:, t, :], w.stats[:, t, :])
    ins.then_inc(w.var_ready, 1)
    own.eng.wait_ge(w.rstd_ready, nth + 1)
    for t in range(T):
        nc.vector.tensor_scalar(dst[:, t, :], src[:, t, :], w.mv[:, t, 0:1], w.rstd[:, t:t + 1],
                                ALU.subtract, ALU.mult).then_inc(done, 1)


def deviation(nc, own, w, nth, eps):
    own.eng.wait_ge(w.var_ready, nth + 1)
    own.add(nc.gpsimd.tensor_single_scalar(w.rstd[:], w.mv[:, :, 1], eps, ALU.add))
    own.settle()
    nc.gpsimd.tensor_tensor(w.rstd[:], w.rstd[:], w.minus_half[:], ALU.pow).then_inc(w.rstd_ready, 1)


def count_edges_and_mix(nc, inp, g):
    with ExitStack() as ctx:
        a = Scope(nc, ctx, "count")
        dst_i, src_i = a.sb("dst_i", [EP, CHUNKS], I32), a.sb("src_i", [EP, CHUNKS], I32)
        dst_f, src_f = a.sb("dst_f", [EP, CHUNKS]), a.sb("src_f", [EP, CHUNKS])
        in_high, field, column = (a.sb(n, [EP, CHUNKS]) for n in ("in_high", "field", "column"))
        node_no = a.sb("node_no", [EP, N + 1], F16)
        hot_dst = a.sb("hot_dst", [EP, GROUP, N + 1], BF16)
        hot_src = a.sb("hot_src", [EP, GROUP, LO + 1], BF16)
        packed = a.sb("packed", [R, 2, T, LO], I32)
        total = a.sb("total", [R, T, N], I32)
        total_lo, total_hi = total[:, :, 0:LO], total[:, :, LO:N]
        low, high = a.sb("low", [R, T, LO], I32), a.sb("high", [R, T, LO], I32)
        w_gat = a.sb("w_gat", [P, KB, GH, GO])
        av_src, av_dst = a.sb("av_src", [R, GH, GO]), a.sb("av_dst", [R, GH, GO])
        ln_w = [a.sb(f"mix_ln{i}", [R, D]) for i in range(4)]
        prod = a.sb("prod", [R, T, GH, GO])
        mean = a.sb("mean", [R, T, MH])
        dev, sq = a.sb("dev", [R, T, MH, MO]), a.sb("sq", [R, T, MH, MO])
        var, half = a.sb("var", [R, T, MH]), a.sb("half", [R, T, MH])
        key, val = a.sb("key", [R, T, D]), a.sb("val", [R, T, D])
        kv = a.sb("kv", [P, KB, P])

        cnt = [a.ps(f"cnt{t}", [P, BANK]) for t in range(T)]
        aux = [a.ps(f"aux{i}", [P, BANK]) for i in range(3)]

        x_in, edges_in, gat_in, mix_in = (a.sem(n) for n in ("x_in", "edges_in", "gat_in", "mix_in"))
        consts, zeros = a.sem("consts"), a.sem("zeros")
        hot, hot_used, counted, unloaded, decoded, summed = (
            a.sem(n) for n in ("hot", "hot_used", "counted", "unloaded", "decoded", "summed"))
        vec = a.sem("vec")
        xn_ready, xt_mm, xt_ready, h_mm, h_ready = (a.sem(n) for n in ("xn_ready", "xt_mm", "xt_ready", "h_mm", "h_ready"))
        dev_ready, sq_ready, kv_in, kv_ready, kv_mm, kv_block, out_mm, base = (
            a.sem(n) for n in ("dev_ready", "sq_ready", "kv_in", "kv_ready", "kv_mm", "kv_block", "out_mm", "base"))
        dn_ready, pool = a.sem("dn_ready"), a.sem("pool")
        block = ctx.enter_context(nc.Block())

        @block.sync
        def _(sp):
            sp.dma_start(dst_i[:], inp["dst"].rearrange("(p c) -> p c", p=EP)).then_inc(edges_in, 16)
            sp.dma_start(src_i[:], inp["src"].rearrange("(p c) -> p c", p=EP)).then_inc(edges_in, 16)
            sp.dma_start(g.x[:], rows(inp["x"])).then_inc(x_in, 16)
            for k in range(KB):
                sp.dma_start(w_gat[:, k], inp["L0_gnn_W"][:, k * P:(k + 1) * P, :].rearrange("h p o -> p h o")).then_inc(gat_in, 16)
            sp.dma_start(av_src[:].rearrange("p h o -> p (h o)"), spread(inp["L0_gnn_a_src"].rearrange("h o -> (h o)"), R)).then_inc(gat_in, 16)
            sp.dma_start(av_dst[:].rearrange("p h o -> p (h o)"), spread(inp["L0_gnn_a_dst"].rearrange("h o -> (h o)"), R)).then_inc(gat_in, 16)
            for i, n in enumerate(("kln_weight", "kln_bias", "vln_weight", "vln_bias")):
                sp.dma_start(ln_w[i][:], spread(inp["L0_mix_" + n].rearrange("h a o -> (h a o)"), R)).then_inc(mix_in, 16)

        @block.gpsimd
        def _(pool_eng):
            own = Own(pool_eng, pool)
            nc.gpsimd.iota(node_no[:], [[1, N + 1]], base=0, channel_multiplier=0,
                           allow_small_or_imprecise_dtypes=True).then_inc(consts, 1)
            nc.gpsimd.memset(g.ones[:], 1.0).then_inc(consts, 1)
            pool_eng.wait_ge(consts, 2)
            nc.gpsimd.affine_select(out=g.ident[:], in_=g.ones[:], compare_op=ALU.is_equal, fill=0.0, base=0,
                                    pattern=[[-1, P]], channel_multiplier=1).then_inc(consts, 1)
            nc.gpsimd.memset(kv[:], 0.0).then_inc(zeros, 1)
            nc.gpsimd.memset(g.xT[:, :, N:NF], 0.0).then_inc(zeros, 1)
            nc.gpsimd.memset(g.edges[:, :, N:NF], 0.0).then_inc(zeros, 1)
            nc.gpsimd.memset(g.edgesT[:, :, N:NF], 0.0).then_inc(zeros, 1)
            nc.gpsimd.memset(g.h[:, :, :, GO:GO + 1], 1.0).then_inc(zeros, 1)

            def add_counts(n):
                pool_eng.wait_ge(decoded, n + 1)
                if n >= 2:
                    pool_eng.wait_ge(summed, n - 1)
                nc.gpsimd.tensor_tensor(total_lo, total_lo, low[:], ALU.add)
                nc.gpsimd.tensor_tensor(total_hi, total_hi, high[:, :, 0:HI], ALU.add).then_inc(summed, 1)

            own.add(nc.gpsimd.memset(g.minus_half[:], -0.5))
            own.add(nc.gpsimd.memset(half[:], 0.5))
            deviation(nc, own, g, 0, 1e-5)
            pool_eng.wait_ge(xn_ready, T)
            nc.gpsimd.tensor_tensor(g.x1[:], g.x[:], g.xn[:], ALU.add).then_inc(base, 1)
            pool_eng.wait_ge(sq_ready, 1)
            own.add(nc.gpsimd.tensor_single_scalar(var[:], var[:], 1.0 / (MO - 1), ALU.mult))
            own.settle()
            own.add(nc.gpsimd.tensor_tensor(var[:], var[:], half[:], ALU.pow))
            own.settle()
            nc.gpsimd.tensor_single_scalar(var[:], var[:], 1e-5, ALU.add).then_inc(dev_ready, 1)
            pool_eng.wait_ge(dn_ready, 1)
            pool_eng.wait_ge(mix_in, 64)
            flat = dev[:].rearrange("p t h o -> p t (h o)")
            for wt, bias, to in ((ln_w[0], ln_w[1], key), (ln_w[2], ln_w[3], val)):
                own.add(nc.gpsimd.tensor_tensor(to[:], flat, wt[:].unsqueeze(1).to_broadcast([R, T, D]), ALU.mult))
            own.settle()
            for wt, bias, to in ((ln_w[0], ln_w[1], key), (ln_w[2], ln_w[3], val)):
                nc.gpsimd.tensor_tensor(to[:], to[:], bias[:].unsqueeze(1).to_broadcast([R, T, D]), ALU.add).then_inc(kv_in, 1)
            for n in range(1, GROUPS):
                add_counts(n)

        @block.vector
        def _(dve):
            own = Own(dve, vec)
            dve.wait_ge(edges_in, 32)
            own.add(nc.vector.tensor_copy(dst_f[:], dst_i[:]))
            own.add(nc.vector.tensor_copy(src_f[:], src_i[:]))
            own.settle()
            own.add(nc.vector.tensor_scalar(in_high[:], src_f[:], float(LO), None, ALU.is_ge))
            own.settle()
            own.add(nc.vector.tensor_scalar(field[:], in_high[:], float(2 ** FIELD - 1), 1.0, ALU.mult, ALU.add))
            own.add(nc.vector.scalar_tensor_tensor(column[:], in_high[:], -float(LO), src_f[:], ALU.mult, ALU.add))
            own.settle()
            dve.wait_ge(consts, 1)

            def one_hots(group, i, last=False):
                if group and last:
                    dve.wait_ge(counted, T * group)
                elif group:
                    dve.wait_ge(hot_used, i + ((GROUP - 1) * (group - 1) + 1))
                c = i + GROUP * group
                nc.vector.tensor_scalar(hot_dst[:, bass.ds(i, 1), :].rearrange("p a n -> p (a n)"), node_no[:],
                                        dst_f[:, bass.ds(c, 1)], None, ALU.is_equal)
                nc.vector.tensor_scalar(hot_src[:, bass.ds(i, 1), :].rearrange("p a n -> p (a n)"), node_no[:, 0:LO + 1],
                                        column[:, bass.ds(c, 1)], field[:, bass.ds(c, 1)], ALU.is_equal, ALU.mult).then_inc(hot, 1)

            def one_hot_group(group):
                one_hots(group, 0)
                with dve.Fori(0, (GROUP - 2) // UNROLL) as i:
                    for j in range(UNROLL):
                        one_hots(group, i * UNROLL + (j + 1))
                one_hots(group, GROUP - 1, last=True)

            def decode(group):
                dve.wait_ge(unloaded, T * (group + 1))
                if group >= 2:
                    dve.wait_ge(summed, group - 1)
                to_low, to_high = (low[:], high[:, :, 0:HI]) if group else (total_lo, total_hi)
                nc.vector.tensor_single_scalar(to_low, packed[:, group % 2], 2 ** FIELD - 1, ALU.bitwise_and)
                nc.vector.tensor_single_scalar(to_high, packed[:, group % 2, :, 0:HI], FIELD, ALU.logical_shift_right).then_inc(decoded, 1)

            one_hot_group(0)
            dve.wait_ge(x_in, 16)
            normalize(nc, own, g, 0, g.x, g.xn, xn_ready)
            one_hot_group(1)
            decode(0)
            dve.wait_ge(xn_ready, T)
            heads = g.xn[:].rearrange("p t (h o) -> p t h o", o=MO)
            own.add(nc.vector.tensor_reduce(mean[:], heads, AX.X, ALU.add))
            own.settle()
            own.add(nc.vector.tensor_single_scalar(mean[:], mean[:], 1.0 / MO, ALU.mult))
            own.settle()
            own.add(nc.vector.tensor_tensor(dev[:], heads, mean[:].unsqueeze(3).to_broadcast([R, T, MH, MO]), ALU.subtract))
            own.settle()
            own.add(nc.vector.tensor_tensor(sq[:], dev[:], dev[:], ALU.mult))
            own.settle()
            nc.vector.tensor_reduce(var[:], sq[:], AX.X, ALU.add).then_inc(sq_ready, 1)
            dve.wait_ge(dev_ready, 1)
            own.add(nc.vector.reciprocal(var[:], var[:]))
            own.settle()
            nc.vector.tensor_tensor(dev[:], dev[:], var[:].unsqueeze(3).to_broadcast([R, T, MH, MO]), ALU.mult).then_inc(dn_ready, 1)
            one_hot_group(2)
            decode(1)
            dve.wait_ge(h_ready, 3)
            dve.wait_ge(gat_in, 64)
            for av, to in ((av_src, g.score_src), (av_dst, g.score_dst)):
                own.add(nc.vector.tensor_tensor(prod[:], g.h[:, :, :, 0:GO], av[:].unsqueeze(1).to_broadcast([R, T, GH, GO]), ALU.mult))
                own.settle()
                own.add(nc.vector.tensor_reduce(to[:], prod[:], AX.X, ALU.add))
                own.settle()
            one_hot_group(3)
            decode(2)
            one_hot_group(4)
            decode(3)
            dve.wait_ge(base, 1)
            for t in range(T):
                dve.wait_ge(out_mm, min(t // 2 * 2 + 2, T))
                nc.vector.tensor_tensor(g.x1[:, t], g.x1[:, t], aux[t // 2][0:R, (t % 2) * D:(t % 2 + 1) * D], ALU.add)
            decode(4)

        @block.scalar
        def _(act):
            def unload(group):
                for t in range(T):
                    act.wait_ge(counted, T * group + t + 1)
                    if group >= 2:
                        act.wait_ge(decoded, group - 1)
                    nc.scalar.copy(packed[:, group % 2, t], cnt[t][0:R, 0:LO]).then_inc(unloaded, 1)

            unload(0)
            unload(1)
            act.wait_ge(xt_mm, 1)
            nc.scalar.copy(g.xT[:, 0, 0:4 * R], aux[0][:, 0:4 * R])
            nc.scalar.copy(g.xT[:, 1, 0:4 * R], aux[2][:, 0:4 * R])
            nc.scalar.copy(g.xT[:, :, 4 * R:N], aux[1][:, 0:2 * R].rearrange("p (k n) -> p k n", k=KB)).then_inc(xt_ready, 1)
            act.wait_ge(zeros, 5)
            for i in range(3):
                n = min(2, T - 2 * i)
                act.wait_ge(h_mm, min(2 * i + 2, T))
                nc.scalar.copy(g.h[:, 2 * i:2 * i + n, :, 0:GO],
                               aux[i][0:R, 0:n * D].rearrange("p (t h o) -> p t h o", t=n, h=GH)).then_inc(h_ready, 1)
            unload(2)
            unload(3)
            act.wait_ge(kv_mm, 2)
            act.wait_ge(zeros, 1)
            for k in range(KB):
                for b in range(P // MO):
                    q = slice(b * MO, (b + 1) * MO)
                    last = nc.scalar.mul(kv[q, k, q], aux[k][q, q], 1.0 / N)
            last.then_inc(kv_block, 1)
            unload(4)
            act.wait_ge(summed, GROUPS - 1)
            nc.scalar.copy(g.edges[:, :, 0:N], total[:])

        @block.tensor
        def _(pe):
            def count(group, i, first=False, last=False):
                pe.wait_ge(hot, i + (GROUP * group + 1))
                for t in range(T):
                    if first and group:
                        pe.wait_ge(unloaded, T * (group - 1) + t + 1)
                    mm = nc.tensor.matmul(cnt[t][0:R, 0:LO], hot_dst[:, bass.ds(i, 1), t * R:(t + 1) * R].rearrange("p a n -> p (a n)"),
                                          hot_src[:, bass.ds(i, 1), 0:LO].rearrange("p a n -> p (a n)"), start=first, stop=last)
                    if last:
                        mm.then_inc(counted, 1)
                if not last:
                    mm.then_inc(hot_used, 1)

            def count_group(group):
                count(group, 0, first=True)
                with pe.Fori(0, (GROUP - 2) // UNROLL) as i:
                    for j in range(UNROLL):
                        count(group, i * UNROLL + (j + 1))
                count(group, GROUP - 1, last=True)

            count_group(0)
            count_group(1)
            pe.wait_ge(xn_ready, T)
            pe.wait_ge(consts, 3)
            for t in range(T):
                for k in range(KB):
                    bank, at = (aux[2 * k], t * R) if t < 4 else (aux[1], k * R)
                    mm = nc.tensor.transpose(bank[:, at:at + R], g.xn[:, t, k * P:(k + 1) * P], g.ident[0:R, 0:R])
            mm.then_inc(xt_mm, 1)
            pe.wait_ge(xt_ready, 1)
            pe.wait_ge(gat_in, 64)
            for t in range(T):
                for k in range(KB):
                    mm = nc.tensor.matmul(aux[t // 2][0:R, (t % 2) * D:(t % 2 + 1) * D], g.xT[:, k, t * R:(t + 1) * R],
                                          w_gat[:, k].rearrange("p h o -> p (h o)"), start=k == 0, stop=k == KB - 1)
                mm.then_inc(h_mm, 1)
            count_group(2)
            count_group(3)
            pe.wait_ge(kv_in, 2)
            pe.wait_ge(h_ready, 3)
            for k in range(KB):
                for t in range(T):
                    mm = nc.tensor.matmul(aux[k][:, 0:P], key[:, t, k * P:(k + 1) * P], val[:, t, k * P:(k + 1) * P],
                                          start=t == 0, stop=t == T - 1)
                mm.then_inc(kv_mm, 1)
            pe.wait_ge(kv_block, 1)
            for t in range(T):
                for k in range(KB):
                    at = (t % 2) * D + k * P
                    mm = nc.tensor.matmul(aux[t // 2][0:R, at:at + P], g.xT[:, k, t * R:(t + 1) * R], kv[:, k], start=True, stop=True)
                mm.then_inc(out_mm, 1)
            count_group(4)


def attend(nc, inp, g):
    with ExitStack() as ctx:
        a = Scope(nc, ctx, "gat")
        mask = a.sb("mask", [R, T, NF])
        diag = a.sb("diag", [R, 2, NF])
        junk = a.sb("junk", [R, 2, NF])
        top = a.sb("top", [R, T, GH])
        above, below, src_leak = a.sb("above", [R, T, GH]), a.sb("below", [R, T, GH]), a.sb("src_leak", [R, T, GH])
        e_pos, e_neg = a.sb("e_pos", [R, 2, T, NF]), a.sb("e_neg", [R, 2, T, NF])
        den = a.sb("den", [R, 2, T])
        agg = a.sb("agg", [R, 2, T, GO])
        slot = [a.ps(f"slot{i}", [P, 2, BANK]) for i in range(3)]
        out = [a.ps(f"agg_ps{i}", [P, BANK]) for i in range(2)]
        turned, copied, diag_made, row_mm, row_used, exp_done, weights, agg_mm, agg_used, vec, maxed = (
            a.sem(n) for n in ("turned", "copied", "diag_made", "row_mm", "row_used", "exp_done", "weights", "agg_mm", "agg_used", "vec", "maxed"))
        block = ctx.enter_context(nc.Block())
        ROWS0 = T
        ROWS1 = T + GH

        @block.tensor
        def _(pe):
            for s in range(T):
                if s >= 3:
                    pe.wait_ge(copied, s - 2)
                for t in range(T):
                    to = slot[s % 3][0:R, t // 4, (t % 4) * R:(t % 4 + 1) * R]
                    mm = nc.tensor.transpose(to, g.edges[:, t, s * R:(s + 1) * R], g.ident[0:R, 0:R])
                mm.then_inc(turned, 1)

            def row(n):
                u = ROWS0 + n
                pe.wait_ge(diag_made, n + 1)
                if u - 3 < ROWS0:
                    pe.wait_ge(copied, u - 3 + 1)
                elif u - 3 < ROWS1:
                    pe.wait_ge(maxed, T * (u - 3 - ROWS0 + 1))
                elif (u - 3 - ROWS1) % 2 == 0:
                    pe.wait_ge(row_used, (u - 3 - ROWS1) // 2 + 1)
                else:
                    pe.wait_ge(exp_done, T * ((u - 3 - ROWS1) // 2 + 1))
                for c in range(2):
                    mm = nc.tensor.matmul(slot[u % 3][0:R, c, 0:CH], g.ones[0:R, 0:R], diag[:, n % 2, c * CH:(c + 1) * CH],
                                          start=True, stop=True)
                mm.then_inc(row_mm, 1)

            def aggregate(h):
                pe.wait_ge(weights, T * (h + 1))
                if h >= 2:
                    pe.wait_ge(agg_used, h - 1)
                for t in range(T):
                    for s in range(T):
                        mm = nc.tensor.matmul(out[h % 2][0:R, t * (GO + 1):(t + 1) * (GO + 1)],
                                              e_pos[:, h % 2, s, t * R:(t + 1) * R], g.h[:, s, h, :], start=s == 0, stop=s == T - 1)
                mm.then_inc(agg_mm, 1)

            for n in range(GH):
                row(n)
            for h in range(GH):
                row(GH + 2 * h)
                row(GH + 2 * h + 1)
                if h:
                    aggregate(h - 1)
            aggregate(GH - 1)

        @block.scalar
        def _(act):
            for s in range(T):
                act.wait_ge(turned, s + 1)
                nc.scalar.copy(g.edgesT[:, s, 0:4 * R], slot[s % 3][0:R, 0, 0:4 * R])
                nc.scalar.copy(g.edgesT[:, s, 4 * R:N], slot[s % 3][0:R, 1, 0:R]).then_inc(copied, 1)
            for h in range(GH):
                if h >= 2:
                    act.wait_ge(agg_mm, h - 1)
                for i, (e, score) in enumerate(((e_pos, g.score_src), (e_neg, src_leak))):
                    u = GH + 2 * h + i
                    act.wait_ge(row_mm, u + 1)
                    for s in range(T):
                        ins = nc.scalar.activation(halves(e[:, h % 2, s]), slot[(ROWS0 + u) % 3][0:R, :, 0:CH], ACT.Exp,
                                                   bias=score[:, s, h:h + 1])
                        if i:
                            ins.then_inc(exp_done, 1)
                    if not i:
                        ins.then_inc(row_used, 1)

        @block.vector
        def _(dve):
            own = Own(dve, vec)
            own.add(nc.vector.tensor_scalar(mask[:], g.edges[:], 0.0, NONE, ALU.is_equal, ALU.mult))
            own.add(nc.vector.memset(diag[:, :, N:NF], 0.0))
            own.add(nc.vector.tensor_single_scalar(src_leak[:], g.score_src[:], LEAK, ALU.mult))
            own.settle()

            def diagonal(n, score, h):
                if n >= 2:
                    dve.wait_ge(row_mm, n - 1)
                nc.vector.tensor_tensor(diag[:, n % 2, 0:N].rearrange("p (t j) -> p t j", t=T),
                                        g.ident[0:R, 0:R].unsqueeze(1).to_broadcast([R, T, R]),
                                        score[:, :, h:h + 1].to_broadcast([R, T, R]), ALU.mult).then_inc(diag_made, 1)

            diagonal(0, g.score_src, 0)
            for h in range(GH):
                if h + 1 < GH:
                    diagonal(h + 1, g.score_src, h + 1)
                dve.wait_ge(row_mm, h + 1)
                for t in range(T):
                    n = T * h + t
                    if n >= 2:
                        dve.wait_ge(maxed, n - 1)
                    nc.vector.tensor_tensor_reduce(halves(junk[:, n % 2]), halves(mask[:, t]), slot[(ROWS0 + h) % 3][0:R, :, 0:CH],
                                                   1.0, NONE, ALU.add, ALU.max, top[:, t, h:h + 1]).then_inc(maxed, 1)
            dve.wait_ge(maxed, T * GH)
            own.add(nc.vector.scalar_tensor_tensor(top[:], top[:], 0.1 * NONE, top[:], ALU.is_gt, ALU.mult))
            own.settle()
            own.add(nc.vector.tensor_tensor(top[:], top[:], g.score_dst[:], ALU.add))
            own.settle()
            own.add(nc.vector.scalar_tensor_tensor(top[:], top[:], LEAK, top[:], ALU.mult, ALU.max))
            own.settle()
            own.add(nc.vector.tensor_tensor(above[:], g.score_dst[:], top[:], ALU.subtract))
            own.add(nc.vector.scalar_tensor_tensor(below[:], g.score_dst[:], LEAK, top[:], ALU.mult, ALU.subtract))
            own.settle()

            def weigh(h):
                for s in range(T):
                    dve.wait_ge(exp_done, T * h + s + 1)
                    b = h % 2
                    own.add(nc.vector.tensor_tensor(e_pos[:, b, s], e_pos[:, b, s], e_neg[:, b, s], ALU.max))
                    own.settle()
                    nc.vector.scalar_tensor_tensor(e_pos[:, b, s], e_pos[:, b, s], 1.0, g.edgesT[:, s], ALU.min, ALU.mult).then_inc(weights, 1)

            def finish(h):
                dve.wait_ge(agg_mm, h + 1)
                b = h % 2
                sums = out[b][0:R, 0:T * (GO + 1)].rearrange("p (t o) -> p t o", t=T)
                own.add(nc.vector.tensor_single_scalar(den[:, b], sums[:, :, GO], 1e-9, ALU.max))
                own.settle()
                own.add(nc.vector.reciprocal(den[:, b], den[:, b]))
                own.settle()
                nc.vector.tensor_tensor(agg[:, b], sums[:, :, 0:GO], den[:, b].unsqueeze(2).to_broadcast([R, T, GO]), ALU.mult).then_inc(agg_used, 1)
                dve.wait_ge(agg_used, h + 1)
                to = g.x1[:, :, h * GO:(h + 1) * GO]
                own.add(nc.vector.scalar_tensor_tensor(to, agg[:, b], 0.0, to, ALU.max, ALU.add))

            for h in range(GH):
                diagonal(GH + 2 * h, above, h)
                diagonal(GH + 2 * h + 1, below, h)
                if h:
                    weigh(h - 1)
                if h >= 2:
                    finish(h - 2)
            weigh(GH - 1)
            finish(GH - 2)
            finish(GH - 1)


class Shared:

    def __init__(self, a):
        self.ident, self.ones = a.sb("ident", [P, P]), a.sb("ones", [P, P])
        self.x, self.xn, self.x1 = a.sb("x", [R, T, D]), a.sb("xn", [R, T, D]), a.sb("x1", [R, T, D])
        self.xT = a.sb("xT", [P, KB, NF])
        self.edges, self.edgesT = a.sb("edges", [R, T, NF]), a.sb("edgesT", [R, T, NF])
        self.h = a.sb("h", [R, T, GH, GO + 1])
        self.score_src, self.score_dst = a.sb("score_src", [R, T, GH]), a.sb("score_dst", [R, T, GH])
        self.stats, self.mv = a.sb("stats", [R, T, 6]), a.sb("mv", [R, T, 2])
        self.rstd, self.minus_half = a.sb("rstd", [R, T]), a.sb("minus_half", [R, T])
        self.var_ready, self.rstd_ready = a.sem("var_ready"), a.sem("rstd_ready")


def run_experts(nc, inp, g, layer, nth):
    pre = f"L{layer}_ffn_"
    top2 = layer == 1
    names = ("expert_w1", "expert_w2", "expert_w3") if top2 else ("W1", "W2", "Wo")
    W = [inp[pre + n] for n in names]
    E = W[0].shape[0]
    PAIRS = E // 2
    BANKS = (T + 1) // 2
    with ExitStack() as ctx:
        a = Scope(nc, ctx, f"ffn{layer}")
        raw = [[a.sb(f"raw{s}_{m}", [P, KB, D]) for m in range(3)] for s in range(2)]
        w = [[a.parts(f"w{s}_{m}", [P, KB, D]) for m in range(3)] for s in range(2)]
        hid = [a.sb(f"hid{m}", [P, KB, NF]) for m in range(2)]
        hid_parts = [a.parts(f"hid{m}", [P, KB, NF]) for m in range(2)]
        xT_parts = a.parts("xT", [P, KB, NF])
        gate_w = a.sb("gate_w", [P, KB, P if top2 else E])
        gate_w2 = a.sb("gate_w2", [P, E])
        gate_b1 = a.sb("gate_b1", [P, 1])
        gate_b = a.sb("gate_b", [R, E])
        logit, prob, gate = (a.sb(n, [R, T, E]) for n in ("logit", "prob", "gate"))
        one1, one2, cand = (a.sb(n, [R, T, E]) for n in ("one1", "one2", "cand"))
        order = a.sb("order", [R, E])
        big, sums, best, second = (a.sb(n, [R, T]) for n in ("big", "sums", "best", "second"))
        gateT = a.sb("gateT", [E, N])
        b3 = a.sb("b3", [E, D])
        PAR = 1 if top2 else 5
        par = a.sb("par", [E, 2, PAR, D])
        par_col = a.sb("par_col", [P, 2, PAR, KB * E])
        exponent = a.sb("exponent", [P, 2, KB * E])
        rh = a.sb("rh", [P, NF])

        fm = [a.ps(f"fm{i}", [P, 2, BANK]) for i in range(2)]
        rt = [a.ps(f"rt{i}", [P, BANK]) for i in range(BANKS)]
        aux = a.ps("aux", [P, BANK])

        par_in, gate_in, w_in = a.sem("par_in"), a.sem("gate_in"), [a.sem(f"w_in{s}") for s in range(2)]
        xn_ready, xt_mm, xt_ready = (a.sem(n) for n in ("xn_ready", "xt_mm", "xt_ready"))
        order_ready, par_mm, par_ready, affine_ready, rh_mm, rh_ready = (
            a.sem(n) for n in ("order_ready", "par_mm", "par_ready", "affine_ready", "rh_mm", "rh_ready"))
        logit_mm, shifted, exped, gate_ready, gt_mm, gt_ready = (
            a.sem(n) for n in ("logit_mm", "shifted", "exped", "gate_ready", "gt_mm", "gt_ready"))
        fm_done, fm_free, rt_done, rt_free = (a.sem(n) for n in ("fm_done", "fm_free", "rt_done", "rt_free"))
        w_hi, w_lo, hid_hi, hid_lo, xt_lo = (a.sem(n) for n in ("w_hi", "w_lo", "hid_hi", "hid_lo", "xt_lo"))
        vec, pool = a.sem("vec"), a.sem("pool")
        block = ctx.enter_context(nc.Block())

        param = (("expert_b1",), ("expert_b2",)) if top2 else (("b1", "g1", "be1", "m1", "v1"), ("b2", "g2", "be2", "m2", "v2"))

        @block.sync
        def _(sp):
            def load(e, s):
                for m in range(3):
                    sp.dma_start(raw[s][m][:], W[m][e].rearrange("(k p) h -> p k h", p=P)).then_inc(w_in[s], 16)

            for s in range(2):
                for i, name in enumerate(param[s]):
                    sp.dma_start(par[:, s, i], inp[pre + name]).then_inc(par_in, 16)
            if top2:
                sp.dma_start(gate_w[:], inp[pre + "router_w1"].rearrange("(k p) h -> p k h", p=P)).then_inc(gate_in, 16)
                sp.dma_start(gate_w2[:], inp[pre + "router_w2"]).then_inc(gate_in, 16)
                sp.dma_start(gate_b1[:], inp[pre + "router_b1"].rearrange("(p a) -> p a", a=1)).then_inc(gate_in, 16)
                sp.dma_start(gate_b[:], spread(inp[pre + "router_b2"], R)).then_inc(gate_in, 16)
                sp.dma_start(b3[:], inp[pre + "expert_b3"]).then_inc(gate_in, 16)
            else:
                sp.dma_start(gate_w[:], inp[pre + "Wr"].rearrange("(k p) e -> p k e", p=P)).then_inc(gate_in, 16)
                sp.dma_start(gate_b[:], spread(inp[pre + "br"], R)).then_inc(gate_in, 16)
                sp.dma_start(b3[:], inp[pre + "bo"]).then_inc(gate_in, 16)
            load(0, 0)
            load(1, 1)
            with sp.Fori(0, PAIRS - 1) as i:
                for s in range(2):
                    for m in range(3):
                        sp.wait_ge(w_lo, i * 6 + (3 * s + m + 1))
                        sp.dma_start(raw[s][m][:], W[m][bass.ds(i * 2 + (2 + s), 1)].rearrange("e (k p) h -> p (e k) h", p=P)).then_inc(w_in[s], 16)

        GATE_IN = 80 if top2 else 48

        @block.gpsimd
        def _(pool_eng):
            own = Own(pool_eng, pool)
            if top2:
                nc.gpsimd.iota(order[:], [[-1, E]], base=E, channel_multiplier=0,
                               allow_small_or_imprecise_dtypes=True).then_inc(order_ready, 1)
            else:
                own.add(nc.gpsimd.memset(exponent[:], -0.5))
                pool_eng.wait_ge(par_ready, 1)
                bias, scale, shift, mean, var = (par_col[:, :, i] for i in range(5))
                own.add(nc.gpsimd.tensor_single_scalar(var, var, 1e-3, ALU.add))
                own.add(nc.gpsimd.tensor_tensor(bias, bias, mean, ALU.subtract))
                own.settle()
                own.add(nc.gpsimd.tensor_tensor(var, var, exponent[:], ALU.pow))
                own.settle()
                own.add(nc.gpsimd.tensor_tensor(scale, scale, var, ALU.mult))
                own.settle()
                own.add(nc.gpsimd.tensor_tensor(bias, bias, scale, ALU.mult))
                own.settle()
                nc.gpsimd.tensor_tensor(bias, bias, shift, ALU.add).then_inc(affine_ready, 1)
            deviation(nc, own, g, nth, 1e-5)

            def split_weights(e, s):
                for m in range(3):
                    pool_eng.wait_ge(w_hi, e * 3 + (m + 1))
                    rest(nc.gpsimd, w[s][m], raw[s][m]).then_inc(w_lo, 1)

            with pool_eng.Fori(0, PAIRS) as i:
                split_weights(i * 2, 0)
                split_weights(i * 2 + 1, 1)

        @block.vector
        def _(dve):
            own = Own(dve, vec)
            normalize(nc, own, g, nth, g.x1, g.xn, xn_ready)
            for k in range(KB):
                dve.wait_ge(xt_ready, k + 1)
                rest(nc.vector, xT_parts, g.xT, (slice(None), k)).then_inc(xt_lo, 1)

            def split_weights(e, s, m, first=False):
                if not first:
                    dve.wait_ge(*((fm_done, e * 4 + (2 * m - 6)) if m < 2 else (rt_done, e * BANKS - BANKS)))
                dve.wait_ge(w_in[s], (e - s) * 24 + 48 if not first else 48)
                nc.vector.tensor_copy(w[s][m][0][:], raw[s][m][:]).then_inc(w_hi, 1)

            for e in range(2):
                for m in range(3):
                    split_weights(e, e, m, first=True)
            dve.wait_ge(gate_in, GATE_IN)
            dve.wait_ge(logit_mm, 1)
            own.add(nc.vector.tensor_tensor(logit[:], aux[0:R, 0:T * E].rearrange("p (t e) -> p t e", t=T),
                                            gate_b[:].unsqueeze(1).to_broadcast([R, T, E]), ALU.add))
            own.settle()
            own.add(nc.vector.tensor_reduce(big[:], logit[:], AX.X, ALU.max))
            own.settle()
            nc.vector.tensor_tensor(logit[:], logit[:], big[:].unsqueeze(2).to_broadcast([R, T, E]), ALU.subtract).then_inc(shifted, 1)
            dve.wait_ge(exped, 1)
            own.add(nc.vector.tensor_reduce(sums[:], prob[:], AX.X, ALU.add))
            own.settle()
            own.add(nc.vector.reciprocal(sums[:], sums[:]))
            own.settle()

            def over_experts(x):
                return x[:].unsqueeze(2).to_broadcast([R, T, E])

            if not top2:
                nc.vector.tensor_tensor(gate[:], prob[:], over_experts(sums), ALU.mult).then_inc(gate_ready, 1)
            else:
                own.add(nc.vector.tensor_tensor(prob[:], prob[:], over_experts(sums), ALU.mult))
                own.settle()

                def pick(one, value):
                    own.add(nc.vector.tensor_reduce(value[:], prob[:], AX.X, ALU.max))
                    own.settle()
                    own.add(nc.vector.tensor_tensor(cand[:], prob[:], over_experts(value), ALU.is_equal))
                    own.settle()
                    own.add(nc.vector.tensor_tensor(cand[:], cand[:], order[:].unsqueeze(1).to_broadcast([R, T, E]), ALU.mult))
                    own.settle()
                    own.add(nc.vector.tensor_reduce(big[:], cand[:], AX.X, ALU.max))
                    own.settle()
                    own.add(nc.vector.tensor_tensor(one[:], cand[:], over_experts(big), ALU.is_equal))
                    own.settle()

                dve.wait_ge(order_ready, 1)
                pick(one1, best)
                own.add(nc.vector.scalar_tensor_tensor(prob[:], one1[:], -2.0, prob[:], ALU.mult, ALU.add))
                own.settle()
                pick(one2, second)
                nc.vector.tensor_tensor(second[:], second[:], best[:], ALU.subtract).then_inc(shifted, 1)
                dve.wait_ge(exped, 2)
                own.add(nc.vector.tensor_single_scalar(sums[:], second[:], 1.0, ALU.add))
                own.settle()
                own.add(nc.vector.reciprocal(sums[:], sums[:]))
                own.add(nc.vector.tensor_tensor(one2[:], one2[:], over_experts(second), ALU.mult))
                own.settle()
                own.add(nc.vector.tensor_tensor(one1[:], one1[:], one2[:], ALU.add))
                own.settle()
                nc.vector.tensor_tensor(gate[:], one1[:], over_experts(sums), ALU.mult).then_inc(gate_ready, 1)

            for b in range(BANKS):
                n = min(2, T - 2 * b)
                dve.wait_ge(rt_done, b + 1)
                to = g.x1[:, 2 * b:2 * b + n]
                nc.vector.tensor_tensor(to, to, rt[b][0:R, 0:n * D].rearrange("p (t d) -> p t d", t=n), ALU.add).then_inc(rt_free, 1)

            def add_expert(e):
                for b in range(BANKS):
                    dve.wait_ge(rt_done, e * BANKS + (BANKS + b + 1))
                    dve.wait_ge(rt_free, e * BANKS + (b + 1))
                    for t in range(2 * b, min(2 * b + 2, T)):
                        at = t % 2 * D
                        ins = nc.vector.scalar_tensor_tensor(g.x1[:, t], rt[b][0:R, at:at + D], gate[:, t, bass.ds(e, 1)], g.x1[:, t],
                                                             ALU.mult, ALU.add)
                    ins.then_inc(rt_free, 1)

            def hidden_rest(e, m):
                for k in range(KB):
                    dve.wait_ge(fm_free, e * 4 + (2 * m + k + 1))
                    rest(nc.vector, hid_parts[m], hid[m], (slice(None), k)).then_inc(hid_lo, 1)

            def expert(e, s, more=True, last=False):
                hidden_rest(e, 1)
                if more:
                    split_weights(e + 2, s, 0)
                if not last:
                    hidden_rest(e + 1, 0)
                if more:
                    split_weights(e + 2, s, 1)
                add_expert(e)
                if more:
                    split_weights(e + 2, s, 2)

            hidden_rest(0, 0)
            with dve.Fori(0, PAIRS - 1) as i:
                expert(i * 2, 0)
                expert(i * 2 + 1, 1)
            expert(E - 2, 0, more=False)
            expert(E - 1, 1, more=False, last=True)

        @block.scalar
        def _(act):
            act.wait_ge(par_mm, 1)
            nc.scalar.copy(par_col[:].rearrange("p m i e -> p (m i e)"), rt[0][:, 0:2 * PAR * KB * E]).then_inc(par_ready, 1)
            nc.scalar.copy(xT_parts[0][:, :, N:NF], g.xT[:, :, N:NF])
            for k in range(KB):
                act.wait_ge(xt_mm, k + 1)
                for to in (xT_parts[0], g.xT):
                    nc.scalar.copy(to[:, k, 0:4 * R], fm[k][:, 0, 0:4 * R])
                    ins = nc.scalar.copy(to[:, k, 4 * R:N], fm[k][:, 1, 0:R])
                ins.then_inc(xt_ready, 1)
            act.wait_ge(gate_in, GATE_IN)
            if top2:
                act.wait_ge(rh_mm, 1)
                nc.scalar.activation(halves(rh[:]), fm[0][:, :, 0:CH], ACT.Relu, bias=gate_b1[:]).then_inc(rh_ready, 1)
            act.wait_ge(shifted, 1)
            nc.scalar.activation(prob[:], logit[:], ACT.Exp).then_inc(exped, 1)
            if top2:
                act.wait_ge(shifted, 2)
                nc.scalar.activation(second[:], second[:], ACT.Exp).then_inc(exped, 1)
            act.wait_ge(gt_mm, 1)
            nc.scalar.copy(gateT[:, 0:4 * R], rt[0][0:E, 0:4 * R])
            nc.scalar.copy(gateT[:, 4 * R:N], rt[1][0:E, 0:R]).then_inc(gt_ready, 1)
            act.wait_ge(par_ready, 1)
            if not top2:
                act.wait_ge(affine_ready, 1)

            def unload(e, m):
                for k in range(KB):
                    act.wait_ge(fm_done, e * 4 + (2 * m + k + 1))
                    at = bass.ds(e + k * E, 1)
                    scale = 1.0 if top2 else par_col[:, m, 1, at]
                    for to, done in ((hid_parts[m][0], hid_hi), (hid[m], fm_free)):
                        nc.scalar.activation(halves(to[:, k]), fm[k][:, :, 0:CH], ACT.Relu,
                                             bias=par_col[:, m, 0, at], scale=scale).then_inc(done, 1)

            with act.Fori(0, E) as e:
                unload(e, 0)
                unload(e, 1)

        @block.tensor
        def _(pe):
            pe.wait_ge(par_in, 16 * 2 * PAR)
            for m in range(2):
                for i in range(PAR):
                    for k in range(KB):
                        at = ((m * PAR + i) * KB + k) * E
                        mm = nc.tensor.transpose(rt[0][:, at:at + E], par[:, m, i, k * P:(k + 1) * P], g.ident[0:E, 0:E])
            mm.then_inc(par_mm, 1)
            for k in range(KB):
                for t in range(T):
                    pe.wait_ge(xn_ready, t + 1)
                    mm = nc.tensor.transpose(fm[k][:, t // 4, t % 4 * R:(t % 4 + 1) * R], g.xn[:, t, k * P:(k + 1) * P], g.ident[0:R, 0:R])
                mm.then_inc(xt_mm, 1)
            pe.wait_ge(gate_in, GATE_IN)
            if top2:
                pe.wait_ge(xt_ready, KB)
                for k in range(KB):
                    for c in range(2):
                        mm = nc.tensor.matmul(fm[0][:, c, 0:CH], gate_w[:, k], g.xT[:, k, c * CH:(c + 1) * CH], start=k == 0, stop=k == KB - 1)
                mm.then_inc(rh_mm, 1)
                pe.wait_ge(rh_ready, 1)
                for t in range(T):
                    mm = nc.tensor.matmul(aux[0:R, t * E:(t + 1) * E], rh[:, t * R:(t + 1) * R], gate_w2[:], start=True, stop=True)
            else:
                pe.wait_ge(xt_ready, KB)
                for t in range(T):
                    for k in range(KB):
                        mm = nc.tensor.matmul(aux[0:R, t * E:(t + 1) * E], g.xT[:, k, t * R:(t + 1) * R], gate_w[:, k], start=k == 0, stop=k == KB - 1)
            mm.then_inc(logit_mm, 1)

            def hidden(e, m, s, first=False):
                src, src_lo = (xT_parts, xt_lo) if m == 0 else (hid_parts[0], hid_lo)
                for f in range(KB):
                    if not first:
                        pe.wait_ge(fm_free, e * 4 + (2 * m + f - 1))
                    for n, (i, j) in enumerate(PASSES):
                        if f == 0 and n == 0:
                            pe.wait_ge(w_hi, e * 3 + (m + 1))
                        elif f == 0 and i:
                            pe.wait_ge(w_lo, e * 3 + (m + 1))
                        for k in range(KB):
                            if f == 0 and m == 1 and n == 0:
                                pe.wait_ge(hid_hi, e * 4 + (k + 1))
                            elif f == 0 and j:
                                pe.wait_ge(src_lo, e * 4 + (k + 1) if m else k + 1)
                            for c in range(2):
                                mm = nc.tensor.matmul(fm[f][:, c, 0:CH], w[s][m][i][:, k, f * P:(f + 1) * P], src[j][:, k, c * CH:(c + 1) * CH],
                                                      start=n == 0 and k == 0, stop=n == 2 and k == KB - 1)
                    mm.then_inc(fm_done, 1)

            def last_layer(e, s):
                pe.wait_ge(hid_lo, e * 4 + 4)
                pe.wait_ge(w_lo, e * 3 + 3)
                for t in range(T):
                    b, at = t // 2, t % 2 * D
                    if t % 2 == 0:
                        pe.wait_ge(rt_free, e * BANKS + (b + 1))
                    for n, (i, j) in enumerate(PASSES):
                        for k in range(KB):
                            mm = nc.tensor.matmul(rt[b][0:R, at:at + D], hid_parts[1][j][:, k, t * R:(t + 1) * R], w[s][2][i][:, k],
                                                  start=n == 0 and k == 0, stop=n == 2 and k == KB - 1)
                    if t % 2 or t == T - 1:
                        mm.then_inc(rt_done, 1)

            hidden(0, 0, 0, first=True)
            pe.wait_ge(gate_ready, 1)
            pe.wait_ge(par_ready, 1)
            for t in range(T):
                mm = nc.tensor.transpose(rt[t // 4][0:E, t % 4 * R:(t % 4 + 1) * R], gate[:, t], g.ident[0:R, 0:R])
            mm.then_inc(gt_mm, 1)
            pe.wait_ge(gt_ready, 1)
            for t in range(T):
                mm = nc.tensor.matmul(rt[t // 2][0:R, t % 2 * D:(t % 2 + 1) * D], gateT[:, t * R:(t + 1) * R], b3[:], start=True, stop=True)
                if t % 2 or t == T - 1:
                    mm.then_inc(rt_done, 1)

            def pair(e, last=False):
                hidden(e, 1, 0)
                hidden(e + 1, 0, 1)
                last_layer(e, 0)
                hidden(e + 1, 1, 1)
                if not last:
                    hidden(e + 2, 0, 0)
                last_layer(e + 1, 1)

            with pe.Fori(0, PAIRS - 1) as i:
                pair(i * 2)
            pair(E - 2, last=True)


def mix_and_convolve(nc, inp, g, nth):
    H, KD = inp["L1_mix_bq"].shape
    DH = inp["L1_gnn_W2"].shape[0]
    HB = DH // P
    SCALE = float(KD) ** -0.25
    EPS = 1e-6 * float(inp["L1_mix_proj"].shape[0]) ** 0.5
    OUT_BANK = (0, 1, 2, 0, 1)
    UQ, K0, Q0 = 4, 6, 8
    AFTER = 6 * H
    with ExitStack() as ctx:
        a = Scope(nc, ctx, "l1")
        wgt = [[a.sb(f"hw{s}_{m}", [P, KB, D]) for m in range(4)] for s in range(2)]
        proj, projT = a.sb("proj", [P, KB, KD]), a.sb("projT", [P, KB, KD])
        hb = a.sb("hb", [H, 3, KD])
        hb_col = a.sb("hb_col", [P, 3, KB, H])
        minus = a.sb("minus", [P, P])
        h3T = a.sb("h3T", [P, HB, NF])
        kT, qT = h3T[:, 0:KB], h3T[:, KB:2 * KB]
        q_sq, k_sq = a.sb("q_sq", [P, KB, NF]), a.sb("k_sq", [P, KB, NF])
        q_sum, k_sum = a.sb("q_sum", [P, NF]), a.sb("k_sum", [P, NF])
        phi_q, phi_k = a.sb("phi_q", [P, KB, NF]), a.sb("phi_k", [R, T, KD])
        sqk = a.sb("sqk", [R, T])
        pxT, kvT = a.sb("pxT", [P, KB, KD]), a.sb("kvT", [P, KB, KD])
        kvo = a.sb("kvo", [P, KB, D + 1])
        vo, vo_diag = a.sb("vo", [P, KB]), a.sb("vo_diag", [P, KB, P])
        rec = a.sb("rec", [R, T])
        att, nrm = a.sb("att", [R, T, D]), a.sb("nrm", [R, T, D])
        attT, ffT = a.sb("attT", [P, KB, NF]), kT
        w_ff = [a.sb(f"w_ff{i}", [P, KB, D]) for i in range(2)]
        b_ff = a.sb("b_ff", [P, KB])
        vecs = a.sb("vecs", [R, 7, D])
        wg = [a.sb("wg1", [P, KB, DH]), a.sb("wg2", [P, HB, DH]), a.sb("wg3", [P, HB, DH]), a.sb("wfc", [P, HB, D])]
        bg = a.sb("bg", [R, 2, DH])
        bg3 = a.sb("bg3", [P, HB])
        deg, dinv_diag, dinv_row = a.sb("deg", [R, T]), a.sb("dinv_diag", [R, NF]), a.sb("dinv_row", [R, NF])
        aggT = a.sb("aggT", [P, HB, NF])
        hid, raw = a.sb("hid", [R, T, DH]), a.sb("raw", [R, 2, DH])

        fm = [a.ps(f"fm{i}", [P, 2, BANK]) for i in range(2)]
        rt = [a.ps(f"rt{i}", [P, BANK]) for i in range(3)]
        aux = a.ps("aux", [P, BANK])

        mix_in, gnn_in, w_in = a.sem("mix_in"), a.sem("gnn_in"), [a.sem(f"w_in{s}") for s in range(2)]
        (xn_ready, xt_mm, xt_ready, consts, proj_mm, proj_ready, hb_mm, hb_ready, fm_done, fm_free, summed, aux_done,
         sqk_ready, aux_free, uk_done, uk_exp, pk_ready, pq_ready, px_done, px_ready, kvt_done, kvt_ready, kvo_done,
         kvo_ready, out_done, out_free, rec_ready, vec, pool, dinv_ready, diag_ready, dinv_mm, adj_ready) = (a.sem(n) for n in (
             "xn_ready", "xt_mm", "xt_ready", "consts", "proj_mm", "proj_ready", "hb_mm", "hb_ready", "fm_done", "fm_free",
             "summed", "aux_done", "sqk_ready", "aux_free", "uk_done", "uk_exp", "pk_ready", "pq_ready", "px_done",
             "px_ready", "kvt_done", "kvt_ready", "kvo_done", "kvo_ready", "out_done", "out_free", "rec_ready", "vec",
             "pool", "dinv_ready", "diag_ready", "dinv_mm", "adj_ready"))
        (norm_done, loops_added, vo_ready, vo_mm, att_ready, at_mm, at_ready, ff_mm, row_mm, row_added, row_ready) = (a.sem(n) for n in (
            "norm_done", "loops_added", "vo_ready", "vo_mm", "att_ready", "at_mm", "at_ready", "ff_mm", "row_mm", "row_added", "row_ready"))
        block = ctx.enter_context(nc.Block())

        def head_weights(h):
            return (inp["L1_mix_Wq"][:, bass.ds(h, 1)], inp["L1_mix_Wk"][:, bass.ds(h, 1)], inp["L1_mix_Wv"][:, bass.ds(h, 1)])

        @block.sync
        def _(sp):
            def load(h, s):
                for m, src in enumerate(head_weights(h)):
                    sp.dma_start(wgt[s][m][:], src.rearrange("(k p) a m -> p k (a m)", p=P)).then_inc(w_in[s], 16)
                sp.dma_start(wgt[s][3][:], inp["L1_mix_Wo"][bass.ds(h, 1)].rearrange("a (k p) d -> p (a k) d", p=P)).then_inc(w_in[s], 16)

            sp.dma_start(proj[:], inp["L1_mix_proj"].rearrange("(k p) d -> p k d", p=P)).then_inc(mix_in, 16)
            for i, n in enumerate(("bq", "bk", "bv")):
                sp.dma_start(hb[:, i], inp["L1_mix_" + n]).then_inc(mix_in, 16)
            load(0, 0)
            load(1, 1)
            for i, n in enumerate(("mix_bo", "mix_g1", "mix_beta1", "mix_bias2", "mix_g2", "mix_beta2", "gnn_bfc")):
                sp.dma_start(vecs[:, i], spread(inp["L1_" + n], R)).then_inc(mix_in, 16)
            sp.dma_start(b_ff[:], inp["L1_mix_bias1"].rearrange("(k p) -> p k", p=P), allow_slow_non_contiguous=True).then_inc(mix_in, 16)
            for i in range(2):
                sp.dma_start(w_ff[i][:], inp[f"L1_mix_W{i + 1}"].rearrange("(k p) d -> p k d", p=P)).then_inc(mix_in, 16)
            for i, n in enumerate(("W1", "W2", "W3", "Wfc")):
                sp.dma_start(wg[i][:], inp["L1_gnn_" + n].rearrange("(k p) d -> p k d", p=P)).then_inc(gnn_in, 16)
            for i in range(2):
                sp.dma_start(bg[:, i], spread(inp[f"L1_gnn_b{i + 1}"], R)).then_inc(gnn_in, 16)
            sp.dma_start(bg3[:], inp["L1_gnn_b3"].rearrange("(k p) -> p k", p=P), allow_slow_non_contiguous=True).then_inc(gnn_in, 16)
            with sp.Fori(0, H // 2 - 1) as i:
                for s in range(2):
                    sp.wait_ge(kvo_done, i * 2 + (s + 1))
                    load(i * 2 + (2 + s), s)

        MIX_IN, GNN_IN = 16 * 14, 16 * 7

        @block.gpsimd
        def _(pool_eng):
            own = Own(pool_eng, pool)
            nc.gpsimd.memset(minus[:], -0.5).then_inc(consts, 1)
            nc.gpsimd.memset(attT[:, :, N:NF], 0.0).then_inc(consts, 1)
            nc.gpsimd.memset(dinv_diag[:, N:NF], 0.0).then_inc(consts, 1)
            deviation(nc, own, g, nth, 1e-5)
            for t in range(T):
                at = slice(t * R, (t + 1) * R)
                nc.gpsimd.tensor_tensor(g.edges[:, t, at], g.edges[:, t, at], g.ident[0:R, 0:R], ALU.add).then_inc(loops_added, 1)
            pool_eng.wait_ge(dinv_ready, 1)
            own.add(nc.gpsimd.tensor_single_scalar(deg[:], deg[:], 1.0, ALU.add))
            own.settle()
            nc.gpsimd.tensor_tensor(deg[:], deg[:], g.minus_half[:], ALU.pow).then_inc(dinv_ready, 1)
            deviation(nc, own, g, nth + 1, 1e-6)
            deviation(nc, own, g, nth + 2, 1e-6)

        @block.vector
        def _(dve):
            own = Own(dve, vec)
            normalize(nc, own, g, nth, g.x1, g.xn, xn_ready)
            dve.wait_ge(xn_ready, T)
            dve.wait_ge(mix_in, MIX_IN)
            for t in range(T):
                nc.vector.tensor_tensor(att[:, t], g.xn[:, t], vecs[:, 0], ALU.add).then_inc(out_free, 1)
            nc.vector.memset(vo[:], 0.0).then_inc(aux_free, 1)

            def sum_squares(h, what):
                dve.wait_ge(fm_free, h * 6 + (2 * what + 2))
                sq, to = (k_sq, k_sum) if what == 0 else (q_sq, q_sum)
                nc.vector.tensor_tensor(to[:], sq[:, 0], sq[:, 1], ALU.add).then_inc(summed, 1)

            def head(h, last=False):
                dve.wait_ge(aux_done, h * 2 + 1)
                nc.vector.tensor_copy(sqk[:], aux[0:R, 0:T]).then_inc(sqk_ready, 1)
                dve.wait_ge(uk_exp, h + 1)
                nc.vector.tensor_single_scalar(phi_k[:], phi_k[:], EPS, ALU.add).then_inc(pk_ready, 1)
                dve.wait_ge(aux_done, h * 2 + 2)
                nc.vector.tensor_copy(kvo[:, :, D], aux[:, 8:8 + KB])
                dve.wait_ge(aux_free, h + 1)
                nc.vector.tensor_tensor(vo[:], vo[:], aux[:, 16:16 + KB], ALU.add).then_inc(aux_free, 1)
                dve.wait_ge(fm_free, h * 6 + (UQ + 2))
                nc.vector.tensor_single_scalar(phi_q[:], phi_q[:], EPS, ALU.add).then_inc(pq_ready, 1)
                if not last:
                    sum_squares(h + 1, 0)
                for t in range(T):
                    dve.wait_ge(out_done, h * T + (t + 1))
                    bank = rt[OUT_BANK[t]]
                    nc.vector.reciprocal(rec[:, t:t + 1], bank[0:R, D:D + 1]).then_inc(rec_ready, 1)
                    dve.wait_ge(rec_ready, h * T + (t + 1))
                    dve.wait_ge(out_free, h * T + (t + 1))
                    nc.vector.scalar_tensor_tensor(att[:, t], bank[0:R, 0:D], rec[:, t:t + 1], att[:, t], ALU.mult, ALU.add).then_inc(out_free, 1)
                if not last:
                    sum_squares(h + 1, 1)

            nc.vector.tensor_reduce(deg[:], g.edgesT[:], AX.X, ALU.add).then_inc(dinv_ready, 1)
            sum_squares(0, 0)
            sum_squares(0, 1)
            dve.wait_ge(dinv_ready, 2)
            dve.wait_ge(consts, 3)
            nc.vector.tensor_tensor(dinv_diag[:, 0:N].rearrange("p (t j) -> p t j", t=T),
                                    g.ident[0:R, 0:R].unsqueeze(1).to_broadcast([R, T, R]),
                                    deg[:].unsqueeze(2).to_broadcast([R, T, R]), ALU.mult).then_inc(diag_ready, 1)
            with dve.Fori(0, H // 2 - 1) as i:
                head(i * 2)
                head(i * 2 + 1)
            head(H - 2)
            head(H - 1, last=True)

            dve.wait_ge(aux_free, H + 1)
            for k in range(KB):
                ins = nc.vector.tensor_scalar(vo_diag[:, k], g.ident[:], vo[:, k:k + 1], None, ALU.mult)
            ins.then_inc(vo_ready, 1)
            dve.wait_ge(dinv_mm, 1)
            own.add(nc.vector.tensor_copy(halves(dinv_row[:]), fm[1][0:R, :, 0:CH]))
            own.settle()
            dve.wait_ge(loops_added, T)
            for t in range(T):
                nc.vector.scalar_tensor_tensor(g.edges[:, t], g.edges[:, t], deg[:, t:t + 1], dinv_row[:], ALU.mult, ALU.mult).then_inc(adj_ready, 1)
            dve.wait_ge(vo_mm, 1)
            dve.wait_ge(out_free, T * (H + 1))
            own.add(nc.vector.tensor_tensor(att[:], att[:], aux[0:R, 0:D].unsqueeze(1).to_broadcast([R, T, D]), ALU.add))
            own.settle()

            def affine(n, scale, shift, out, done):
                normalize(nc, own, g, n, att, nrm, norm_done)
                dve.wait_ge(norm_done, T * (n - nth))
                own.add(nc.vector.tensor_tensor(nrm[:], nrm[:], vecs[:, scale].unsqueeze(1).to_broadcast([R, T, D]), ALU.mult))
                own.settle()
                nc.vector.tensor_tensor(out[:], nrm[:], vecs[:, shift].unsqueeze(1).to_broadcast([R, T, D]), ALU.add).then_inc(done, 1)

            affine(nth + 1, 1, 2, att, att_ready)
            own.add(nc.vector.tensor_tensor(g.x1[:], g.x1[:], vecs[:, 6].unsqueeze(1).to_broadcast([R, T, D]), ALU.add))

            def add_rows(layer):
                dve.wait_ge(gnn_in, GNN_IN)
                for t in range(T):
                    v = T * layer + t
                    dve.wait_ge(row_mm, v + 1)
                    if v >= 2:
                        dve.wait_ge(row_ready, v - 1)
                    nc.vector.tensor_tensor(raw[:, v % 2], rt[v % 3][0:R, 0:DH], bg[:, layer], ALU.add).then_inc(row_added, 1)

            add_rows(0)
            dve.wait_ge(at_ready, 3)
            own.add(nc.vector.tensor_tensor(att[:], att[:], vecs[:, 3].unsqueeze(1).to_broadcast([R, T, D]), ALU.add))
            own.settle()
            add_rows(1)
            for b in range(3):
                n = min(2, T - 2 * b)
                dve.wait_ge(ff_mm, b + 1)
                to = att[:, 2 * b:2 * b + n]
                nc.vector.tensor_tensor(to, to, aux[0:R, 0:n * D].rearrange("p (t d) -> p t d", t=n), ALU.add).then_inc(att_ready, 1)
            dve.wait_ge(att_ready, 4)
            affine(nth + 2, 4, 5, nrm, att_ready)
            dve.wait_ge(att_ready, 5)
            own.add(nc.vector.tensor_tensor(g.x1[:], g.x1[:], nrm[:], ALU.add))
            own.settle()
            for t in range(T):
                v = 2 * T + t
                dve.wait_ge(row_mm, v + 1)
                nc.vector.tensor_tensor(g.x1[:, t], g.x1[:, t], rt[v % 3][0:R, 0:D], ALU.add).then_inc(row_added, 1)

        @block.scalar
        def _(act):
            for k in range(KB):
                act.wait_ge(xt_mm, k + 1)
                nc.scalar.copy(g.xT[:, k, 0:4 * R], fm[k][:, 0, 0:4 * R])
                nc.scalar.copy(g.xT[:, k, 4 * R:N], fm[k][:, 1, 0:R]).then_inc(xt_ready, 1)
            act.wait_ge(proj_mm, 1)
            nc.scalar.copy(projT[:].rearrange("p k m -> p (k m)"), rt[0][:]).then_inc(proj_ready, 1)
            act.wait_ge(hb_mm, 1)
            n = 2 * KB * H
            nc.scalar.mul(hb_col[:, 0:2].rearrange("p a k h -> p (a k h)"), aux[:, 0:n], SCALE)
            nc.scalar.copy(hb_col[:, 2].rearrange("p k h -> p (k h)"), aux[:, n:n + KB * H]).then_inc(hb_ready, 1)
            act.wait_ge(hb_ready, 1)

            def unload_qk(h, f, use, what, bf):
                act.wait_ge(fm_done, use + 1)
                to, sq = ((qT, q_sq), (kT, k_sq))[what]
                bias = hb_col[:, what, f, bass.ds(bf, 1)]
                nc.scalar.activation(halves(sq[:, f]), fm[f][:, :, 0:CH], ACT.Square, bias=bias, scale=SCALE)
                nc.scalar.activation(halves(to[:, f]), fm[f][:, :, 0:CH], ACT.Identity, bias=bias, scale=SCALE).then_inc(fm_free, 1)

            for f in range(KB):
                unload_qk(0, f, f, 1, 0)
            for f in range(KB):
                unload_qk(0, f, KB + f, 0, 0)

            def features(h, f):
                act.wait_ge(fm_done, h * 6 + (UQ + f + 1))
                nc.scalar.activation(halves(phi_q[:, f]), fm[f][:, :, 0:CH], ACT.Exp).then_inc(fm_free, 1)

            def head(h, last=False):
                act.wait_ge(sqk_ready, h + 1)
                for b in range(3):
                    act.wait_ge(uk_done, h * 3 + (b + 1))
                    for t in range(2 * b, min(2 * b + 2, T)):
                        ins = nc.scalar.activation(phi_k[:, t], rt[b][0:R, t % 2 * KD:(t % 2 + 1) * KD], ACT.Exp, bias=sqk[:, t:t + 1])
                ins.then_inc(uk_exp, 1)
                features(h, 0)
                act.wait_ge(px_done, h + 1)
                nc.scalar.copy(pxT[:].rearrange("p k m -> p (k m)"), rt[0][:]).then_inc(px_ready, 1)
                features(h, 1)
                act.wait_ge(kvt_done, h + 1)
                nc.scalar.copy(kvT[:].rearrange("p k m -> p (k m)"), rt[1][:]).then_inc(kvt_ready, 1)
                if not last:
                    unload_qk(h, 0, h * 6 + K0, 1, h + 1)
                act.wait_ge(kvo_done, h + 1)
                nc.scalar.copy(kvo[:, :, 0:D], rt[2][:].rearrange("p (k m) -> p k m", k=KB)).then_inc(kvo_ready, 1)
                if not last:
                    unload_qk(h, 1, h * 6 + (K0 + 1), 1, h + 1)
                    unload_qk(h, 0, h * 6 + Q0, 0, h + 1)
                    unload_qk(h, 1, h * 6 + (Q0 + 1), 0, h + 1)

            with act.Fori(0, H // 2 - 1) as i:
                head(i * 2)
                head(i * 2 + 1)
            head(H - 2)
            head(H - 1, last=True)

            def unload_fm(first, n, to, bias=None):
                for f in range(n):
                    u = AFTER + first + f
                    act.wait_ge(fm_done, u + 1)
                    src = fm[u % 2][:, :, 0:CH]
                    if bias is None:
                        nc.scalar.copy(halves(to[:, f]), src).then_inc(fm_free, 1)
                    else:
                        nc.scalar.activation(halves(to[:, f]), src, ACT.Relu, bias=bias[:, f:f + 1]).then_inc(fm_free, 1)

            def relu_rows(layer):
                for t in range(T):
                    v = T * layer + t
                    act.wait_ge(row_added, v + 1)
                    nc.scalar.activation(hid[:, t], raw[:, v % 2], ACT.Relu).then_inc(row_ready, 1)

            act.wait_ge(gnn_in, GNN_IN)
            act.wait_ge(mix_in, MIX_IN)
            unload_fm(0, KB, aggT)
            relu_rows(0)
            for n in range(3):
                act.wait_ge(at_mm, n + 1)
                if n < 2:
                    nc.scalar.copy(attT[:, n, 0:4 * R], aux[:, 0:4 * R]).then_inc(at_ready, 1)
                else:
                    nc.scalar.copy(attT[:, :, 4 * R:N], aux[:, 0:KB * R].rearrange("p (k j) -> p k j", k=KB)).then_inc(at_ready, 1)
            unload_fm(KB, HB, aggT)
            relu_rows(1)
            unload_fm(KB + HB, KB, ffT, b_ff)
            unload_fm(2 * KB + HB, HB, aggT)
            unload_fm(2 * KB + 2 * HB, HB, h3T, bg3)

        @block.tensor
        def _(pe):
            pe.wait_ge(mix_in, MIX_IN)
            for m in range(KB):
                for k in range(KB):
                    mm = nc.tensor.transpose(rt[0][:, k * KD + m * P:k * KD + (m + 1) * P], proj[:, m, k * P:(k + 1) * P], g.ident[:])
            mm.then_inc(proj_mm, 1)
            for i in range(3):
                for k in range(KB):
                    at = (i * KB + k) * H
                    mm = nc.tensor.transpose(aux[:, at:at + H], hb[:, i, k * P:(k + 1) * P], g.ident[0:H, 0:H])
            mm.then_inc(hb_mm, 1)
            for k in range(KB):
                for t in range(T):
                    pe.wait_ge(xn_ready, t + 1)
                    mm = nc.tensor.transpose(fm[k][:, t // 4, t % 4 * R:(t % 4 + 1) * R], g.xn[:, t, k * P:(k + 1) * P], g.ident[0:R, 0:R])
                mm.then_inc(xt_mm, 1)

            def feature_major(to, lhs, rhs, n, more=()):
                for k in range(n):
                    for c in range(2):
                        mm = nc.tensor.matmul(to[:, c, 0:CH], lhs(k), rhs(k)[:, c * CH:(c + 1) * CH], start=k == 0, stop=k == n - 1 and not more)
                for l, r in more:
                    for c in range(2):
                        mm = nc.tensor.matmul(to[:, c, 0:CH], l, r[:, c * CH:(c + 1) * CH], start=False, stop=True)
                mm.then_inc(fm_done, 1)

            def project(f, use, w, first=False):
                if not first:
                    pe.wait_ge(fm_free, use - 1)
                feature_major(fm[f], lambda k: w[:, k, f * P:(f + 1) * P], lambda k: g.xT[:, k], KB)

            def query_features(h, f):
                if f == 0:
                    pe.wait_ge(summed, h * 2 + 2)
                pe.wait_ge(fm_free, h * 6 + (UQ + f - 1))
                feature_major(fm[f], lambda k: projT[:, k, f * P:(f + 1) * P], lambda k: qT[:, k], KB, more=((minus[:], q_sum[:]),))

            def head(h, s, last=False):
                pe.wait_ge(summed, h * 2 + 1)
                pe.wait_ge(aux_free, h + 1)
                for t in range(T):
                    mm = nc.tensor.matmul(aux[0:R, t:t + 1], k_sum[:, t * R:(t + 1) * R], minus[:, 0:1], start=True, stop=True)
                mm.then_inc(aux_done, 1)
                for t in range(T):
                    if t % 2 == 0:
                        pe.wait_ge(out_free, h * T + (4, 5, 3)[t // 2])
                    for k in range(KB):
                        mm = nc.tensor.matmul(rt[t // 2][0:R, t % 2 * KD:(t % 2 + 1) * KD], kT[:, k, t * R:(t + 1) * R], projT[:, k],
                                              start=k == 0, stop=k == KB - 1)
                    if t % 2 or t == T - 1:
                        mm.then_inc(uk_done, 1)
                query_features(h, 0)
                pe.wait_ge(pk_ready, h + 1)
                for k in range(KB):
                    for t in range(T):
                        mm = nc.tensor.matmul(rt[0][:, k * KD:(k + 1) * KD], g.xn[:, t, k * P:(k + 1) * P], phi_k[:, t], start=t == 0, stop=t == T - 1)
                mm.then_inc(px_done, 1)
                for m in range(KB):
                    for t in range(T):
                        nc.tensor.matmul(aux[:, 8 + m:9 + m], phi_k[:, t, m * P:(m + 1) * P], g.ones[0:R, 0:1], start=t == 0, stop=t == T - 1)
                for m in range(KB):
                    for k in range(KB):
                        mm = nc.tensor.matmul(aux[:, 16 + m:17 + m], wgt[s][3][:, k, m * P:(m + 1) * P], hb_col[:, 2, k, bass.ds(h, 1)],
                                              start=k == 0, stop=k == KB - 1)
                mm.then_inc(aux_done, 1)
                query_features(h, 1)
                pe.wait_ge(px_ready, h + 1)
                for f in range(KB):
                    for k in range(KB):
                        mm = nc.tensor.matmul(rt[1][:, f * KD:(f + 1) * KD], wgt[s][2][:, k, f * P:(f + 1) * P], pxT[:, k], start=k == 0, stop=k == KB - 1)
                mm.then_inc(kvt_done, 1)
                if not last:
                    pe.wait_ge(w_in[1 - s], (h + s) * 32 + 64)
                    project(0, h * 6 + K0, wgt[1 - s][1])
                pe.wait_ge(kvt_ready, h + 1)
                for m in range(KB):
                    for k in range(KB):
                        mm = nc.tensor.matmul(rt[2][:, m * D:(m + 1) * D], kvT[:, k, m * P:(m + 1) * P], wgt[s][3][:, k], start=k == 0, stop=k == KB - 1)
                mm.then_inc(kvo_done, 1)
                if not last:
                    project(1, h * 6 + (K0 + 1), wgt[1 - s][1])
                    project(0, h * 6 + Q0, wgt[1 - s][0])
                pe.wait_ge(kvo_ready, h + 1)
                pe.wait_ge(aux_free, h + 2)
                pe.wait_ge(pq_ready, h + 1)
                for t in range(T):
                    if t >= 3:
                        pe.wait_ge(out_free, h * T + (T + t - 2))
                    for k in range(KB):
                        mm = nc.tensor.matmul(rt[OUT_BANK[t]][0:R, 0:D + 1], phi_q[:, k, t * R:(t + 1) * R], kvo[:, k], start=k == 0, stop=k == KB - 1)
                    mm.then_inc(out_done, 1)
                if not last:
                    project(1, h * 6 + (Q0 + 1), wgt[1 - s][0])

            pe.wait_ge(w_in[0], 64)
            pe.wait_ge(xt_ready, KB)
            for f in range(KB):
                project(f, f, wgt[0][1], first=True)
            for f in range(KB):
                project(f, KB + f, wgt[0][0])
            pe.wait_ge(hb_ready, 1)
            pe.wait_ge(proj_ready, 1)
            with pe.Fori(0, H // 2 - 1) as i:
                head(i * 2, 0)
                head(i * 2 + 1, 1)
            head(H - 2, 0)
            head(H - 1, 1, last=True)

            pe.wait_ge(diag_ready, 1)
            pe.wait_ge(fm_free, AFTER)
            for c in range(2):
                mm = nc.tensor.matmul(fm[1][0:R, c, 0:CH], g.ones[0:R, 0:R], dinv_diag[:, c * CH:(c + 1) * CH], start=True, stop=True)
            mm.then_inc(dinv_mm, 1)
            pe.wait_ge(vo_ready, 1)
            nc.tensor.matmul(aux[0:R, 0:D], g.ones[:, 0:R], vo_diag[:].rearrange("p k d -> p (k d)"), start=True, stop=True).then_inc(vo_mm, 1)

            def spread_edges(first, n, src):
                for f in range(n):
                    u = AFTER + first + f
                    if f == 0:
                        pe.wait_ge(adj_ready, T)
                    pe.wait_ge(fm_free, u - 1)
                    feature_major(fm[u % 2], lambda t: src[:, t, f * P:(f + 1) * P], lambda t: g.edges[:, t], T)

            def to_rows(layer, blocks, src, src_ready, w, cols):
                pe.wait_ge(fm_free, AFTER + src_ready)
                for t in range(T):
                    v = T * layer + t
                    if v >= 3:
                        pe.wait_ge(row_added, v - 2)
                    for k in range(blocks):
                        mm = nc.tensor.matmul(rt[v % 3][0:R, 0:cols], src[:, k, t * R:(t + 1) * R], w[:, k], start=k == 0, stop=k == blocks - 1)
                    mm.then_inc(row_mm, 1)

            pe.wait_ge(gnn_in, GNN_IN)
            spread_edges(0, KB, g.xn)
            pe.wait_ge(out_free, T * (H + 1))
            to_rows(0, KB, aggT, KB, wg[0], DH)
            pe.wait_ge(att_ready, 1)
            for n in range(3):
                if n:
                    pe.wait_ge(at_ready, n)
                for j in range(4 if n < 2 else KB):
                    t, k = (j, n) if n < 2 else (4, j)
                    mm = nc.tensor.transpose(aux[:, j * R:(j + 1) * R], att[:, t, k * P:(k + 1) * P], g.ident[0:R, 0:R])
                mm.then_inc(at_mm, 1)
            pe.wait_ge(row_ready, T)
            spread_edges(KB, HB, hid)
            to_rows(1, HB, aggT, KB + HB, wg[1], DH)
            pe.wait_ge(at_ready, 3)
            for f in range(KB):
                u = AFTER + KB + HB + f
                pe.wait_ge(fm_free, u - 1)
                feature_major(fm[u % 2], lambda k: w_ff[0][:, k, f * P:(f + 1) * P], lambda k: attT[:, k], KB)
            pe.wait_ge(row_ready, 2 * T)
            spread_edges(2 * KB + HB, HB, hid)
            for b in range(3):
                if b:
                    pe.wait_ge(att_ready, b + 1)
                for t in range(2 * b, min(2 * b + 2, T)):
                    for k in range(KB):
                        mm = nc.tensor.matmul(aux[0:R, t % 2 * D:(t % 2 + 1) * D], ffT[:, k, t * R:(t + 1) * R], w_ff[1][:, k], start=k == 0, stop=k == KB - 1)
                mm.then_inc(ff_mm, 1)
            pe.wait_ge(fm_free, AFTER + 2 * KB + 2 * HB)
            for f in range(HB):
                u = AFTER + 2 * KB + 2 * HB + f
                pe.wait_ge(fm_free, u - 1)
                feature_major(fm[u % 2], lambda k: wg[2][:, k, f * P:(f + 1) * P], lambda k: aggT[:, k], HB)
            to_rows(2, HB, h3T, 2 * KB + 3 * HB, wg[3], D)


def store(nc, g, out):
    with ExitStack() as ctx:
        a = Scope(nc, ctx, "store")
        stored = a.sem("stored")
        block = ctx.enter_context(nc.Block())

        @block.sync
        def _(sp):
            sp.dma_start(rows(out), g.x1[:]).then_inc(stored, 16)
            sp.wait_ge(stored, 16)


def gps_two_layers(nc, inp, out):
    with ExitStack() as ctx:
        g = Shared(Scope(nc, ctx, "g"))
        count_edges_and_mix(nc, inp, g)
        attend(nc, inp, g)
        run_experts(nc, inp, g, 0, 1)
        mix_and_convolve(nc, inp, g, 2)
        run_experts(nc, inp, g, 1, 5)
        store(nc, g, out)


def kernel(**inputs):
    import concourse.bacc as bacc
    from concourse.bass_utils import run_bass_kernel_spmd

    nc = bacc.Bacc("TRN2", target_bir_lowering=False, num_devices=1)
    arrays, inp = {}, {}
    for name, value in inputs.items():
        value = np.ascontiguousarray(value)
        arrays[f"in_{name}"] = value
        inp[name] = nc.dram_tensor(f"in_{name}", value.shape, mybir.dt.from_np(value.dtype), kind="ExternalInput").ap()
    out = nc.dram_tensor("out", inputs["x"].shape, F32, kind="ExternalOutput").ap()
    gps_two_layers(nc, inp, out)
    return run_bass_kernel_spmd(nc, [arrays], core_ids=[0]).results[0]["out"]
```

```python
from contextlib import ExitStack

import numpy as np

import concourse.bass as bass
from concourse import mybir

F32 = mybir.dt.float32
F16 = mybir.dt.float16
F32R = mybir.dt.float32r
BF16 = mybir.dt.bfloat16
I32 = mybir.dt.int32
ALU = mybir.AluOpType
ACT = mybir.ActivationFunctionType
AX = mybir.AxisListType

N = 625
R = 125
T = N // R
D = 256
P = 128
KB = D // P
NF = 628
CH = NF // 2
NE = 20000
EP = 125
CHUNKS = NE // EP
BANK = 512

LO = 313
HI = N - LO
FIELD = 12
GROUP = 32
GROUPS = CHUNKS // GROUP
UNROLL = 10
SCALAR_HOT = (1, 4, 7)
BODIES, PER_BODY = (GROUP - 2) // UNROLL, len(SCALAR_HOT)
assert GROUP * EP < 2 ** FIELD and (GROUP - 2) % UNROLL == 0 and GROUPS * GROUP == CHUNKS

PASSES = ((0, 0), (1, 0), (0, 1))

GH, GO = 4, 64
LEAK = 0.2
NONE = -1e30
MH, MO = 8, 32


class Own:

    def __init__(self, eng, sem):
        self.eng, self.sem, self.count = eng, sem, 0

    def add(self, instruction):
        self.count += 1
        instruction.then_inc(self.sem, 1)

    def settle(self):
        self.eng.wait_ge(self.sem, self.count)


class Scope:

    def __init__(self, nc, ctx, part):
        self.nc, self.ctx, self.part = nc, ctx, part

    def sb(self, name, shape, dt=F32):
        return self.ctx.enter_context(self.nc.sbuf_tensor(f"{self.part}_{name}", shape, dt))

    def parts(self, name, shape):
        return self.sb(name + "_hi", shape, F32R), self.sb(name + "_lo", shape, F32R)

    def ps(self, name, shape):
        return self.ctx.enter_context(self.nc.psum_tensor(f"{self.part}_{name}", shape, F32))

    def sem(self, name):
        return self.nc.alloc_semaphore(f"{self.part}_{name}")


def rows(ap):
    return ap.rearrange("(t p) d -> p t d", p=R)


def spread(ap, n):
    return ap.rearrange("(a d) -> a d", a=1).to_broadcast([n, ap.shape[0]])


def halves(ap):
    return ap.rearrange("p (c n) -> p c n", c=2)


def rest(engine, parts, whole, at=()):
    hi, lo = parts
    at = at or slice(None)
    return engine.tensor_tensor(lo[at], whole[at], hi[at].bitcast(F32), ALU.subtract)


def product(pe, nc, outs, blocks, left, right, left_low=(), right_low=(), more=False):
    for n, (i, j) in enumerate(PASSES):
        if n == 1 and left_low:
            pe.wait_ge(*left_low)
        if n == 2 and right_low:
            pe.wait_ge(*right_low)
        for k in range(blocks):
            for to, at in outs:
                mm = nc.tensor.matmul(to, left(i, k), right(j, k)[:, at], start=n == 0 and k == 0,
                                      stop=n == 2 and k == blocks - 1 and not more)
    return mm


def both_halves(bank_pair):
    return [(bank_pair[:, c, 0:CH], slice(c * CH, (c + 1) * CH)) for c in range(2)]


def moments(nc, own, w, src):
    for t in range(T):
        own.add(nc.vector.bn_stats(w.stats[:, t, :], src[:, t, :]))
    own.settle()
    for t in range(T):
        ins = nc.vector.bn_aggr(w.mv[:, t, :], w.stats[:, t, :])
    ins.then_inc(w.var_ready, 1)


def standardize(nc, own, w, nth, src, dst, done):
    own.eng.wait_ge(w.rstd_ready, nth + 1)
    for t in range(T):
        nc.vector.tensor_scalar(dst[:, t, :], src[:, t, :], w.mv[:, t, 0:1], w.rstd[:, t:t + 1],
                                ALU.subtract, ALU.mult).then_inc(done, 1)


def normalize(nc, own, w, nth, src, dst, done):
    moments(nc, own, w, src)
    standardize(nc, own, w, nth, src, dst, done)


def deviation(nc, own, w, nth, eps):
    own.eng.wait_ge(w.var_ready, nth + 1)
    own.add(nc.gpsimd.tensor_single_scalar(w.rstd[:], w.mv[:, :, 1], eps, ALU.add))
    own.settle()
    nc.gpsimd.tensor_tensor(w.rstd[:], w.rstd[:], w.minus_half[:], ALU.pow).then_inc(w.rstd_ready, 1)


def count_edges_and_mix(nc, inp, g):
    with ExitStack() as ctx:
        a = Scope(nc, ctx, "count")
        dst_i, src_i = a.sb("dst_i", [EP, CHUNKS], I32), a.sb("src_i", [EP, CHUNKS], I32)
        dst_f, src_f = a.sb("dst_f", [EP, CHUNKS]), a.sb("src_f", [EP, CHUNKS])
        in_high, field, column = (a.sb(n, [EP, CHUNKS]) for n in ("in_high", "field", "column"))
        neg_field, neg_column = a.sb("neg_field", [EP, CHUNKS]), a.sb("neg_column", [EP, CHUNKS])
        node_no = a.sb("node_no", [EP, N + 1], F16)
        away = a.sb("away", [EP, len(SCALAR_HOT), LO + 1], F16)
        hot_dst = a.sb("hot_dst", [EP, GROUP, N + 1], BF16)
        hot_src = a.sb("hot_src", [EP, GROUP, LO + 1], BF16)
        packed = a.sb("packed", [R, 2, T, LO], I32)
        total = a.sb("total", [R, T, N], I32)
        total_lo, total_hi = total[:, :, 0:LO], total[:, :, LO:N]
        low, high = a.sb("low", [R, T, LO], I32), a.sb("high", [R, T, LO], I32)
        w_gat = a.sb("w_gat", [P, KB, GH, GO])
        av_src, av_dst = a.sb("av_src", [R, GH, GO]), a.sb("av_dst", [R, GH, GO])
        ln_w = [a.sb(f"mix_ln{i}", [R, D]) for i in range(4)]
        prod = a.sb("prod", [R, T, GH, GO])
        mean = a.sb("mean", [R, T, MH])
        dev, sq = a.sb("dev", [R, T, MH, MO]), a.sb("sq", [R, T, MH, MO])
        var, half = a.sb("var", [R, T, MH]), a.sb("half", [R, T, MH])
        key, val = a.sb("key", [R, T, D]), a.sb("val", [R, T, D])
        kv = a.sb("kv", [P, KB, P])

        cnt = [a.ps(f"cnt{t}", [P, BANK]) for t in range(T)]
        aux = [a.ps(f"aux{i}", [P, BANK]) for i in range(3)]

        x_in, edges_in, gat_in, mix_in = (a.sem(n) for n in ("x_in", "edges_in", "gat_in", "mix_in"))
        consts, zeros = a.sem("consts"), a.sem("zeros")
        earlier_counts = a.sem("earlier_counts")
        hot, src_hot, away_ready, split_edges, hot_used, counted, unloaded, decoded, summed = (
            a.sem(n) for n in ("hot", "src_hot", "away_ready", "split_edges", "hot_used", "counted", "unloaded", "decoded", "summed"))
        vec = a.sem("vec")
        xn_ready, xt_mm, xt_ready, h_mm, h_ready = (a.sem(n) for n in ("xn_ready", "xt_mm", "xt_ready", "h_mm", "h_ready"))
        dev_ready, sq_ready, kv_in, kv_ready, kv_mm, kv_block, out_mm, base = (
            a.sem(n) for n in ("dev_ready", "sq_ready", "kv_in", "kv_ready", "kv_mm", "kv_block", "out_mm", "base"))
        dn_ready, pool = a.sem("dn_ready"), a.sem("pool")
        block = ctx.enter_context(nc.Block())

        @block.sync
        def _(sp):
            sp.dma_start(dst_i[:], inp["dst"].rearrange("(p c) -> p c", p=EP)).then_inc(edges_in, 16)
            sp.dma_start(src_i[:], inp["src"].rearrange("(p c) -> p c", p=EP)).then_inc(edges_in, 16)
            sp.dma_start(g.x[:], rows(inp["x"])).then_inc(x_in, 16)
            for k in range(KB):
                sp.dma_start(w_gat[:, k], inp["L0_gnn_W"][:, k * P:(k + 1) * P, :].rearrange("h p o -> p h o")).then_inc(gat_in, 16)
            sp.dma_start(av_src[:].rearrange("p h o -> p (h o)"), spread(inp["L0_gnn_a_src"].rearrange("h o -> (h o)"), R)).then_inc(gat_in, 16)
            sp.dma_start(av_dst[:].rearrange("p h o -> p (h o)"), spread(inp["L0_gnn_a_dst"].rearrange("h o -> (h o)"), R)).then_inc(gat_in, 16)
            for i, n in enumerate(("kln_weight", "kln_bias", "vln_weight", "vln_bias")):
                sp.dma_start(ln_w[i][:], spread(inp["L0_mix_" + n].rearrange("h a o -> (h a o)"), R)).then_inc(mix_in, 16)

        @block.gpsimd
        def _(pool_eng):
            own = Own(pool_eng, pool)
            nc.gpsimd.iota(node_no[:], [[1, N + 1]], base=0, channel_multiplier=0,
                           allow_small_or_imprecise_dtypes=True).then_inc(consts, 1)
            nc.gpsimd.memset(g.ones[:], 1.0).then_inc(consts, 1)
            pool_eng.wait_ge(consts, 2)
            nc.gpsimd.affine_select(out=g.ident[:], in_=g.ones[:], compare_op=ALU.is_equal, fill=0.0, base=0,
                                    pattern=[[-1, P]], channel_multiplier=1).then_inc(consts, 1)
            nc.gpsimd.memset(kv[:], 0.0).then_inc(zeros, 1)
            nc.gpsimd.memset(g.xT[:, :, N:NF], 0.0).then_inc(zeros, 1)
            nc.gpsimd.memset(g.edges[:, :, N:NF], 0.0).then_inc(zeros, 1)
            nc.gpsimd.memset(g.edgesT[:, :, N:NF], 0.0).then_inc(zeros, 1)
            nc.gpsimd.memset(g.h[:, :, :, GO:GO + 1], 1.0).then_inc(zeros, 1)

            def add_counts(n):
                pool_eng.wait_ge(decoded, n + 1)
                if n >= 2:
                    pool_eng.wait_ge(summed, n - 1)
                nc.gpsimd.tensor_tensor(total_lo, total_lo, low[:], ALU.add)
                nc.gpsimd.tensor_tensor(total_hi, total_hi, high[:, :, 0:HI], ALU.add).then_inc(summed, 1)

            own.add(nc.gpsimd.memset(g.minus_half[:], -0.5))
            own.add(nc.gpsimd.memset(half[:], 0.5))
            deviation(nc, own, g, 0, 1e-5)
            pool_eng.wait_ge(xn_ready, T)
            nc.gpsimd.tensor_tensor(g.x1[:], g.x[:], g.xn[:], ALU.add).then_inc(base, 1)
            pool_eng.wait_ge(sq_ready, 1)
            own.add(nc.gpsimd.tensor_single_scalar(var[:], var[:], 1.0 / (MO - 1), ALU.mult))
            own.settle()
            own.add(nc.gpsimd.tensor_tensor(var[:], var[:], half[:], ALU.pow))
            own.settle()
            nc.gpsimd.tensor_single_scalar(var[:], var[:], 1e-5, ALU.add).then_inc(dev_ready, 1)
            pool_eng.wait_ge(dn_ready, 1)
            pool_eng.wait_ge(mix_in, 64)
            flat = dev[:].rearrange("p t h o -> p t (h o)")
            for wt, bias, to in ((ln_w[0], ln_w[1], key), (ln_w[2], ln_w[3], val)):
                own.add(nc.gpsimd.tensor_tensor(to[:], flat, wt[:].unsqueeze(1).to_broadcast([R, T, D]), ALU.mult))
            own.settle()
            for wt, bias, to in ((ln_w[0], ln_w[1], key), (ln_w[2], ln_w[3], val)):
                nc.gpsimd.tensor_tensor(to[:], to[:], bias[:].unsqueeze(1).to_broadcast([R, T, D]), ALU.add).then_inc(kv_in, 1)
            for n in range(1, GROUPS - 1):
                add_counts(n)

        @block.vector
        def _(dve):
            own = Own(dve, vec)
            dve.wait_ge(edges_in, 32)
            own.add(nc.vector.tensor_copy(dst_f[:], dst_i[:]))
            own.add(nc.vector.tensor_copy(src_f[:], src_i[:]))
            own.settle()
            own.add(nc.vector.tensor_scalar(in_high[:], src_f[:], float(LO), None, ALU.is_ge))
            own.settle()
            own.add(nc.vector.tensor_scalar(field[:], in_high[:], float(2 ** FIELD - 1), 1.0, ALU.mult, ALU.add))
            nc.vector.scalar_tensor_tensor(column[:], in_high[:], -float(LO), src_f[:], ALU.mult, ALU.add).then_inc(split_edges, 1)
            dve.wait_ge(split_edges, 1)
            own.settle()
            dve.wait_ge(consts, 1)

            def one_hots(group, i, last=False, src=True):
                if group and last:
                    dve.wait_ge(counted, T * group)
                elif group:
                    dve.wait_ge(hot_used, i + ((GROUP - 1) * (group - 1) + 1))
                c = i + GROUP * group
                ins = nc.vector.tensor_scalar(hot_dst[:, bass.ds(i, 1), :].rearrange("p a n -> p (a n)"), node_no[:],
                                              dst_f[:, bass.ds(c, 1)], None, ALU.is_equal)
                if src:
                    ins = nc.vector.tensor_scalar(hot_src[:, bass.ds(i, 1), :].rearrange("p a n -> p (a n)"), node_no[:, 0:LO + 1],
                                                  column[:, bass.ds(c, 1)], field[:, bass.ds(c, 1)], ALU.is_equal, ALU.mult)
                ins.then_inc(hot, 1)

            def one_hot_group(group):
                one_hots(group, 0)
                with dve.Fori(0, (GROUP - 2) // UNROLL) as i:
                    for j in range(UNROLL):
                        one_hots(group, i * UNROLL + (j + 1), src=j not in SCALAR_HOT)
                one_hots(group, GROUP - 1, last=True)

            def decode(group):
                dve.wait_ge(unloaded, T * (group + 1))
                if group >= 2:
                    dve.wait_ge(summed, group - 1)
                to_low, to_high = (low[:], high[:, :, 0:HI]) if group else (total_lo, total_hi)
                nc.vector.tensor_single_scalar(to_low, packed[:, group % 2], 2 ** FIELD - 1, ALU.bitwise_and)
                nc.vector.tensor_single_scalar(to_high, packed[:, group % 2, :, 0:HI], FIELD, ALU.logical_shift_right).then_inc(decoded, 1)

            one_hot_group(0)
            dve.wait_ge(x_in, 16)
            normalize(nc, own, g, 0, g.x, g.xn, xn_ready)
            one_hot_group(1)
            decode(0)
            dve.wait_ge(xn_ready, T)
            heads = g.xn[:].rearrange("p t (h o) -> p t h o", o=MO)
            own.add(nc.vector.tensor_reduce(mean[:], heads, AX.X, ALU.add))
            own.settle()
            own.add(nc.vector.tensor_single_scalar(mean[:], mean[:], 1.0 / MO, ALU.mult))
            own.settle()
            own.add(nc.vector.tensor_tensor(dev[:], heads, mean[:].unsqueeze(3).to_broadcast([R, T, MH, MO]), ALU.subtract))
            own.settle()
            own.add(nc.vector.tensor_tensor(sq[:], dev[:], dev[:], ALU.mult))
            own.settle()
            nc.vector.tensor_reduce(var[:], sq[:], AX.X, ALU.add).then_inc(sq_ready, 1)
            dve.wait_ge(dev_ready, 1)
            own.add(nc.vector.reciprocal(var[:], var[:]))
            own.settle()
            nc.vector.tensor_tensor(dev[:], dev[:], var[:].unsqueeze(3).to_broadcast([R, T, MH, MO]), ALU.mult).then_inc(dn_ready, 1)
            one_hot_group(2)
            decode(1)
            dve.wait_ge(h_ready, 3)
            dve.wait_ge(gat_in, 64)
            for av, to in ((av_src, g.score_src), (av_dst, g.score_dst)):
                own.add(nc.vector.tensor_tensor(prod[:], g.h[:, :, :, 0:GO], av[:].unsqueeze(1).to_broadcast([R, T, GH, GO]), ALU.mult))
                own.settle()
                own.add(nc.vector.tensor_reduce(to[:], prod[:], AX.X, ALU.add))
                own.settle()
            one_hot_group(3)
            decode(2)
            one_hot_group(4)
            decode(3)
            dve.wait_ge(base, 1)
            for t in range(T):
                dve.wait_ge(out_mm, min(t // 2 * 2 + 2, T))
                nc.vector.tensor_tensor(g.x1[:, t], g.x1[:, t], aux[t // 2][0:R, (t % 2) * D:(t % 2 + 1) * D], ALU.add)
            decode(4)
            dve.wait_ge(decoded, GROUPS)
            dve.wait_ge(earlier_counts, 1)
            nc.vector.tensor_tensor(g.edges[:, :, 0:LO], g.edges[:, :, 0:LO], low[:], ALU.add)
            nc.vector.tensor_tensor(g.edges[:, :, LO:N], g.edges[:, :, LO:N], high[:, :, 0:HI], ALU.add)

        @block.scalar
        def _(act):
            def source_hots(group):
                with act.Fori(0, BODIES) as body:
                    before = body * PER_BODY + group * BODIES * PER_BODY
                    act.wait_ge(src_hot, before + 1)
                    for n, j in enumerate(SCALAR_HOT):
                        c = body * UNROLL + (j + 1 + GROUP * group)
                        nc.scalar.activation(away[:, n], node_no[:, 0:LO + 1], ACT.Abs, bias=neg_column[:, bass.ds(c, 1)]).then_inc(away_ready, 1)
                    for n, j in enumerate(SCALAR_HOT):
                        i = body * UNROLL + (j + 1)
                        c = i + GROUP * group
                        if group:
                            act.wait_ge(hot_used, i + ((GROUP - 1) * (group - 1) + 1))
                        act.wait_ge(away_ready, before + (n + 1))
                        nc.scalar.activation(hot_src[:, bass.ds(i, 1), :].rearrange("p a n -> p (a n)"), away[:, n], ACT.Relu,
                                             bias=field[:, bass.ds(c, 1)], scale=neg_field[:, bass.ds(c, 1)]).then_inc(src_hot, 1)

            def unload(group):
                for t in range(T):
                    act.wait_ge(counted, T * group + t + 1)
                    if group >= 2:
                        act.wait_ge(decoded, group - 1)
                    nc.scalar.copy(packed[:, group % 2, t], cnt[t][0:R, 0:LO]).then_inc(unloaded, 1)

            act.wait_ge(consts, 1)
            act.wait_ge(split_edges, 1)
            nc.scalar.mul(neg_column[:], column[:], -1.0)
            nc.scalar.mul(neg_field[:], field[:], -1.0).then_inc(src_hot, 1)
            source_hots(0)
            source_hots(1)
            unload(0)
            source_hots(2)
            unload(1)
            act.wait_ge(xt_mm, 1)
            nc.scalar.copy(g.xT[:, 0, 0:4 * R], aux[0][:, 0:4 * R])
            nc.scalar.copy(g.xT[:, 1, 0:4 * R], aux[2][:, 0:4 * R])
            nc.scalar.copy(g.xT[:, :, 4 * R:N], aux[1][:, 0:2 * R].rearrange("p (k n) -> p k n", k=KB)).then_inc(xt_ready, 1)
            act.wait_ge(zeros, 5)
            for i in range(3):
                n = min(2, T - 2 * i)
                act.wait_ge(h_mm, min(2 * i + 2, T))
                nc.scalar.copy(g.h[:, 2 * i:2 * i + n, :, 0:GO],
                               aux[i][0:R, 0:n * D].rearrange("p (t h o) -> p t h o", t=n, h=GH)).then_inc(h_ready, 1)
            source_hots(3)
            unload(2)
            source_hots(4)
            unload(3)
            act.wait_ge(kv_mm, 2)
            act.wait_ge(zeros, 1)
            for k in range(KB):
                for b in range(P // MO):
                    q = slice(b * MO, (b + 1) * MO)
                    last = nc.scalar.mul(kv[q, k, q], aux[k][q, q], 1.0 / N)
            last.then_inc(kv_block, 1)
            act.wait_ge(summed, GROUPS - 2)
            nc.scalar.copy(g.edges[:, :, 0:N], total[:]).then_inc(earlier_counts, 1)
            unload(4)

        @block.tensor
        def _(pe):
            def count(group, i, first=False, last=False):
                for t in range(T):
                    if first and group:
                        pe.wait_ge(unloaded, T * (group - 1) + t + 1)
                    mm = nc.tensor.matmul(cnt[t][0:R, 0:LO], hot_dst[:, bass.ds(i, 1), t * R:(t + 1) * R].rearrange("p a n -> p (a n)"),
                                          hot_src[:, bass.ds(i, 1), 0:LO].rearrange("p a n -> p (a n)"), start=first, stop=last)
                    if last:
                        mm.then_inc(counted, 1)
                if not last:
                    mm.then_inc(hot_used, 1)

            def count_group(group):
                pe.wait_ge(hot, GROUP * group + 1)
                count(group, 0, first=True)
                with pe.Fori(0, BODIES) as i:
                    pe.wait_ge(hot, i * UNROLL + (UNROLL + GROUP * group + 1))
                    pe.wait_ge(src_hot, i * PER_BODY + (BODIES * group * PER_BODY + PER_BODY + 1))
                    for j in range(UNROLL):
                        count(group, i * UNROLL + (j + 1))
                pe.wait_ge(hot, GROUP * (group + 1))
                count(group, GROUP - 1, last=True)

            count_group(0)
            count_group(1)
            pe.wait_ge(xn_ready, T)
            pe.wait_ge(consts, 3)
            for t in range(T):
                for k in range(KB):
                    bank, at = (aux[2 * k], t * R) if t < 4 else (aux[1], k * R)
                    mm = nc.tensor.transpose(bank[:, at:at + R], g.xn[:, t, k * P:(k + 1) * P], g.ident[0:R, 0:R])
            mm.then_inc(xt_mm, 1)
            pe.wait_ge(xt_ready, 1)
            pe.wait_ge(gat_in, 64)
            for t in range(T):
                for k in range(KB):
                    mm = nc.tensor.matmul(aux[t // 2][0:R, (t % 2) * D:(t % 2 + 1) * D], g.xT[:, k, t * R:(t + 1) * R],
                                          w_gat[:, k].rearrange("p h o -> p (h o)"), start=k == 0, stop=k == KB - 1)
                mm.then_inc(h_mm, 1)
            count_group(2)
            count_group(3)
            pe.wait_ge(kv_in, 2)
            pe.wait_ge(h_ready, 3)
            for k in range(KB):
                for t in range(T):
                    mm = nc.tensor.matmul(aux[k][:, 0:P], key[:, t, k * P:(k + 1) * P], val[:, t, k * P:(k + 1) * P],
                                          start=t == 0, stop=t == T - 1)
                mm.then_inc(kv_mm, 1)
            pe.wait_ge(kv_block, 1)
            for t in range(T):
                for k in range(KB):
                    at = (t % 2) * D + k * P
                    mm = nc.tensor.matmul(aux[t // 2][0:R, at:at + P], g.xT[:, k, t * R:(t + 1) * R], kv[:, k], start=True, stop=True)
                mm.then_inc(out_mm, 1)
            count_group(4)


def attend(nc, inp, g):
    with ExitStack() as ctx:
        a = Scope(nc, ctx, "gat")
        mask = a.sb("mask", [R, T, NF])
        diag = a.sb("diag", [R, 3, NF])
        junk = a.sb("junk", [R, 2, NF])
        top = a.sb("top", [R, T, GH])
        above, below, src_leak = a.sb("above", [R, T, GH]), a.sb("below", [R, T, GH]), a.sb("src_leak", [R, T, GH])
        e_pos, e_neg = a.sb("e_pos", [R, 2, T, NF]), a.sb("e_neg", [R, 2, T, NF])
        sumsT = a.sb("sumsT", [GO + 1, NF])
        den = a.sb("den", [R, 2, T])
        agg = a.sb("agg", [R, 2, T, GO])
        slot = [a.ps(f"slot{i}", [P, 2, BANK]) for i in range(3)]
        out = a.ps("agg_ps", [P, 2, BANK])
        SRC, ABOVE, BELOW = range(3)
        ORDER = ((SRC, 0), (SRC, 1), (ABOVE, 0), (BELOW, 0), (SRC, 2), (ABOVE, 1), (BELOW, 1), (SRC, 3),
                 (ABOVE, 2), (BELOW, 2), (ABOVE, 3), (BELOW, 3))
        assert GH == 4
        (turned, copied, degrees, diag_made, row_mm, above_used, below_used, weights, agg_mm, sums_copied, back_mm, agg_used, vec, maxed,
         leaked, level_ready) = (a.sem(n) for n in ("turned", "copied", "degrees", "diag_made", "row_mm", "above_used", "below_used", "weights",
                                       "agg_mm", "sums_copied", "back_mm", "agg_used", "vec", "maxed", "leaked", "level_ready"))
        block = ctx.enter_context(nc.Block())

        @block.gpsimd
        def _(pool_eng):
            nc.gpsimd.tensor_single_scalar(src_leak[:], g.score_src[:], LEAK, ALU.mult).then_inc(leaked, 1)
            for i in range(3):
                nc.gpsimd.memset(diag[:, i, N:NF], 0.0)
            for n, (kind, h) in enumerate(ORDER):
                if kind != SRC:
                    pool_eng.wait_ge(level_ready, h + 1)
                if n >= 3:
                    pool_eng.wait_ge(row_mm, n - 2)
                score = (g.score_src, above, below)[kind]
                nc.gpsimd.tensor_tensor(diag[:, n % 3, 0:N].rearrange("p (t j) -> p t j", t=T),
                                        g.ident[0:R, 0:R].unsqueeze(1).to_broadcast([R, T, R]),
                                        score[:, :, h:h + 1].to_broadcast([R, T, R]), ALU.mult).then_inc(diag_made, 1)
            pool_eng.wait_ge(degrees, T)
            nc.gpsimd.tensor_single_scalar(g.deg[:], g.deg[:], 1.0, ALU.add).then_inc(degrees, 1)
            pool_eng.wait_ge(degrees, T + 1)
            nc.gpsimd.tensor_tensor(g.deg[:], g.deg[:], g.minus_half[:], ALU.pow)

        @block.tensor
        def _(pe):
            for s in range(T):
                if s >= 3:
                    pe.wait_ge(copied, s - 2)
                for t in range(T):
                    to = slot[s % 3][0:R, t // 4, (t % 4) * R:(t % 4 + 1) * R]
                    mm = nc.tensor.transpose(to, g.edges[:, t, s * R:(s + 1) * R], g.ident[0:R, 0:R])
                mm.then_inc(turned, 1)

            def row(kind, h):
                n = ORDER.index((kind, h))
                pe.wait_ge(diag_made, n + 1)
                if h == 0:
                    pe.wait_ge(copied, T)
                elif kind == SRC:
                    pe.wait_ge(maxed, T * h)
                else:
                    pe.wait_ge(above_used if kind == ABOVE else below_used, T * h)
                for c in range(2):
                    mm = nc.tensor.matmul(slot[kind][0:R, c, 0:CH], g.ones[0:R, 0:R], diag[:, n % 3, c * CH:(c + 1) * CH],
                                          start=True, stop=True)
                mm.then_inc(row_mm, 1)

            def aggregate(h):
                if h:
                    pe.wait_ge(agg_used, h)
                for s in range(T):
                    pe.wait_ge(weights, T * h + s + 1)
                    for c in range(2):
                        mm = nc.tensor.matmul(out[0:GO + 1, c, 0:CH], g.h[:, s, h, :], e_pos[:, h % 2, s, c * CH:(c + 1) * CH],
                                              start=s == 0, stop=s == T - 1)
                mm.then_inc(agg_mm, 1)

            def turn_back(h):
                pe.wait_ge(sums_copied, h + 1)
                for t in range(T):
                    mm = nc.tensor.transpose(out[0:R, 0, t * (GO + 1):(t + 1) * (GO + 1)], sumsT[:, t * R:(t + 1) * R],
                                             g.ident[0:GO + 1, 0:GO + 1])
                mm.then_inc(back_mm, 1)

            for kind, h in ORDER[:7]:
                row(kind, h)
            aggregate(0)
            for kind, h in ORDER[7:10]:
                row(kind, h)
            turn_back(0)
            aggregate(1)
            for kind, h in ORDER[10:]:
                row(kind, h)
            turn_back(1)
            aggregate(2)
            turn_back(2)
            aggregate(3)
            turn_back(3)

        @block.scalar
        def _(act):
            for s in range(T):
                act.wait_ge(turned, s + 1)
                nc.scalar.copy(g.edgesT[:, s, 0:4 * R], slot[s % 3][0:R, 0, 0:4 * R])
                nc.scalar.copy(g.edgesT[:, s, 4 * R:N], slot[s % 3][0:R, 1, 0:R]).then_inc(copied, 1)

            def exponentials(h):
                if h >= 2:
                    act.wait_ge(agg_mm, h - 1)
                for kind, e, score, done in ((ABOVE, e_pos, g.score_src, above_used), (BELOW, e_neg, src_leak, below_used)):
                    act.wait_ge(row_mm, ORDER.index((kind, h)) + 1)
                    for s in range(T):
                        nc.scalar.activation(halves(e[:, h % 2, s]), slot[kind][0:R, :, 0:CH], ACT.Exp,
                                             bias=score[:, s, h:h + 1]).then_inc(done, 1)

            def copy_sums(h):
                act.wait_ge(agg_mm, h + 1)
                nc.scalar.copy(halves(sumsT[:]), out[0:GO + 1, :, 0:CH]).then_inc(sums_copied, 1)

            act.wait_ge(leaked, 1)
            exponentials(0)
            exponentials(1)
            copy_sums(0)
            exponentials(2)
            copy_sums(1)
            exponentials(3)
            copy_sums(2)
            copy_sums(3)

        @block.vector
        def _(dve):
            own = Own(dve, vec)
            own.add(nc.vector.tensor_scalar(mask[:], g.edges[:], 0.0, NONE, ALU.is_equal, ALU.mult))
            own.settle()

            def levels(h):
                dve.wait_ge(row_mm, ORDER.index((SRC, h)) + 1)
                for t in range(T):
                    n = T * h + t
                    if n >= 2:
                        dve.wait_ge(maxed, n - 1)
                    nc.vector.tensor_tensor_reduce(halves(junk[:, n % 2]), halves(mask[:, t]), slot[SRC][0:R, :, 0:CH],
                                                   1.0, NONE, ALU.add, ALU.max, top[:, t, h:h + 1]).then_inc(maxed, 1)
                dve.wait_ge(maxed, T * (h + 1))
                best, score = top[:, :, h], g.score_dst[:, :, h]
                own.add(nc.vector.scalar_tensor_tensor(best, best, 0.1 * NONE, best, ALU.is_gt, ALU.mult))
                own.settle()
                own.add(nc.vector.tensor_tensor(best, best, score, ALU.add))
                own.settle()
                own.add(nc.vector.scalar_tensor_tensor(best, best, LEAK, best, ALU.mult, ALU.max))
                own.settle()
                nc.vector.tensor_tensor(above[:, :, h], score, best, ALU.subtract)
                nc.vector.scalar_tensor_tensor(below[:, :, h], score, LEAK, best, ALU.mult, ALU.subtract).then_inc(level_ready, 1)

            def weigh(h):
                dve.wait_ge(copied, T)
                for s in range(T):
                    dve.wait_ge(above_used, T * h + s + 1)
                    dve.wait_ge(below_used, T * h + s + 1)
                    b = h % 2
                    own.add(nc.vector.tensor_tensor(e_pos[:, b, s], e_pos[:, b, s], e_neg[:, b, s], ALU.max))
                    own.settle()
                    nc.vector.scalar_tensor_tensor(e_pos[:, b, s], e_pos[:, b, s], 1.0, g.edgesT[:, s], ALU.min, ALU.mult).then_inc(weights, 1)

            def finish(h):
                dve.wait_ge(back_mm, h + 1)
                b = h % 2
                sums = out[0:R, 0, 0:T * (GO + 1)].rearrange("p (t o) -> p t o", t=T)
                own.add(nc.vector.tensor_single_scalar(den[:, b], sums[:, :, GO], 1e-9, ALU.max))
                own.settle()
                own.add(nc.vector.reciprocal(den[:, b], den[:, b]))
                own.settle()
                nc.vector.tensor_tensor(agg[:, b], sums[:, :, 0:GO], den[:, b].unsqueeze(2).to_broadcast([R, T, GO]), ALU.mult).then_inc(agg_used, 1)
                dve.wait_ge(agg_used, h + 1)
                to = g.x1[:, :, h * GO:(h + 1) * GO]
                own.add(nc.vector.scalar_tensor_tensor(to, agg[:, b], 0.0, to, ALU.max, ALU.add))

            levels(0)
            levels(1)
            weigh(0)
            levels(2)
            weigh(1)
            finish(0)
            levels(3)
            weigh(2)
            finish(1)
            weigh(3)
            for s in range(T):
                nc.vector.tensor_reduce(g.deg[:, s:s + 1], g.edgesT[:, s], AX.X, ALU.add).then_inc(degrees, 1)
            finish(2)
            finish(3)


class Shared:

    def __init__(self, a):
        self.ident, self.ones = a.sb("ident", [P, P]), a.sb("ones", [P, P])
        self.xn, self.x1 = a.sb("xn", [R, T, D]), a.sb("x1", [R, T, D])
        self.xT = a.sb("xT", [P, KB, NF])
        self.edges = a.sb("edges", [R, T, NF])
        self.deg = a.sb("deg", [R, T])
        self.stats, self.mv = a.sb("stats", [R, T, 6]), a.sb("mv", [R, T, 2])
        self.rstd, self.minus_half = a.sb("rstd", [R, T]), a.sb("minus_half", [R, T])
        self.var_ready, self.rstd_ready = a.sem("var_ready"), a.sem("rstd_ready")


def share_attention(g, a):
    g.x = a.sb("x", [R, T, D])
    g.edgesT = a.sb("edgesT", [R, T, NF])
    g.h = a.sb("h", [R, T, GH, GO + 1])
    g.score_src, g.score_dst = a.sb("score_src", [R, T, GH]), a.sb("score_dst", [R, T, GH])


def share_layer1(g, a):
    g.xn_parts = a.parts("xn", [R, T, D])
    g.adj = a.parts("adj", [R, T, NF])
    g.att, g.vo = a.sb("att", [R, T, D]), a.sb("vo", [P, KB])


def run_experts(nc, inp, g, layer, nth):
    pre = f"L{layer}_ffn_"
    top2 = layer == 1
    names = ("expert_w1", "expert_w2", "expert_w3") if top2 else ("W1", "W2", "Wo")
    W = [inp[pre + n] for n in names]
    E = W[0].shape[0]
    PAIRS = E // 2
    BANKS = (T + 1) // 2
    with ExitStack() as ctx:
        a = Scope(nc, ctx, f"ffn{layer}")
        raw = [[a.sb(f"raw{s}_{m}", [P, KB, D]) for m in range(3)] for s in range(2)]
        w = [[a.parts(f"w{s}_{m}", [P, KB, D]) for m in range(3)] for s in range(2)]
        hid = [a.sb(f"hid{m}", [P, KB, NF]) for m in range(2)]
        hid_parts = [a.parts(f"hid{m}", [P, KB, NF]) for m in range(2)]
        xT_parts = a.parts("xT", [P, KB, NF])
        gate_w = a.sb("gate_w", [P, KB, P if top2 else E])
        gate_w2 = a.sb("gate_w2", [P, E])
        gate_b1 = a.sb("gate_b1", [P, 1])
        gate_b = a.sb("gate_b", [R, E])
        logit, prob, gate = (a.sb(n, [R, T, E]) for n in ("logit", "prob", "gate"))
        one1, one2, cand = (a.sb(n, [R, T, E]) for n in ("one1", "one2", "cand"))
        order = a.sb("order", [R, E])
        big, sums, best, second = (a.sb(n, [R, T]) for n in ("big", "sums", "best", "second"))
        gateT = a.sb("gateT", [E, N])
        b3 = a.sb("b3", [E, D])
        PAR = 1 if top2 else 5
        par = a.sb("par", [E, 2, PAR, D])
        par_col = a.sb("par_col", [P, 2, PAR, KB * E])
        exponent = a.sb("exponent", [P, 2, KB * E])
        rh = a.sb("rh", [P, NF])

        fm = [a.ps(f"fm{i}", [P, 2, BANK]) for i in range(2)]
        rt = [a.ps(f"rt{i}", [P, BANK]) for i in range(BANKS)]
        aux = a.ps("aux", [P, BANK])

        par_in, gate_in, w_in = a.sem("par_in"), a.sem("gate_in"), [a.sem(f"w_in{s}") for s in range(2)]
        xn_ready, xt_mm, xt_ready = (a.sem(n) for n in ("xn_ready", "xt_mm", "xt_ready"))
        order_ready, par_mm, par_ready, affine_ready, rh_mm, rh_ready = (
            a.sem(n) for n in ("order_ready", "par_mm", "par_ready", "affine_ready", "rh_mm", "rh_ready"))
        logit_mm, shifted, exped, gate_ready, gt_mm, gt_ready = (
            a.sem(n) for n in ("logit_mm", "shifted", "exped", "gate_ready", "gt_mm", "gt_ready"))
        fm_done, fm_free, rt_done, rt_free = (a.sem(n) for n in ("fm_done", "fm_free", "rt_done", "rt_free"))
        w_hi, w_lo, hid_hi, hid_lo, xt_lo, pads = (a.sem(n) for n in ("w_hi", "w_lo", "hid_hi", "hid_lo", "xt_lo", "pads"))
        vec, pool = a.sem("vec"), a.sem("pool")
        block = ctx.enter_context(nc.Block())

        param = (("expert_b1",), ("expert_b2",)) if top2 else (("b1", "g1", "be1", "m1", "v1"), ("b2", "g2", "be2", "m2", "v2"))

        @block.sync
        def _(sp):
            def load(e, s):
                for m in range(3):
                    sp.dma_start(raw[s][m][:], W[m][e].rearrange("(k p) h -> p k h", p=P)).then_inc(w_in[s], 16)

            for s in range(2):
                for i, name in enumerate(param[s]):
                    sp.dma_start(par[:, s, i], inp[pre + name]).then_inc(par_in, 16)
            if top2:
                sp.dma_start(gate_w[:], inp[pre + "router_w1"].rearrange("(k p) h -> p k h", p=P)).then_inc(gate_in, 16)
                sp.dma_start(gate_w2[:], inp[pre + "router_w2"]).then_inc(gate_in, 16)
                sp.dma_start(gate_b1[:], inp[pre + "router_b1"].rearrange("(p a) -> p a", a=1)).then_inc(gate_in, 16)
                sp.dma_start(gate_b[:], spread(inp[pre + "router_b2"], R)).then_inc(gate_in, 16)
                sp.dma_start(b3[:], inp[pre + "expert_b3"]).then_inc(gate_in, 16)
            else:
                sp.dma_start(gate_w[:], inp[pre + "Wr"].rearrange("(k p) e -> p k e", p=P)).then_inc(gate_in, 16)
                sp.dma_start(gate_b[:], spread(inp[pre + "br"], R)).then_inc(gate_in, 16)
                sp.dma_start(b3[:], inp[pre + "bo"]).then_inc(gate_in, 16)
            load(0, 0)
            load(1, 1)
            with sp.Fori(0, PAIRS - 1) as i:
                for s in range(2):
                    for m in range(3):
                        sp.wait_ge(w_lo, i * 6 + (3 * s + m + 1))
                        sp.dma_start(raw[s][m][:], W[m][bass.ds(i * 2 + (2 + s), 1)].rearrange("e (k p) h -> p (e k) h", p=P)).then_inc(w_in[s], 16)

        GATE_IN = 80 if top2 else 48

        @block.gpsimd
        def _(pool_eng):
            own = Own(pool_eng, pool)
            nc.gpsimd.memset(g.xT[:, :, N:NF], 0.0).then_inc(pads, 1)
            nc.gpsimd.memset(xT_parts[0][:, :, N:NF].bitcast(F32), 0.0).then_inc(pads, 1)
            if top2:
                nc.gpsimd.iota(order[:], [[-1, E]], base=E, channel_multiplier=0,
                               allow_small_or_imprecise_dtypes=True).then_inc(order_ready, 1)
            else:
                own.add(nc.gpsimd.memset(exponent[:], -0.5))
                pool_eng.wait_ge(par_ready, 1)
                bias, scale, shift, mean, var = (par_col[:, :, i] for i in range(5))
                own.add(nc.gpsimd.tensor_single_scalar(var, var, 1e-3, ALU.add))
                own.add(nc.gpsimd.tensor_tensor(bias, bias, mean, ALU.subtract))
                own.settle()
                own.add(nc.gpsimd.tensor_tensor(var, var, exponent[:], ALU.pow))
                own.settle()
                own.add(nc.gpsimd.tensor_tensor(scale, scale, var, ALU.mult))
                own.settle()
                own.add(nc.gpsimd.tensor_tensor(bias, bias, scale, ALU.mult))
                own.settle()
                nc.gpsimd.tensor_tensor(bias, bias, shift, ALU.add).then_inc(affine_ready, 1)
            deviation(nc, own, g, nth, 1e-5)

            def split_weights(e, s):
                for m in range(3):
                    pool_eng.wait_ge(w_hi, e * 3 + (m + 1))
                    rest(nc.gpsimd, w[s][m], raw[s][m]).then_inc(w_lo, 1)

            with pool_eng.Fori(0, PAIRS) as i:
                split_weights(i * 2, 0)
                split_weights(i * 2 + 1, 1)

        @block.vector
        def _(dve):
            own = Own(dve, vec)
            normalize(nc, own, g, nth, g.x1, g.xn, xn_ready)
            dve.wait_ge(pads, 2)
            for k in range(KB):
                dve.wait_ge(xt_ready, k + 1)
                rest(nc.vector, xT_parts, g.xT, (slice(None), k)).then_inc(xt_lo, 1)

            def split_weights(e, s, m, first=False):
                if not first:
                    dve.wait_ge(*((fm_done, e * 4 + (2 * m - 6)) if m < 2 else (rt_done, e * BANKS - BANKS)))
                dve.wait_ge(w_in[s], (e - s) * 24 + 48 if not first else 48)
                nc.vector.tensor_copy(w[s][m][0][:], raw[s][m][:]).then_inc(w_hi, 1)

            for e in range(2):
                for m in range(3):
                    split_weights(e, e, m, first=True)
            dve.wait_ge(gate_in, GATE_IN)
            dve.wait_ge(logit_mm, 1)
            own.add(nc.vector.tensor_tensor(logit[:], aux[0:R, 0:T * E].rearrange("p (t e) -> p t e", t=T),
                                            gate_b[:].unsqueeze(1).to_broadcast([R, T, E]), ALU.add))
            own.settle()
            own.add(nc.vector.tensor_reduce(big[:], logit[:], AX.X, ALU.max))
            own.settle()
            nc.vector.tensor_tensor(logit[:], logit[:], big[:].unsqueeze(2).to_broadcast([R, T, E]), ALU.subtract).then_inc(shifted, 1)
            dve.wait_ge(exped, 1)
            own.add(nc.vector.tensor_reduce(sums[:], prob[:], AX.X, ALU.add))
            own.settle()
            own.add(nc.vector.reciprocal(sums[:], sums[:]))
            own.settle()

            def over_experts(x):
                return x[:].unsqueeze(2).to_broadcast([R, T, E])

            if not top2:
                nc.vector.tensor_tensor(gate[:], prob[:], over_experts(sums), ALU.mult).then_inc(gate_ready, 1)
            else:
                own.add(nc.vector.tensor_tensor(prob[:], prob[:], over_experts(sums), ALU.mult))
                own.settle()

                def pick(one, value):
                    own.add(nc.vector.tensor_reduce(value[:], prob[:], AX.X, ALU.max))
                    own.settle()
                    own.add(nc.vector.tensor_tensor(cand[:], prob[:], over_experts(value), ALU.is_equal))
                    own.settle()
                    own.add(nc.vector.tensor_tensor(cand[:], cand[:], order[:].unsqueeze(1).to_broadcast([R, T, E]), ALU.mult))
                    own.settle()
                    own.add(nc.vector.tensor_reduce(big[:], cand[:], AX.X, ALU.max))
                    own.settle()
                    own.add(nc.vector.tensor_tensor(one[:], cand[:], over_experts(big), ALU.is_equal))
                    own.settle()

                dve.wait_ge(order_ready, 1)
                pick(one1, best)
                own.add(nc.vector.scalar_tensor_tensor(prob[:], one1[:], -2.0, prob[:], ALU.mult, ALU.add))
                own.settle()
                pick(one2, second)
                nc.vector.tensor_tensor(second[:], second[:], best[:], ALU.subtract).then_inc(shifted, 1)
                dve.wait_ge(exped, 2)
                own.add(nc.vector.tensor_single_scalar(sums[:], second[:], 1.0, ALU.add))
                own.settle()
                own.add(nc.vector.reciprocal(sums[:], sums[:]))
                own.add(nc.vector.tensor_tensor(one2[:], one2[:], over_experts(second), ALU.mult))
                own.settle()
                own.add(nc.vector.tensor_tensor(one1[:], one1[:], one2[:], ALU.add))
                own.settle()
                nc.vector.tensor_tensor(gate[:], one1[:], over_experts(sums), ALU.mult).then_inc(gate_ready, 1)

            for b in range(BANKS):
                n = min(2, T - 2 * b)
                dve.wait_ge(rt_done, b + 1)
                to = g.x1[:, 2 * b:2 * b + n]
                nc.vector.tensor_tensor(to, to, rt[b][0:R, 0:n * D].rearrange("p (t d) -> p t d", t=n), ALU.add).then_inc(rt_free, 1)

            def add_expert(e):
                for b in range(BANKS):
                    dve.wait_ge(rt_done, e * BANKS + (BANKS + b + 1))
                    dve.wait_ge(rt_free, e * BANKS + (b + 1))
                    for t in range(2 * b, min(2 * b + 2, T)):
                        at = t % 2 * D
                        ins = nc.vector.scalar_tensor_tensor(g.x1[:, t], rt[b][0:R, at:at + D], gate[:, t, bass.ds(e, 1)], g.x1[:, t],
                                                             ALU.mult, ALU.add)
                    ins.then_inc(rt_free, 1)

            def hidden_rest(e, m):
                for k in range(KB):
                    dve.wait_ge(fm_free, e * 4 + (2 * m + k + 1))
                    rest(nc.vector, hid_parts[m], hid[m], (slice(None), k)).then_inc(hid_lo, 1)

            def expert(e, s, more=True, last=False):
                hidden_rest(e, 1)
                if more:
                    split_weights(e + 2, s, 0)
                if not last:
                    hidden_rest(e + 1, 0)
                if more:
                    split_weights(e + 2, s, 1)
                add_expert(e)
                if more:
                    split_weights(e + 2, s, 2)

            hidden_rest(0, 0)
            with dve.Fori(0, PAIRS - 1) as i:
                expert(i * 2, 0)
                expert(i * 2 + 1, 1)
            expert(E - 2, 0, more=False)
            expert(E - 1, 1, more=False, last=True)

        @block.scalar
        def _(act):
            act.wait_ge(par_mm, 1)
            nc.scalar.copy(par_col[:].rearrange("p m i e -> p (m i e)"), rt[0][:, 0:2 * PAR * KB * E]).then_inc(par_ready, 1)
            for k in range(KB):
                act.wait_ge(xt_mm, k + 1)
                for to in (xT_parts[0], g.xT):
                    nc.scalar.copy(to[:, k, 0:4 * R], fm[k][:, 0, 0:4 * R])
                    ins = nc.scalar.copy(to[:, k, 4 * R:N], fm[k][:, 1, 0:R])
                ins.then_inc(xt_ready, 1)
            act.wait_ge(gate_in, GATE_IN)
            if top2:
                act.wait_ge(rh_mm, 1)
                nc.scalar.activation(halves(rh[:]), fm[0][:, :, 0:CH], ACT.Relu, bias=gate_b1[:]).then_inc(rh_ready, 1)
            act.wait_ge(shifted, 1)
            nc.scalar.activation(prob[:], logit[:], ACT.Exp).then_inc(exped, 1)
            if top2:
                act.wait_ge(shifted, 2)
                nc.scalar.activation(second[:], second[:], ACT.Exp).then_inc(exped, 1)
            act.wait_ge(gt_mm, 1)
            nc.scalar.copy(gateT[:, 0:4 * R], rt[0][0:E, 0:4 * R])
            nc.scalar.copy(gateT[:, 4 * R:N], rt[1][0:E, 0:R]).then_inc(gt_ready, 1)
            act.wait_ge(par_ready, 1)
            if not top2:
                act.wait_ge(affine_ready, 1)

            def unload(e, m):
                for k in range(KB):
                    act.wait_ge(fm_done, e * 4 + (2 * m + k + 1))
                    at = bass.ds(e + k * E, 1)
                    scale = 1.0 if top2 else par_col[:, m, 1, at]
                    for to, done in ((hid_parts[m][0], hid_hi), (hid[m], fm_free)):
                        nc.scalar.activation(halves(to[:, k]), fm[k][:, :, 0:CH], ACT.Relu,
                                             bias=par_col[:, m, 0, at], scale=scale).then_inc(done, 1)

            with act.Fori(0, E) as e:
                unload(e, 0)
                unload(e, 1)

        @block.tensor
        def _(pe):
            pe.wait_ge(par_in, 16 * 2 * PAR)
            for m in range(2):
                for i in range(PAR):
                    for k in range(KB):
                        at = ((m * PAR + i) * KB + k) * E
                        mm = nc.tensor.transpose(rt[0][:, at:at + E], par[:, m, i, k * P:(k + 1) * P], g.ident[0:E, 0:E])
            mm.then_inc(par_mm, 1)
            for k in range(KB):
                for t in range(T):
                    pe.wait_ge(xn_ready, t + 1)
                    mm = nc.tensor.transpose(fm[k][:, t // 4, t % 4 * R:(t % 4 + 1) * R], g.xn[:, t, k * P:(k + 1) * P], g.ident[0:R, 0:R])
                mm.then_inc(xt_mm, 1)
            pe.wait_ge(gate_in, GATE_IN)
            if top2:
                pe.wait_ge(xt_ready, KB)
                for k in range(KB):
                    for c in range(2):
                        mm = nc.tensor.matmul(fm[0][:, c, 0:CH], gate_w[:, k], g.xT[:, k, c * CH:(c + 1) * CH], start=k == 0, stop=k == KB - 1)
                mm.then_inc(rh_mm, 1)
                pe.wait_ge(rh_ready, 1)
                for t in range(T):
                    mm = nc.tensor.matmul(aux[0:R, t * E:(t + 1) * E], rh[:, t * R:(t + 1) * R], gate_w2[:], start=True, stop=True)
            else:
                pe.wait_ge(xt_ready, KB)
                for t in range(T):
                    for k in range(KB):
                        mm = nc.tensor.matmul(aux[0:R, t * E:(t + 1) * E], g.xT[:, k, t * R:(t + 1) * R], gate_w[:, k], start=k == 0, stop=k == KB - 1)
            mm.then_inc(logit_mm, 1)

            def hidden(e, m, s, first=False):
                src, src_lo = (xT_parts, xt_lo) if m == 0 else (hid_parts[0], hid_lo)
                for f in range(KB):
                    if not first:
                        pe.wait_ge(fm_free, e * 4 + (2 * m + f - 1))
                    for n, (i, j) in enumerate(PASSES):
                        if f == 0 and n == 0:
                            pe.wait_ge(w_hi, e * 3 + (m + 1))
                        elif f == 0 and i:
                            pe.wait_ge(w_lo, e * 3 + (m + 1))
                        for k in range(KB):
                            if f == 0 and m == 1 and n == 0:
                                pe.wait_ge(hid_hi, e * 4 + (k + 1))
                            elif f == 0 and j:
                                pe.wait_ge(src_lo, e * 4 + (k + 1) if m else k + 1)
                            for c in range(2):
                                mm = nc.tensor.matmul(fm[f][:, c, 0:CH], w[s][m][i][:, k, f * P:(f + 1) * P], src[j][:, k, c * CH:(c + 1) * CH],
                                                      start=n == 0 and k == 0, stop=n == 2 and k == KB - 1)
                    mm.then_inc(fm_done, 1)

            def last_layer(e, s):
                pe.wait_ge(hid_lo, e * 4 + 4)
                pe.wait_ge(w_lo, e * 3 + 3)
                for t in range(T):
                    b, at = t // 2, t % 2 * D
                    if t % 2 == 0:
                        pe.wait_ge(rt_free, e * BANKS + (b + 1))
                    for n, (i, j) in enumerate(PASSES):
                        for k in range(KB):
                            mm = nc.tensor.matmul(rt[b][0:R, at:at + D], hid_parts[1][j][:, k, t * R:(t + 1) * R], w[s][2][i][:, k],
                                                  start=n == 0 and k == 0, stop=n == 2 and k == KB - 1)
                    if t % 2 or t == T - 1:
                        mm.then_inc(rt_done, 1)

            hidden(0, 0, 0, first=True)
            pe.wait_ge(gate_ready, 1)
            pe.wait_ge(par_ready, 1)
            for t in range(T):
                mm = nc.tensor.transpose(rt[t // 4][0:E, t % 4 * R:(t % 4 + 1) * R], gate[:, t], g.ident[0:R, 0:R])
            mm.then_inc(gt_mm, 1)
            pe.wait_ge(gt_ready, 1)
            for t in range(T):
                mm = nc.tensor.matmul(rt[t // 2][0:R, t % 2 * D:(t % 2 + 1) * D], gateT[:, t * R:(t + 1) * R], b3[:], start=True, stop=True)
                if t % 2 or t == T - 1:
                    mm.then_inc(rt_done, 1)

            def pair(e, last=False):
                hidden(e, 1, 0)
                hidden(e + 1, 0, 1)
                last_layer(e, 0)
                hidden(e + 1, 1, 1)
                if not last:
                    hidden(e + 2, 0, 0)
                last_layer(e + 1, 1)

            with pe.Fori(0, PAIRS - 1) as i:
                pair(i * 2)
            pair(E - 2, last=True)


def run_heads(nc, inp, g, nth):
    H, KD = inp["L1_mix_bq"].shape
    SCALE = float(KD) ** -0.25
    EPS = 1e-6 * float(inp["L1_mix_proj"].shape[0]) ** 0.5
    OUT_BANK = (0, 1, 2, 0, 1)
    ROW = D + 2
    UQ, K0, Q0 = 4, 6, 8
    WQ, WK, WV, WO = range(4)
    with ExitStack() as ctx:
        a = Scope(nc, ctx, "heads")
        raw = [a.sb(f"raw{m}", [P, KB, D]) for m in range(4)]
        wgt = [a.parts(f"w{m}", [P, KB, D]) for m in range(4)]
        proj, projT = a.sb("proj", [P, KB, KD]), a.parts("projT", [P, KB, KD])
        hb = a.sb("hb", [H, 3, KD])
        hb_col = a.sb("hb_col", [P, 3, KB, H])
        bo = a.sb("bo", [R, D])
        minus = a.sb("minus", [P, P])
        xT = a.parts("xT", [P, KB, NF])
        qT, kT = a.sb("qT", [P, KB, NF]), a.sb("kT", [P, KB, NF])
        qT_parts, kT_parts = a.parts("qT", [P, KB, NF]), a.parts("kT", [P, KB, NF])
        q_sq, k_sq = a.sb("q_sq", [P, KB, NF]), a.sb("k_sq", [P, KB, NF])
        q_sum, k_sum = a.sb("q_sum", [P, NF]), a.sb("k_sum", [P, NF])
        exp_k, exp_q = g.xn, g.xT
        phi_q, phi_k = a.parts("phi_q", [P, KB, NF]), a.parts("phi_k", [R, T, KD])
        sqk = a.sb("sqk", [R, T])
        pxT, kvT = a.parts("pxT", [P, KB, KD]), a.parts("kvT", [P, KB, KD])
        kvo = a.parts("kvo", [P, KB, ROW])
        rec = a.sb("rec", [R, T])
        dinv_diag, dinv_row = a.sb("dinv_diag", [R, NF]), a.sb("dinv_row", [R, NF])

        fm = [a.ps(f"fm{i}", [P, 2, BANK]) for i in range(2)]
        rt = [a.ps(f"rt{i}", [P, BANK]) for i in range(3)]
        aux = a.ps("aux", [P, BANK])

        proj_in, bias_in, w_in = a.sem("proj_in"), a.sem("bias_in"), [a.sem(f"w_in{m}") for m in range(4)]
        w_hi, w_lo = [a.sem(f"w_hi{m}") for m in range(4)], [a.sem(f"w_lo{m}") for m in range(4)]
        (xn_ready, xt_mm, xt_hi, xt_lo, consts, proj_mm, proj_hi, proj_lo, hb_mm, hb_ready, fm_done, fm_free, squared, qk_lo,
         summed, aux_done, sqk_ready, aux_free, uk_done, uk_exp, pk_ready, pq_ready, px_done, px_hi, px_lo, kvt_done,
         kvt_hi, kvt_lo, kvo_done, kvo_hi, kvo_lo, out_done, out_free, rec_ready, vec, pool, diag_ready, dinv_mm,
         loops_added, adj_ready) = (a.sem(n) for n in (
             "xn_ready", "xt_mm", "xt_hi", "xt_lo", "consts", "proj_mm", "proj_hi", "proj_lo", "hb_mm", "hb_ready",
             "fm_done", "fm_free", "squared", "qk_lo", "summed", "aux_done", "sqk_ready", "aux_free", "uk_done", "uk_exp",
             "pk_ready", "pq_ready", "px_done", "px_hi", "px_lo", "kvt_done", "kvt_hi", "kvt_lo", "kvo_done", "kvo_hi",
             "kvo_lo", "out_done", "out_free", "rec_ready", "vec", "pool", "diag_ready", "dinv_mm", "loops_added", "adj_ready"))
        block = ctx.enter_context(nc.Block())

        @block.sync
        def _(sp):
            def load(h, m):
                if m == WO:
                    src = inp["L1_mix_Wo"][bass.ds(h, 1)].rearrange("a (k p) d -> p (a k) d", p=P)
                else:
                    src = inp["L1_mix_" + ("Wq", "Wk", "Wv")[m]][:, bass.ds(h, 1)].rearrange("(k p) a m -> p k (a m)", p=P)
                sp.dma_start(raw[m][:], src).then_inc(w_in[m], 16)

            load(0, WK)
            load(0, WQ)
            sp.dma_start(proj[:], inp["L1_mix_proj"].rearrange("(k p) d -> p k d", p=P)).then_inc(proj_in, 16)
            for i, n in enumerate(("bq", "bk", "bv")):
                sp.dma_start(hb[:, i], inp["L1_mix_" + n]).then_inc(bias_in, 16)
            sp.dma_start(bo[:], spread(inp["L1_mix_bo"], R)).then_inc(bias_in, 16)
            load(0, WV)
            load(0, WO)
            with sp.Fori(0, H - 1) as h:
                for m in (WK, WQ, WV, WO):
                    sp.wait_ge(w_lo[m], h + 1)
                    if m == WO:
                        sp.wait_ge(aux_done, h * 2 + 2)
                    load(h + 1, m)

        @block.gpsimd
        def _(pool_eng):
            own = Own(pool_eng, pool)
            nc.gpsimd.memset(dinv_diag[:, N:NF], 0.0).then_inc(consts, 1)
            nc.gpsimd.memset(minus[:], -0.5).then_inc(consts, 1)
            for part in range(2):
                nc.gpsimd.memset(xT[part][:, :, N:NF].bitcast(F32), 0.0).then_inc(consts, 1)
                nc.gpsimd.memset(kvo[part][:, :, D + 1:ROW].bitcast(F32), 0.0).then_inc(consts, 1)
            for t in range(T):
                at = slice(t * R, (t + 1) * R)
                nc.gpsimd.tensor_tensor(g.edges[:, t, at], g.edges[:, t, at], g.ident[0:R, 0:R], ALU.add).then_inc(loops_added, 1)
            deviation(nc, own, g, nth, 1e-5)

            def weights_low(h, m):
                pool_eng.wait_ge(w_hi[m], h + 1)
                rest(nc.gpsimd, wgt[m], raw[m]).then_inc(w_lo[m], 1)

            def qk_low(h, what, f):
                pool_eng.wait_ge(fm_free, h * 6 + (2 * what + f + 1))
                parts, whole = ((kT_parts, kT), (qT_parts, qT))[what]
                rest(nc.gpsimd, parts, whole, (slice(None), f)).then_inc(qk_lo, 1)

            def next_head(h):
                weights_low(h, WK)
                weights_low(h, WQ)
                weights_low(h, WV)
                qk_low(h, 0, 0)
                weights_low(h, WO)
                qk_low(h, 0, 1)
                qk_low(h, 1, 0)
                qk_low(h, 1, 1)

            weights_low(0, WK)
            weights_low(0, WQ)
            for what in range(2):
                for f in range(KB):
                    qk_low(0, what, f)
            weights_low(0, WV)
            weights_low(0, WO)
            with pool_eng.Fori(0, H - 1) as h:
                next_head(h + 1)
            for t in range(T):
                pool_eng.wait_ge(adj_ready, t + 1)
                own.add(nc.gpsimd.tensor_copy(g.adj[0][:, t], g.edges[:, t]))
                own.settle()
                rest(nc.gpsimd, g.adj, g.edges, (slice(None), t))

        @block.vector
        def _(dve):
            own = Own(dve, vec)
            normalize(nc, own, g, nth, g.x1, g.xn, xn_ready)
            dve.wait_ge(consts, 6)
            nc.vector.tensor_tensor(dinv_diag[:, 0:N].rearrange("p (t j) -> p t j", t=T),
                                    g.ident[0:R, 0:R].unsqueeze(1).to_broadcast([R, T, R]),
                                    g.deg[:].unsqueeze(2).to_broadcast([R, T, R]), ALU.mult).then_inc(diag_ready, 1)
            for k in range(KB):
                dve.wait_ge(xt_hi, k + 1)
                for c, at in ((0, slice(0, 4 * R)), (1, slice(4 * R, N))):
                    ins = nc.vector.tensor_tensor(xT[1][:, k, at], fm[k][:, c, 0:at.stop - at.start], xT[0][:, k, at].bitcast(F32), ALU.subtract)
                ins.then_inc(xt_lo, 1)
            dve.wait_ge(proj_hi, 1)
            nc.vector.tensor_tensor(projT[1][:].rearrange("p k m -> p (k m)"), rt[0][:],
                                    projT[0][:].rearrange("p k m -> p (k m)").bitcast(F32), ALU.subtract).then_inc(proj_lo, 1)
            dve.wait_ge(dinv_mm, 1)
            for c in range(2):
                nc.vector.tensor_copy(dinv_row[:, c * CH:(c + 1) * CH], rt[1 + c][0:R, 0:CH]).then_inc(dinv_mm, 1)

            def sum_squares(h, what):
                dve.wait_ge(squared, h * 4 + (2 * what + 2))
                sq, to = (k_sq, k_sum) if what == 0 else (q_sq, q_sum)
                nc.vector.tensor_tensor(to[:], sq[:, 0], sq[:, 1], ALU.add).then_inc(summed, 1)

            sum_squares(0, 0)
            dve.wait_ge(bias_in, 64)
            dve.wait_ge(xn_ready, T)
            for t in range(T):
                nc.vector.tensor_tensor(g.att[:, t], g.xn[:, t], bo[:], ALU.add).then_inc(out_free, 1)
            own.add(nc.vector.tensor_copy(g.xn_parts[0][:], g.xn[:]))
            sum_squares(0, 1)
            own.settle()
            own.add(rest(nc.vector, g.xn_parts, g.xn))
            nc.vector.memset(g.vo[:], 0.0).then_inc(aux_free, 1)
            dve.wait_ge(dinv_mm, 3)
            dve.wait_ge(loops_added, T)
            for t in range(T):
                nc.vector.scalar_tensor_tensor(g.edges[:, t], g.edges[:, t], g.deg[:, t:t + 1], dinv_row[:], ALU.mult, ALU.mult).then_inc(adj_ready, 1)
            own.settle()

            def head(h, last=False):
                dve.wait_ge(aux_done, h * 2 + 1)
                nc.vector.tensor_copy(sqk[:], aux[0:R, 0:T]).then_inc(sqk_ready, 1)
                dve.wait_ge(uk_exp, h + 1)
                nc.vector.tensor_single_scalar(phi_k[0][:], exp_k[:], EPS, ALU.add).then_inc(pk_ready, 1)
                dve.wait_ge(pk_ready, h * 2 + 1)
                nc.vector.scalar_tensor_tensor(phi_k[1][:], exp_k[:], EPS, phi_k[0][:].bitcast(F32), ALU.add, ALU.subtract).then_inc(pk_ready, 1)
                dve.wait_ge(px_hi, h + 1)
                nc.vector.tensor_tensor(pxT[1][:].rearrange("p k m -> p (k m)"), rt[0][:],
                                        pxT[0][:].rearrange("p k m -> p (k m)").bitcast(F32), ALU.subtract).then_inc(px_lo, 1)
                dve.wait_ge(aux_done, h * 2 + 2)
                nc.vector.tensor_single_scalar(kvo[0][:, :, D], aux[:, 8:8 + KB], N * EPS, ALU.add).then_inc(rec_ready, 1)
                dve.wait_ge(aux_free, h + 1)
                dve.wait_ge(rec_ready, h * (T + 1) + 1)
                nc.vector.scalar_tensor_tensor(kvo[1][:, :, D], aux[:, 8:8 + KB], N * EPS, kvo[0][:, :, D].bitcast(F32), ALU.add, ALU.subtract)
                nc.vector.tensor_tensor(g.vo[:], g.vo[:], aux[:, 16:16 + KB], ALU.add).then_inc(aux_free, 1)
                dve.wait_ge(kvt_hi, h + 1)
                nc.vector.tensor_tensor(kvT[1][:].rearrange("p k m -> p (k m)"), rt[1][:],
                                        kvT[0][:].rearrange("p k m -> p (k m)").bitcast(F32), ALU.subtract).then_inc(kvt_lo, 1)
                dve.wait_ge(fm_free, h * 6 + (UQ + 2))
                nc.vector.tensor_single_scalar(phi_q[0][:], exp_q[:], EPS, ALU.add).then_inc(pq_ready, 1)
                dve.wait_ge(pq_ready, h * 2 + 1)
                nc.vector.scalar_tensor_tensor(phi_q[1][:], exp_q[:], EPS, phi_q[0][:].bitcast(F32), ALU.add, ALU.subtract).then_inc(pq_ready, 1)
                dve.wait_ge(kvo_hi, h + 1)
                nc.vector.tensor_tensor(kvo[1][:, :, 0:D], rt[2][:].rearrange("p (k m) -> p k m", k=KB),
                                        kvo[0][:, :, 0:D].bitcast(F32), ALU.subtract).then_inc(kvo_lo, 1)
                if not last:
                    sum_squares(h + 1, 0)
                for t in range(T):
                    dve.wait_ge(out_done, h * T + (t + 1))
                    bank = rt[OUT_BANK[t]]
                    nc.vector.reciprocal(rec[:, t:t + 1], bank[0:R, D:D + 1]).then_inc(rec_ready, 1)
                    dve.wait_ge(rec_ready, h * (T + 1) + (t + 2))
                    dve.wait_ge(out_free, h * T + (t + 1))
                    nc.vector.scalar_tensor_tensor(g.att[:, t], bank[0:R, 0:D], rec[:, t:t + 1], g.att[:, t], ALU.mult, ALU.add).then_inc(out_free, 1)
                if not last:
                    sum_squares(h + 1, 1)

            with dve.Fori(0, H - 1) as h:
                head(h)
            head(H - 1, last=True)

        @block.scalar
        def _(act):
            def weights_high(h, m):
                act.wait_ge(w_in[m], h * 16 + 16)
                nc.scalar.copy(wgt[m][0][:], raw[m][:]).then_inc(w_hi[m], 1)

            weights_high(0, WK)
            weights_high(0, WQ)
            act.wait_ge(proj_mm, 1)
            nc.scalar.copy(projT[0][:].rearrange("p k m -> p (k m)"), rt[0][:]).then_inc(proj_hi, 1)
            act.wait_ge(hb_mm, 1)
            n = 2 * KB * H
            nc.scalar.mul(hb_col[:, 0:2].rearrange("p a k h -> p (a k h)"), aux[:, 0:n], SCALE)
            nc.scalar.copy(hb_col[:, 2].rearrange("p k h -> p (k h)"), aux[:, n:n + KB * H]).then_inc(hb_ready, 1)
            for k in range(KB):
                act.wait_ge(xt_mm, k + 1)
                nc.scalar.copy(xT[0][:, k, 0:4 * R], fm[k][:, 0, 0:4 * R])
                nc.scalar.copy(xT[0][:, k, 4 * R:N], fm[k][:, 1, 0:R]).then_inc(xt_hi, 1)
            act.wait_ge(hb_ready, 1)

            def unload_qk(h, f, what, bf):
                act.wait_ge(fm_done, h * 6 + (2 * what + f + 1))
                sq, parts, whole = ((k_sq, kT_parts, kT), (q_sq, qT_parts, qT))[what]
                bias = hb_col[:, 1 - what, f, bass.ds(bf, 1)]
                for to, fun, done in ((sq, ACT.Square, squared), (parts[0], ACT.Identity, None), (whole, ACT.Identity, fm_free)):
                    ins = nc.scalar.activation(halves(to[:, f]), fm[f][:, :, 0:CH], fun, bias=bias, scale=SCALE)
                    if done:
                        ins.then_inc(done, 1)

            for what in range(2):
                for f in range(KB):
                    unload_qk(0, f, what, 0)
            weights_high(0, WV)
            weights_high(0, WO)

            def features(h, f):
                act.wait_ge(fm_done, h * 6 + (UQ + f + 1))
                nc.scalar.activation(halves(exp_q[:, f]), fm[f][:, :, 0:CH], ACT.Exp).then_inc(fm_free, 1)

            def head(h, last=False):
                if not last:
                    weights_high(h + 1, WK)
                act.wait_ge(sqk_ready, h + 1)
                for b in range(3):
                    act.wait_ge(uk_done, h * 3 + (b + 1))
                    for t in range(2 * b, min(2 * b + 2, T)):
                        ins = nc.scalar.activation(exp_k[:, t], rt[b][0:R, t % 2 * KD:(t % 2 + 1) * KD], ACT.Exp, bias=sqk[:, t:t + 1])
                ins.then_inc(uk_exp, 1)
                features(h, 0)
                if not last:
                    weights_high(h + 1, WQ)
                act.wait_ge(px_done, h + 1)
                nc.scalar.copy(pxT[0][:].rearrange("p k m -> p (k m)"), rt[0][:]).then_inc(px_hi, 1)
                features(h, 1)
                act.wait_ge(kvt_done, h + 1)
                nc.scalar.copy(kvT[0][:].rearrange("p k m -> p (k m)"), rt[1][:]).then_inc(kvt_hi, 1)
                if not last:
                    weights_high(h + 1, WV)
                    unload_qk(h + 1, 0, 0, h + 1)
                act.wait_ge(kvo_done, h + 1)
                nc.scalar.copy(kvo[0][:, :, 0:D], rt[2][:].rearrange("p (k m) -> p k m", k=KB)).then_inc(kvo_hi, 1)
                if not last:
                    weights_high(h + 1, WO)
                    unload_qk(h + 1, 1, 0, h + 1)
                    unload_qk(h + 1, 0, 1, h + 1)
                    unload_qk(h + 1, 1, 1, h + 1)

            with act.Fori(0, H - 1) as h:
                head(h)
            head(H - 1, last=True)

        @block.tensor
        def _(pe):
            pe.wait_ge(proj_in, 16)
            for m in range(KB):
                for k in range(KB):
                    mm = nc.tensor.transpose(rt[0][:, k * KD + m * P:k * KD + (m + 1) * P], proj[:, m, k * P:(k + 1) * P], g.ident[:])
            mm.then_inc(proj_mm, 1)
            pe.wait_ge(bias_in, 64)
            for i in range(3):
                for k in range(KB):
                    at = (i * KB + k) * H
                    mm = nc.tensor.transpose(aux[:, at:at + H], hb[:, i, k * P:(k + 1) * P], g.ident[0:H, 0:H])
            mm.then_inc(hb_mm, 1)
            for k in range(KB):
                for t in range(T):
                    pe.wait_ge(xn_ready, t + 1)
                    mm = nc.tensor.transpose(fm[k][:, t // 4, t % 4 * R:(t % 4 + 1) * R], g.xn[:, t, k * P:(k + 1) * P], g.ident[0:R, 0:R])
                mm.then_inc(xt_mm, 1)
            pe.wait_ge(diag_ready, 1)
            for c in range(2):
                mm = nc.tensor.matmul(rt[1 + c][0:R, 0:CH], g.ones[0:R, 0:R], dinv_diag[:, c * CH:(c + 1) * CH], start=True, stop=True)
            mm.then_inc(dinv_mm, 1)

            def project(h, f, m, first=False):
                if not first:
                    pe.wait_ge(fm_free, h * 6 + ((2 if m == WQ else 0) + f - 1))
                if f == 0:
                    pe.wait_ge(w_hi[m], h + 1)
                product(pe, nc, both_halves(fm[f]), KB, lambda i, k: wgt[m][i][:, k, f * P:(f + 1) * P], lambda j, k: xT[j][:, k],
                        left_low=(w_lo[m], h + 1)).then_inc(fm_done, 1)

            def query_features(h, f):
                pe.wait_ge(fm_free, h * 6 + UQ)
                if f:
                    pe.wait_ge(fm_free, h * 6 + (UQ + f - 1))
                product(pe, nc, both_halves(fm[f]), KB, lambda i, k: projT[i][:, k, f * P:(f + 1) * P], lambda j, k: qT_parts[j][:, k],
                        right_low=(qk_lo, h * 4 + 4), more=True)
                pe.wait_ge(summed, h * 2 + 2)
                for to, at in both_halves(fm[f]):
                    mm = nc.tensor.matmul(to, minus[:], q_sum[:, at], start=False, stop=True)
                mm.then_inc(fm_done, 1)

            whole = slice(0, D)

            def head(h, last=False):
                pe.wait_ge(summed, h * 2 + 1)
                pe.wait_ge(aux_free, h + 1)
                for t in range(T):
                    mm = nc.tensor.matmul(aux[0:R, t:t + 1], k_sum[:, t * R:(t + 1) * R], minus[:, 0:1], start=True, stop=True)
                mm.then_inc(aux_done, 1)
                pe.wait_ge(qk_lo, h * 4 + 2)
                for t in range(T):
                    if t % 2 == 0:
                        pe.wait_ge(out_free, h * T + (4, 5, 3)[t // 2])
                    mm = product(pe, nc, [(rt[t // 2][0:R, t % 2 * KD:(t % 2 + 1) * KD], whole)], KB,
                                 lambda i, k: kT_parts[i][:, k, t * R:(t + 1) * R], lambda j, k: projT[j][:, k])
                    if t % 2 or t == T - 1:
                        mm.then_inc(uk_done, 1)
                query_features(h, 0)
                pe.wait_ge(pk_ready, h * 2 + 1)
                for k in range(KB):
                    mm = product(pe, nc, [(rt[0][:, k * KD:(k + 1) * KD], whole)], T,
                                 lambda i, t: g.xn_parts[i][:, t, k * P:(k + 1) * P], lambda j, t: phi_k[j][:, t],
                                 right_low=(pk_ready, h * 2 + 2))
                mm.then_inc(px_done, 1)
                for m in range(KB):
                    for t in range(T):
                        nc.tensor.matmul(aux[:, 8 + m:9 + m], exp_k[:, t, m * P:(m + 1) * P], g.ones[0:R, 0:1], start=t == 0, stop=t == T - 1)
                pe.wait_ge(w_in[WO], h * 16 + 16)
                for m in range(KB):
                    for k in range(KB):
                        mm = nc.tensor.matmul(aux[:, 16 + m:17 + m], raw[WO][:, k, m * P:(m + 1) * P], hb_col[:, 2, k, bass.ds(h, 1)],
                                              start=k == 0, stop=k == KB - 1)
                mm.then_inc(aux_done, 1)
                query_features(h, 1)
                pe.wait_ge(px_lo, h + 1)
                pe.wait_ge(w_lo[WV], h + 1)
                for f in range(KB):
                    mm = product(pe, nc, [(rt[1][:, f * KD:(f + 1) * KD], whole)], KB,
                                 lambda i, k: wgt[WV][i][:, k, f * P:(f + 1) * P], lambda j, k: pxT[j][:, k])
                mm.then_inc(kvt_done, 1)
                if not last:
                    project(h + 1, 0, WK)
                pe.wait_ge(kvt_lo, h + 1)
                pe.wait_ge(w_lo[WO], h + 1)
                for m in range(KB):
                    mm = product(pe, nc, [(rt[2][:, m * D:(m + 1) * D], whole)], KB,
                                 lambda i, k: kvT[i][:, k, m * P:(m + 1) * P], lambda j, k: wgt[WO][j][:, k])
                mm.then_inc(kvo_done, 1)
                if not last:
                    project(h + 1, 1, WK)
                    project(h + 1, 0, WQ)
                pe.wait_ge(kvo_lo, h + 1)
                pe.wait_ge(pq_ready, h * 2 + 2)
                for t in range(T):
                    if t >= 3:
                        pe.wait_ge(out_free, h * T + (T + t - 2))
                    product(pe, nc, [(rt[OUT_BANK[t]][0:R, 0:ROW], slice(0, ROW))], KB,
                            lambda i, k: phi_q[i][:, k, t * R:(t + 1) * R], lambda j, k: kvo[j][:, k]).then_inc(out_done, 1)
                if not last:
                    project(h + 1, 1, WQ)

            pe.wait_ge(xt_lo, KB)
            for m in (WK, WQ):
                for f in range(KB):
                    project(0, f, m, first=m == WK)
            pe.wait_ge(hb_ready, 1)
            pe.wait_ge(proj_lo, 1)
            pe.wait_ge(dinv_mm, 3)
            with pe.Fori(0, H - 1) as h:
                head(h)
            head(H - 1, last=True)


def convolve(nc, inp, g, nth):
    DH = inp["L1_gnn_W2"].shape[0]
    HB = DH // P
    AGG0, AGG1, FF, AGG2, H3 = 0, KB, KB + HB, 2 * KB + HB, 2 * KB + 2 * HB
    WIDE = max(T * DH, HB * NF)
    with ExitStack() as ctx:
        a = Scope(nc, ctx, "conv")
        vecs = a.sb("vecs", [R, 6, D])
        w_ff = [a.sb(f"w_ff{i}", [P, KB, D]) for i in range(2)]
        b_ff = a.sb("b_ff", [P, KB])
        bg, bg3 = a.sb("bg", [R, 2, DH]), a.sb("bg3", [P, HB])
        raw_a, raw_b = a.sb("raw_a", [P, HB, DH]), a.sb("raw_b", [P, HB, D])
        raw = [raw_b[:].rearrange("p (k a) d -> p k (a d)", k=KB), raw_a[:], raw_a[:], raw_b[:]]
        wg = [a.parts("wg1", [P, KB, DH]), a.parts("wg2", [P, HB, DH]), a.parts("wg3", [P, HB, DH]), a.parts("wfc", [P, HB, D])]
        vo_diag = a.sb("vo_diag", [P, KB, P])
        nrm, attT, ffT = g.xn, a.sb("attT", [P, KB, NF]), a.sb("ffT", [P, KB, NF])
        aggT = a.parts("aggT", [P, HB, NF])
        row = a.sb("row", [R, 2, DH])
        hid_all = a.parts("hid", [P, WIDE])
        hid = [x[0:R, 0:T * DH].rearrange("p (t d) -> p t d", t=T) for x in hid_all]
        h3T = [x[:, 0:HB * NF].rearrange("p (k n) -> p k n", k=HB) for x in hid_all]
        h3_whole = g.xT

        fm = [a.ps(f"fm{i}", [P, 2, BANK]) for i in range(2)]
        rt = [a.ps(f"rt{i}", [P, BANK]) for i in range(3)]
        aux = a.ps("aux", [P, BANK])

        ff_in, w_in, bias_in = a.sem("ff_in"), [a.sem(f"w_in{i}") for i in range(4)], a.sem("bias_in")
        fm_done, fm_free = a.sem("fm_done"), [a.sem(f"fm_free{b}") for b in range(2)]
        (zeros, w_hi, w_lo, agg_hi, h3_whole_ready, vo_ready, vo_mm, norm_done, att_ready, at_mm, at_ready, ff_mm,
         row_mm, row_added, row_hi, row_lo, vec, pool) = (a.sem(n) for n in (
             "zeros", "w_hi", "w_lo", "agg_hi", "h3_whole_ready", "vo_ready", "vo_mm", "norm_done", "att_ready", "at_mm",
             "at_ready", "ff_mm", "row_mm", "row_added", "row_hi", "row_lo", "vec", "pool"))
        block = ctx.enter_context(nc.Block())

        @block.sync
        def _(sp):
            def load(i):
                sp.dma_start(raw[i], inp["L1_gnn_" + ("W1", "W2", "W3", "Wfc")[i]].rearrange("(k p) d -> p k d", p=P)).then_inc(w_in[i], 16)

            load(0)
            for i in range(2):
                sp.dma_start(bg[:, i], spread(inp[f"L1_gnn_b{i + 1}"], R)).then_inc(bias_in, 16)
            sp.dma_start(bg3[:], inp["L1_gnn_b3"].rearrange("(k p) -> p k", p=P), allow_slow_non_contiguous=True).then_inc(bias_in, 16)
            load(1)
            for i, n in enumerate(("mix_g1", "mix_beta1", "mix_bias2", "mix_g2", "mix_beta2", "gnn_bfc")):
                sp.dma_start(vecs[:, i], spread(inp["L1_" + n], R)).then_inc(ff_in, 16)
            sp.dma_start(b_ff[:], inp["L1_mix_bias1"].rearrange("(k p) -> p k", p=P), allow_slow_non_contiguous=True).then_inc(ff_in, 16)
            for i in range(2):
                sp.dma_start(w_ff[i][:], inp[f"L1_mix_W{i + 1}"].rearrange("(k p) d -> p k d", p=P)).then_inc(ff_in, 16)
            sp.wait_ge(w_lo, 1)
            load(3)
            sp.wait_ge(w_lo, 2)
            load(2)

        FF_IN, BIAS_IN = 16 * 9, 16 * 3

        @block.gpsimd
        def _(pool_eng):
            own = Own(pool_eng, pool)
            nc.gpsimd.memset(attT[:, :, N:NF], 0.0).then_inc(zeros, 1)
            for i in range(4):
                pool_eng.wait_ge(w_hi, i + 1)
                nc.gpsimd.tensor_tensor(wg[i][1][:], raw[i], wg[i][0][:].bitcast(F32), ALU.subtract).then_inc(w_lo, 1)
                if i == 1:
                    deviation(nc, own, g, nth, 1e-6)
            deviation(nc, own, g, nth + 1, 1e-6)

        @block.vector
        def _(dve):
            own = Own(dve, vec)
            for k in range(KB):
                ins = nc.vector.tensor_scalar(vo_diag[:, k], g.ident[:], g.vo[:, k:k + 1], None, ALU.mult)
            ins.then_inc(vo_ready, 1)

            def agg_low(first, f):
                dve.wait_ge(agg_hi, (first if first < FF else first - KB) + f + 1)
                u = first + f
                nc.vector.tensor_tensor(halves(aggT[1][:, f]), fm[u % 2][:, :, 0:CH], halves(aggT[0][:, f].bitcast(F32)),
                                        ALU.subtract).then_inc(fm_free[u % 2], 1)

            def hidden_rows(layer):
                def low(t):
                    v = T * layer + t
                    dve.wait_ge(row_hi, v + 1)
                    nc.vector.scalar_tensor_tensor(hid[1][:, t], row[:, v % 2], 0.0, hid[0][:, t].bitcast(F32),
                                                   ALU.max, ALU.subtract).then_inc(row_lo, 1)

                for t in range(T):
                    v = T * layer + t
                    dve.wait_ge(row_mm, v + 1)
                    if v >= 2:
                        dve.wait_ge(row_lo, v - 1)
                    nc.vector.tensor_tensor(row[:, v % 2], rt[v % 3][0:R, 0:DH], bg[:, layer], ALU.add).then_inc(row_added, 1)
                    if t:
                        low(t - 1)
                low(T - 1)

            def everywhere(i):
                return vecs[:, i].unsqueeze(1).to_broadcast([R, T, D])

            def affine(n, scale, shift, out, done):
                dve.wait_ge(norm_done, T * (n + 1))
                own.add(nc.vector.tensor_tensor(nrm[:], nrm[:], everywhere(scale), ALU.mult))
                own.settle()
                nc.vector.tensor_tensor(out[:], nrm[:], everywhere(shift), ALU.add).then_inc(done, 1)

            agg_low(AGG0, 0)
            agg_low(AGG0, 1)
            dve.wait_ge(bias_in, BIAS_IN)
            hidden_rows(0)
            dve.wait_ge(vo_mm, 1)
            own.add(nc.vector.tensor_tensor(g.att[:], g.att[:], aux[0:R, 0:D].unsqueeze(1).to_broadcast([R, T, D]), ALU.add))
            agg_low(AGG1, 0)
            own.settle()
            moments(nc, own, g, g.att)
            agg_low(AGG1, 1)
            standardize(nc, own, g, nth, g.att, nrm, norm_done)
            agg_low(AGG1, 2)
            dve.wait_ge(ff_in, FF_IN)
            affine(0, 0, 1, g.att, att_ready)
            agg_low(AGG1, 3)
            own.add(nc.vector.tensor_tensor(g.x1[:], g.x1[:], everywhere(5), ALU.add))
            hidden_rows(1)
            dve.wait_ge(at_ready, 3)
            own.add(nc.vector.tensor_tensor(g.att[:], g.att[:], everywhere(2), ALU.add))
            own.settle()
            for f in range(HB):
                agg_low(AGG2, f)
            for b in range(3):
                n = min(2, T - 2 * b)
                dve.wait_ge(ff_mm, b + 1)
                to = g.att[:, 2 * b:2 * b + n]
                nc.vector.tensor_tensor(to, to, aux[0:R, 0:n * D].rearrange("p (t d) -> p t d", t=n), ALU.add).then_inc(att_ready, 1)

            def h3_low(f):
                u = H3 + f
                dve.wait_ge(fm_free[u % 2], u // 2 + 1)
                nc.vector.tensor_tensor(h3T[1][:, f], h3_whole[:, f % 2], h3T[0][:, f].bitcast(F32), ALU.subtract).then_inc(row_lo, 1)

            dve.wait_ge(att_ready, 4)
            moments(nc, own, g, g.att)
            h3_low(0)
            standardize(nc, own, g, nth + 1, g.att, nrm, norm_done)
            h3_low(1)
            affine(1, 3, 4, nrm, att_ready)
            h3_low(2)
            dve.wait_ge(att_ready, 5)
            own.add(nc.vector.tensor_tensor(g.x1[:], g.x1[:], nrm[:], ALU.add))
            h3_low(3)
            own.settle()
            for t in range(T):
                v = 2 * T + t
                dve.wait_ge(row_mm, v + 1)
                nc.vector.tensor_tensor(g.x1[:, t], g.x1[:, t], rt[v % 3][0:R, 0:D], ALU.add).then_inc(row_added, 1)

        @block.scalar
        def _(act):
            def weights_high(i):
                act.wait_ge(w_in[i], 16)
                nc.scalar.copy(wg[i][0][:], raw[i]).then_inc(w_hi, 1)

            def agg_high(first, f):
                u = first + f
                act.wait_ge(fm_done, u + 1)
                nc.scalar.copy(halves(aggT[0][:, f]), fm[u % 2][:, :, 0:CH]).then_inc(agg_hi, 1)

            def hidden_high(layer):
                for t in range(T):
                    v = T * layer + t
                    act.wait_ge(row_added, v + 1)
                    nc.scalar.activation(hid[0][:, t], row[:, v % 2], ACT.Relu).then_inc(row_hi, 1)

            agg_high(AGG0, 0)
            weights_high(0)
            agg_high(AGG0, 1)
            weights_high(1)
            hidden_high(0)
            for f in range(HB):
                agg_high(AGG1, f)
            for n in range(3):
                act.wait_ge(at_mm, n + 1)
                if n < 2:
                    nc.scalar.copy(attT[:, n, 0:4 * R], aux[:, 0:4 * R]).then_inc(at_ready, 1)
                else:
                    nc.scalar.copy(attT[:, :, 4 * R:N], aux[:, 0:KB * R].rearrange("p (k j) -> p k j", k=KB)).then_inc(at_ready, 1)
            weights_high(2)
            hidden_high(1)
            act.wait_ge(ff_in, FF_IN)
            for f in range(KB):
                u = FF + f
                act.wait_ge(fm_done, u + 1)
                nc.scalar.activation(halves(ffT[:, f]), fm[u % 2][:, :, 0:CH], ACT.Relu, bias=b_ff[:, f:f + 1]).then_inc(fm_free[u % 2], 1)
            for f in range(HB):
                agg_high(AGG2, f)
            weights_high(3)
            act.wait_ge(bias_in, BIAS_IN)
            for f in range(HB):
                u = H3 + f
                act.wait_ge(fm_done, u + 1)
                if f >= 2:
                    act.wait_ge(row_lo, 2 * T + f - 1)
                for to, done in ((h3_whole[:, f % 2], h3_whole_ready), (h3T[0][:, f], fm_free[u % 2])):
                    nc.scalar.activation(halves(to), fm[u % 2][:, :, 0:CH], ACT.Relu, bias=bg3[:, f:f + 1]).then_inc(done, 1)

        @block.tensor
        def _(pe):
            def next_fm(u):
                if u >= 2:
                    pe.wait_ge(fm_free[u % 2], u // 2)
                return both_halves(fm[u % 2])

            def spread_edges(first, n, src, src_low=()):
                for f in range(n):
                    outs = next_fm(first + f)
                    product(pe, nc, outs, T, lambda i, t: src[i][:, t, f * P:(f + 1) * P], lambda j, t: g.adj[j][:, t],
                            left_low=src_low).then_inc(fm_done, 1)

            def to_rows(layer, blocks, src, w, cols):
                for t in range(T):
                    v = T * layer + t
                    if v >= 3:
                        pe.wait_ge(row_added, v - 2)
                    product(pe, nc, [(rt[v % 3][0:R, 0:cols], slice(0, cols))], blocks,
                            lambda i, k: src[i][:, k, t * R:(t + 1) * R], lambda j, k: w[j][:, k]).then_inc(row_mm, 1)

            def agg_in_parts(end):
                pe.wait_ge(fm_free[(end - 1) % 2], (end + 1) // 2)
                pe.wait_ge(fm_free[end % 2], end // 2)

            spread_edges(AGG0, KB, g.xn_parts)
            pe.wait_ge(vo_ready, 1)
            nc.tensor.matmul(aux[0:R, 0:D], g.ones[:, 0:R], vo_diag[:].rearrange("p k d -> p (k d)"), start=True, stop=True).then_inc(vo_mm, 1)
            agg_in_parts(AGG1)
            pe.wait_ge(w_lo, 1)
            to_rows(0, KB, aggT, wg[0], DH)
            pe.wait_ge(row_hi, T)
            spread_edges(AGG1, HB, hid, (row_lo, T))
            pe.wait_ge(att_ready, 1)
            for n in range(3):
                if n:
                    pe.wait_ge(at_ready, n)
                for j in range(4 if n < 2 else KB):
                    t, k = (j, n) if n < 2 else (4, j)
                    mm = nc.tensor.transpose(aux[:, j * R:(j + 1) * R], g.att[:, t, k * P:(k + 1) * P], g.ident[0:R, 0:R])
                mm.then_inc(at_mm, 1)
            agg_in_parts(FF)
            pe.wait_ge(w_lo, 2)
            to_rows(1, HB, aggT, wg[1], DH)
            pe.wait_ge(zeros, 1)
            pe.wait_ge(at_ready, 3)
            for f in range(KB):
                outs = next_fm(FF + f)
                for k in range(KB):
                    for to, at in outs:
                        mm = nc.tensor.matmul(to, w_ff[0][:, k, f * P:(f + 1) * P], attT[:, k, at], start=k == 0, stop=k == KB - 1)
                mm.then_inc(fm_done, 1)
            pe.wait_ge(row_hi, 2 * T)
            spread_edges(AGG2, HB, hid, (row_lo, 2 * T))
            for b in range(3):
                if b:
                    pe.wait_ge(att_ready, b + 1)
                for t in range(2 * b, min(2 * b + 2, T)):
                    for k in range(KB):
                        mm = nc.tensor.matmul(aux[0:R, t % 2 * D:(t % 2 + 1) * D], ffT[:, k, t * R:(t + 1) * R], w_ff[1][:, k], start=k == 0, stop=k == KB - 1)
                mm.then_inc(ff_mm, 1)
            agg_in_parts(H3)
            pe.wait_ge(w_lo, 3)
            for f in range(HB):
                outs = next_fm(H3 + f)
                product(pe, nc, outs, HB, lambda i, k: wg[2][i][:, k, f * P:(f + 1) * P], lambda j, k: aggT[j][:, k]).then_inc(fm_done, 1)
            pe.wait_ge(row_lo, 2 * T + HB)
            pe.wait_ge(w_lo, 4)
            to_rows(2, HB, h3T, wg[3], D)


def store(nc, g, out):
    with ExitStack() as ctx:
        a = Scope(nc, ctx, "store")
        stored = a.sem("stored")
        block = ctx.enter_context(nc.Block())

        @block.sync
        def _(sp):
            sp.dma_start(rows(out), g.x1[:]).then_inc(stored, 16)
            sp.wait_ge(stored, 16)


def gps_two_layers(nc, inp, out):
    with ExitStack() as ctx:
        g = Shared(Scope(nc, ctx, "g"))
        with nc.cleanup_on_exit():
            with ExitStack() as early:
                share_attention(g, Scope(nc, early, "early"))
                count_edges_and_mix(nc, inp, g)
                attend(nc, inp, g)
            run_experts(nc, inp, g, 0, 1)
        with ExitStack() as layer1:
            share_layer1(g, Scope(nc, layer1, "layer1"))
            run_heads(nc, inp, g, 2)
            convolve(nc, inp, g, 3)
        run_experts(nc, inp, g, 1, 5)
        store(nc, g, out)


def kernel(**inputs):
    import concourse.bacc as bacc
    from concourse.bass_utils import run_bass_kernel_spmd

    nc = bacc.Bacc("TRN2", target_bir_lowering=False, num_devices=1)
    arrays, inp = {}, {}
    for name, value in inputs.items():
        value = np.ascontiguousarray(value)
        arrays[f"in_{name}"] = value
        inp[name] = nc.dram_tensor(f"in_{name}", value.shape, mybir.dt.from_np(value.dtype), kind="ExternalInput").ap()
    out = nc.dram_tensor("out", inputs["x"].shape, F32, kind="ExternalOutput").ap()
    gps_two_layers(nc, inp, out)
    return run_bass_kernel_spmd(nc, [arrays], core_ids=[0]).results[0]["out"]
```

```python
from contextlib import ExitStack

import numpy as np

import concourse.bass as bass
from concourse import mybir

F32 = mybir.dt.float32
F16 = mybir.dt.float16
F32R = mybir.dt.float32r
BF16 = mybir.dt.bfloat16
I32 = mybir.dt.int32
ALU = mybir.AluOpType
ACT = mybir.ActivationFunctionType
AX = mybir.AxisListType

N = 625
R = 125
T = N // R
D = 256
P = 128
KB = D // P
NF = 628
CH = NF // 2
NE = 20000
EP = 125
CHUNKS = NE // EP
BANK = 512

LO = 313
HI = N - LO
FIELD = 12
GROUP = 32
GROUPS = CHUNKS // GROUP
UNROLL = 10
SCALAR_HOT = (1, 3, 6, 8)
BODIES, PER_BODY = (GROUP - 2) // UNROLL, len(SCALAR_HOT)
assert GROUP * EP < 2 ** FIELD and (GROUP - 2) % UNROLL == 0 and GROUPS * GROUP == CHUNKS

PASSES = ((0, 0), (1, 0), (0, 1))

GH, GO = 4, 64
LEAK = 0.2
NONE = -1e30
BATCH_NORM = ("b", "g", "be", "m", "v")
E0 = 8
EXPERT_WEIGHTS = (("W1", "W2", "Wo"), ("expert_w1", "expert_w2", "expert_w3"))
WQ, WK, WV, WO = range(4)
MH, MO = 8, 32


class Own:

    def __init__(self, eng, sem):
        self.eng, self.sem, self.count = eng, sem, 0

    def add(self, instruction):
        self.count += 1
        instruction.then_inc(self.sem, 1)

    def settle(self):
        self.eng.wait_ge(self.sem, self.count)


class Scope:

    def __init__(self, nc, ctx, part):
        self.nc, self.ctx, self.part = nc, ctx, part

    def sb(self, name, shape, dt=F32):
        return self.ctx.enter_context(self.nc.sbuf_tensor(f"{self.part}_{name}", shape, dt))

    def parts(self, name, shape):
        return self.sb(name + "_hi", shape, F32R), self.sb(name + "_lo", shape, F32R)

    def ps(self, name, shape):
        return self.ctx.enter_context(self.nc.psum_tensor(f"{self.part}_{name}", shape, F32))

    def sem(self, name):
        return self.nc.alloc_semaphore(f"{self.part}_{name}")


def rows(ap):
    return ap.rearrange("(t p) d -> p t d", p=R)


def spread(ap, n):
    return ap.rearrange("(a d) -> a d", a=1).to_broadcast([n, ap.shape[0]])


def halves(ap):
    return ap.rearrange("p (c n) -> p c n", c=2)


def rest(engine, parts, whole, at=()):
    hi, lo = parts
    at = at or slice(None)
    return engine.tensor_tensor(lo[at], whole[at], hi[at].bitcast(F32), ALU.subtract)


def product(pe, nc, outs, blocks, left, right, left_low=(), right_low=(), more=False):
    for n, (i, j) in enumerate(PASSES):
        if n == 1 and left_low:
            pe.wait_ge(*left_low)
        if n == 2 and right_low:
            pe.wait_ge(*right_low)
        for k in range(blocks):
            for to, at in outs:
                mm = nc.tensor.matmul(to, left(i, k), right(j, k)[:, at], start=n == 0 and k == 0,
                                      stop=n == 2 and k == blocks - 1 and not more)
    return mm


def both_halves(bank_pair):
    return [(bank_pair[:, c, 0:CH], slice(c * CH, (c + 1) * CH)) for c in range(2)]


def tile_moments(nc, own, w, src, t):
    own.add(nc.vector.bn_stats(w.stats[:, t, :], src[:, t, :]))


def all_moments(nc, own, w):
    own.settle()
    for t in range(T):
        ins = nc.vector.bn_aggr(w.mv[:, t, :], w.stats[:, t, :])
    ins.then_inc(w.var_ready, 1)


def moments(nc, own, w, src):
    for t in range(T):
        tile_moments(nc, own, w, src, t)
    all_moments(nc, own, w)


def standardize(nc, own, w, nth, src, dst, done):
    own.eng.wait_ge(w.rstd_ready, nth + 1)
    for t in range(T):
        nc.vector.tensor_scalar(dst[:, t, :], src[:, t, :], w.mv[:, t, 0:1], w.rstd[:, t:t + 1],
                                ALU.subtract, ALU.mult).then_inc(done, 1)


def normalize(nc, own, w, nth, src, dst, done):
    moments(nc, own, w, src)
    standardize(nc, own, w, nth, src, dst, done)


def deviation(nc, own, w, nth, eps):
    own.eng.wait_ge(w.var_ready, nth + 1)
    own.add(nc.gpsimd.tensor_single_scalar(w.rstd[:], w.mv[:, :, 1], eps, ALU.add))
    own.settle()
    nc.gpsimd.tensor_tensor(w.rstd[:], w.rstd[:], w.minus_half[:], ALU.pow).then_inc(w.rstd_ready, 1)


def count_edges_and_mix(nc, inp, g):
    with ExitStack() as ctx:
        a = Scope(nc, ctx, "count")
        dst_i, src_i = a.sb("dst_i", [EP, CHUNKS], I32), a.sb("src_i", [EP, CHUNKS], I32)
        dst_f, src_f = a.sb("dst_f", [EP, CHUNKS]), a.sb("src_f", [EP, CHUNKS])
        in_high, field, column = (a.sb(n, [EP, CHUNKS]) for n in ("in_high", "field", "column"))
        neg_field, neg_column = a.sb("neg_field", [EP, CHUNKS]), a.sb("neg_column", [EP, CHUNKS])
        node_no = a.sb("node_no", [EP, N + 1], F16)
        away = a.sb("away", [EP, len(SCALAR_HOT), LO + 1], F16)
        hot_dst = a.sb("hot_dst", [EP, GROUP, N + 1], BF16)
        hot_src = a.sb("hot_src", [EP, GROUP, LO + 1], BF16)
        packed = a.sb("packed", [R, 2, T, LO], I32)
        total = a.sb("total", [R, T, N], I32)
        total_lo, total_hi = total[:, :, 0:LO], total[:, :, LO:N]
        low, high = a.sb("low", [R, T, LO], I32), a.sb("high", [R, T, LO], I32)
        w_gat = a.sb("w_gat", [P, KB, GH, GO])
        av_src, av_dst = a.sb("av_src", [R, GH, GO]), a.sb("av_dst", [R, GH, GO])
        ln_w = [a.sb(f"mix_ln{i}", [R, D]) for i in range(4)]
        prod = a.sb("prod", [R, T, GH, GO])
        mean = a.sb("mean", [R, T, MH])
        dev, sq = a.sb("dev", [R, T, MH, MO]), a.sb("sq", [R, T, MH, MO])
        var, half = a.sb("var", [R, T, MH]), a.sb("half", [R, T, MH])
        key, val = a.sb("key", [R, T, D]), a.sb("val", [R, T, D])
        kv = a.sb("kv", [P, KB, P])

        cnt = [a.ps(f"cnt{t}", [P, BANK]) for t in range(T)]
        aux = [a.ps(f"aux{i}", [P, BANK]) for i in range(3)]

        x_in, edges_in, gat_in, mix_in = (a.sem(n) for n in ("x_in", "edges_in", "gat_in", "mix_in"))
        consts, zeros = a.sem("consts"), a.sem("zeros")
        earlier_counts = a.sem("earlier_counts")
        hot, src_hot, away_ready, split_edges, hot_used, counted, unloaded, decoded, summed = (
            a.sem(n) for n in ("hot", "src_hot", "away_ready", "split_edges", "hot_used", "counted", "unloaded", "decoded", "summed"))
        vec = a.sem("vec")
        xn_ready, xt_mm, xt_ready, h_mm, h_ready = (a.sem(n) for n in ("xn_ready", "xt_mm", "xt_ready", "h_mm", "h_ready"))
        dev_ready, sq_ready, kv_in, kv_ready, kv_mm, kv_block, out_mm, base = (
            a.sem(n) for n in ("dev_ready", "sq_ready", "kv_in", "kv_ready", "kv_mm", "kv_block", "out_mm", "base"))
        dn_ready, pool = a.sem("dn_ready"), a.sem("pool")
        block = ctx.enter_context(nc.Block())

        @block.sync
        def _(sp):
            sp.dma_start(dst_i[:], inp["dst"].rearrange("(p c) -> p c", p=EP)).then_inc(edges_in, 16)
            sp.dma_start(src_i[:], inp["src"].rearrange("(p c) -> p c", p=EP)).then_inc(edges_in, 16)
            sp.dma_start(g.x[:], rows(inp["x"])).then_inc(x_in, 16)
            for k in range(KB):
                sp.dma_start(w_gat[:, k], inp["L0_gnn_W"][:, k * P:(k + 1) * P, :].rearrange("h p o -> p h o")).then_inc(gat_in, 16)
            sp.dma_start(av_src[:].rearrange("p h o -> p (h o)"), spread(inp["L0_gnn_a_src"].rearrange("h o -> (h o)"), R)).then_inc(gat_in, 16)
            sp.dma_start(av_dst[:].rearrange("p h o -> p (h o)"), spread(inp["L0_gnn_a_dst"].rearrange("h o -> (h o)"), R)).then_inc(gat_in, 16)
            for i, n in enumerate(("kln_weight", "kln_bias", "vln_weight", "vln_bias")):
                sp.dma_start(ln_w[i][:], spread(inp["L0_mix_" + n].rearrange("h a o -> (h a o)"), R)).then_inc(mix_in, 16)

        @block.gpsimd
        def _(pool_eng):
            own = Own(pool_eng, pool)
            nc.gpsimd.iota(node_no[:], [[1, N + 1]], base=0, channel_multiplier=0,
                           allow_small_or_imprecise_dtypes=True).then_inc(consts, 1)
            nc.gpsimd.memset(g.ones[:], 1.0).then_inc(consts, 1)
            pool_eng.wait_ge(consts, 2)
            nc.gpsimd.affine_select(out=g.ident[:], in_=g.ones[:], compare_op=ALU.is_equal, fill=0.0, base=0,
                                    pattern=[[-1, P]], channel_multiplier=1).then_inc(consts, 1)
            nc.gpsimd.memset(kv[:], 0.0).then_inc(zeros, 1)
            nc.gpsimd.memset(g.xT[:, :, N:NF], 0.0).then_inc(zeros, 1)
            nc.gpsimd.memset(g.edges[:, :, N:NF], 0.0).then_inc(zeros, 1)
            nc.gpsimd.memset(g.edgesT[:, :, N:NF], 0.0).then_inc(zeros, 1)
            nc.gpsimd.memset(g.h[:, :, :, GO:GO + 1], 1.0).then_inc(zeros, 1)

            def add_counts(n):
                pool_eng.wait_ge(decoded, n + 1)
                if n >= 2:
                    pool_eng.wait_ge(summed, n - 1)
                nc.gpsimd.tensor_tensor(total_lo, total_lo, low[:], ALU.add)
                nc.gpsimd.tensor_tensor(total_hi, total_hi, high[:, :, 0:HI], ALU.add).then_inc(summed, 1)

            own.add(nc.gpsimd.memset(g.minus_half[:], -0.5))
            own.add(nc.gpsimd.memset(half[:], 0.5))
            deviation(nc, own, g, 0, 1e-5)
            pool_eng.wait_ge(xn_ready, T)
            nc.gpsimd.tensor_tensor(g.x1[:], g.x[:], g.xn[:], ALU.add).then_inc(base, 1)
            pool_eng.wait_ge(sq_ready, 1)
            own.add(nc.gpsimd.tensor_single_scalar(var[:], var[:], 1.0 / (MO - 1), ALU.mult))
            own.settle()
            own.add(nc.gpsimd.tensor_tensor(var[:], var[:], half[:], ALU.pow))
            own.settle()
            nc.gpsimd.tensor_single_scalar(var[:], var[:], 1e-5, ALU.add).then_inc(dev_ready, 1)
            pool_eng.wait_ge(dn_ready, 1)
            pool_eng.wait_ge(mix_in, 64)
            flat = dev[:].rearrange("p t h o -> p t (h o)")
            for wt, bias, to in ((ln_w[0], ln_w[1], key), (ln_w[2], ln_w[3], val)):
                own.add(nc.gpsimd.tensor_tensor(to[:], flat, wt[:].unsqueeze(1).to_broadcast([R, T, D]), ALU.mult))
            own.settle()
            for wt, bias, to in ((ln_w[0], ln_w[1], key), (ln_w[2], ln_w[3], val)):
                nc.gpsimd.tensor_tensor(to[:], to[:], bias[:].unsqueeze(1).to_broadcast([R, T, D]), ALU.add).then_inc(kv_in, 1)
            for n in range(1, GROUPS - 1):
                add_counts(n)

        @block.vector
        def _(dve):
            own = Own(dve, vec)
            dve.wait_ge(edges_in, 32)
            own.add(nc.vector.tensor_copy(dst_f[:], dst_i[:]))
            own.add(nc.vector.tensor_copy(src_f[:], src_i[:]))
            own.settle()
            own.add(nc.vector.tensor_scalar(in_high[:], src_f[:], float(LO), None, ALU.is_ge))
            own.settle()
            own.add(nc.vector.tensor_scalar(field[:], in_high[:], float(2 ** FIELD - 1), 1.0, ALU.mult, ALU.add))
            nc.vector.scalar_tensor_tensor(column[:], in_high[:], -float(LO), src_f[:], ALU.mult, ALU.add).then_inc(split_edges, 1)
            dve.wait_ge(split_edges, 1)
            own.settle()
            dve.wait_ge(consts, 1)

            def one_hots(group, i, last=False, src=True):
                if group and last:
                    dve.wait_ge(counted, T * group)
                elif group:
                    dve.wait_ge(hot_used, i + ((GROUP - 1) * (group - 1) + 1))
                c = i + GROUP * group
                ins = nc.vector.tensor_scalar(hot_dst[:, bass.ds(i, 1), :].rearrange("p a n -> p (a n)"), node_no[:],
                                              dst_f[:, bass.ds(c, 1)], None, ALU.is_equal)
                if src:
                    ins = nc.vector.tensor_scalar(hot_src[:, bass.ds(i, 1), :].rearrange("p a n -> p (a n)"), node_no[:, 0:LO + 1],
                                                  column[:, bass.ds(c, 1)], field[:, bass.ds(c, 1)], ALU.is_equal, ALU.mult)
                ins.then_inc(hot, 1)

            def one_hot_group(group):
                one_hots(group, 0)
                with dve.Fori(0, (GROUP - 2) // UNROLL) as i:
                    for j in range(UNROLL):
                        one_hots(group, i * UNROLL + (j + 1), src=j not in SCALAR_HOT)
                one_hots(group, GROUP - 1, last=True)

            def decode(group):
                dve.wait_ge(unloaded, T * (group + 1))
                if group >= 2:
                    dve.wait_ge(summed, group - 1)
                to_low, to_high = (low[:], high[:, :, 0:HI]) if group else (total_lo, total_hi)
                nc.vector.tensor_single_scalar(to_low, packed[:, group % 2], 2 ** FIELD - 1, ALU.bitwise_and)
                nc.vector.tensor_single_scalar(to_high, packed[:, group % 2, :, 0:HI], FIELD, ALU.logical_shift_right).then_inc(decoded, 1)

            one_hot_group(0)
            dve.wait_ge(x_in, 16)
            normalize(nc, own, g, 0, g.x, g.xn, xn_ready)
            one_hot_group(1)
            decode(0)
            dve.wait_ge(xn_ready, T)
            heads = g.xn[:].rearrange("p t (h o) -> p t h o", o=MO)
            own.add(nc.vector.tensor_reduce(mean[:], heads, AX.X, ALU.add))
            own.settle()
            own.add(nc.vector.tensor_single_scalar(mean[:], mean[:], 1.0 / MO, ALU.mult))
            own.settle()
            own.add(nc.vector.tensor_tensor(dev[:], heads, mean[:].unsqueeze(3).to_broadcast([R, T, MH, MO]), ALU.subtract))
            own.settle()
            own.add(nc.vector.tensor_tensor(sq[:], dev[:], dev[:], ALU.mult))
            own.settle()
            nc.vector.tensor_reduce(var[:], sq[:], AX.X, ALU.add).then_inc(sq_ready, 1)
            dve.wait_ge(dev_ready, 1)
            own.add(nc.vector.reciprocal(var[:], var[:]))
            own.settle()
            nc.vector.tensor_tensor(dev[:], dev[:], var[:].unsqueeze(3).to_broadcast([R, T, MH, MO]), ALU.mult).then_inc(dn_ready, 1)
            one_hot_group(2)
            decode(1)
            dve.wait_ge(h_ready, 3)
            dve.wait_ge(gat_in, 64)
            for av, to in ((av_src, g.score_src), (av_dst, g.score_dst)):
                own.add(nc.vector.tensor_tensor(prod[:], g.h[:, :, :, 0:GO], av[:].unsqueeze(1).to_broadcast([R, T, GH, GO]), ALU.mult))
                own.settle()
                own.add(nc.vector.tensor_reduce(to[:], prod[:], AX.X, ALU.add))
                own.settle()
            one_hot_group(3)
            decode(2)
            one_hot_group(4)
            decode(3)
            dve.wait_ge(base, 1)
            for t in range(T):
                dve.wait_ge(out_mm, min(t // 2 * 2 + 2, T))
                nc.vector.tensor_tensor(g.x1[:, t], g.x1[:, t], aux[t // 2][0:R, (t % 2) * D:(t % 2 + 1) * D], ALU.add)
            decode(4)
            dve.wait_ge(decoded, GROUPS)
            dve.wait_ge(earlier_counts, 1)
            nc.vector.tensor_tensor(g.edges[:, :, 0:LO], g.edges[:, :, 0:LO], low[:], ALU.add)
            nc.vector.tensor_tensor(g.edges[:, :, LO:N], g.edges[:, :, LO:N], high[:, :, 0:HI], ALU.add)

        @block.scalar
        def _(act):
            def source_hots(group):
                with act.Fori(0, BODIES) as body:
                    before = body * PER_BODY + group * BODIES * PER_BODY
                    act.wait_ge(src_hot, before + 1)
                    for n, j in enumerate(SCALAR_HOT):
                        c = body * UNROLL + (j + 1 + GROUP * group)
                        nc.scalar.activation(away[:, n], node_no[:, 0:LO + 1], ACT.Abs, bias=neg_column[:, bass.ds(c, 1)]).then_inc(away_ready, 1)
                    for n, j in enumerate(SCALAR_HOT):
                        i = body * UNROLL + (j + 1)
                        c = i + GROUP * group
                        if group:
                            act.wait_ge(hot_used, i + ((GROUP - 1) * (group - 1) + 1))
                        act.wait_ge(away_ready, before + (n + 1))
                        nc.scalar.activation(hot_src[:, bass.ds(i, 1), :].rearrange("p a n -> p (a n)"), away[:, n], ACT.Relu,
                                             bias=field[:, bass.ds(c, 1)], scale=neg_field[:, bass.ds(c, 1)]).then_inc(src_hot, 1)

            def unload(group):
                for t in range(T):
                    act.wait_ge(counted, T * group + t + 1)
                    if group >= 2:
                        act.wait_ge(decoded, group - 1)
                    nc.scalar.copy(packed[:, group % 2, t], cnt[t][0:R, 0:LO]).then_inc(unloaded, 1)

            act.wait_ge(consts, 1)
            act.wait_ge(split_edges, 1)
            nc.scalar.mul(neg_column[:], column[:], -1.0)
            nc.scalar.mul(neg_field[:], field[:], -1.0).then_inc(src_hot, 1)
            source_hots(0)
            source_hots(1)
            unload(0)
            source_hots(2)
            unload(1)
            act.wait_ge(xt_mm, 1)
            nc.scalar.copy(g.xT[:, 0, 0:4 * R], aux[0][:, 0:4 * R])
            nc.scalar.copy(g.xT[:, 1, 0:4 * R], aux[2][:, 0:4 * R])
            nc.scalar.copy(g.xT[:, :, 4 * R:N], aux[1][:, 0:2 * R].rearrange("p (k n) -> p k n", k=KB)).then_inc(xt_ready, 1)
            act.wait_ge(zeros, 5)
            for i in range(3):
                n = min(2, T - 2 * i)
                act.wait_ge(h_mm, min(2 * i + 2, T))
                nc.scalar.copy(g.h[:, 2 * i:2 * i + n, :, 0:GO],
                               aux[i][0:R, 0:n * D].rearrange("p (t h o) -> p t h o", t=n, h=GH)).then_inc(h_ready, 1)
            source_hots(3)
            unload(2)
            source_hots(4)
            unload(3)
            act.wait_ge(kv_mm, 2)
            act.wait_ge(zeros, 1)
            for k in range(KB):
                for b in range(P // MO):
                    q = slice(b * MO, (b + 1) * MO)
                    last = nc.scalar.mul(kv[q, k, q], aux[k][q, q], 1.0 / N)
            last.then_inc(kv_block, 1)
            act.wait_ge(summed, GROUPS - 2)
            nc.scalar.copy(g.edges[:, :, 0:N], total[:]).then_inc(earlier_counts, 1)
            unload(4)

        @block.tensor
        def _(pe):
            def count(group, i, first=False, last=False):
                for t in range(T):
                    if first and group:
                        pe.wait_ge(unloaded, T * (group - 1) + t + 1)
                    mm = nc.tensor.matmul(cnt[t][0:R, 0:LO], hot_dst[:, bass.ds(i, 1), t * R:(t + 1) * R].rearrange("p a n -> p (a n)"),
                                          hot_src[:, bass.ds(i, 1), 0:LO].rearrange("p a n -> p (a n)"), start=first, stop=last)
                    if last:
                        mm.then_inc(counted, 1)
                if not last:
                    mm.then_inc(hot_used, 1)

            def count_group(group):
                pe.wait_ge(hot, GROUP * group + 1)
                count(group, 0, first=True)
                peeled = 0
                if group == 0:
                    peeled = 1
                    for j in range(UNROLL):
                        pe.wait_ge(hot, j + 2)
                        if j in SCALAR_HOT:
                            pe.wait_ge(src_hot, SCALAR_HOT.index(j) + 2)
                        count(group, j + 1)
                with pe.Fori(0, BODIES - peeled) as i:
                    pe.wait_ge(hot, (i + peeled) * UNROLL + (UNROLL + GROUP * group + 1))
                    pe.wait_ge(src_hot, (i + peeled) * PER_BODY + (BODIES * group * PER_BODY + PER_BODY + 1))
                    for j in range(UNROLL):
                        count(group, i * UNROLL + (peeled * UNROLL + j + 1))
                pe.wait_ge(hot, GROUP * (group + 1))
                count(group, GROUP - 1, last=True)

            count_group(0)
            count_group(1)
            pe.wait_ge(xn_ready, T)
            pe.wait_ge(consts, 3)
            for t in range(T):
                for k in range(KB):
                    bank, at = (aux[2 * k], t * R) if t < 4 else (aux[1], k * R)
                    mm = nc.tensor.transpose(bank[:, at:at + R], g.xn[:, t, k * P:(k + 1) * P], g.ident[0:R, 0:R])
            mm.then_inc(xt_mm, 1)
            pe.wait_ge(xt_ready, 1)
            pe.wait_ge(gat_in, 64)
            for t in range(T):
                for k in range(KB):
                    mm = nc.tensor.matmul(aux[t // 2][0:R, (t % 2) * D:(t % 2 + 1) * D], g.xT[:, k, t * R:(t + 1) * R],
                                          w_gat[:, k].rearrange("p h o -> p (h o)"), start=k == 0, stop=k == KB - 1)
                mm.then_inc(h_mm, 1)
            count_group(2)
            count_group(3)
            pe.wait_ge(kv_in, 2)
            pe.wait_ge(h_ready, 3)
            for k in range(KB):
                for t in range(T):
                    mm = nc.tensor.matmul(aux[k][:, 0:P], key[:, t, k * P:(k + 1) * P], val[:, t, k * P:(k + 1) * P],
                                          start=t == 0, stop=t == T - 1)
                mm.then_inc(kv_mm, 1)
            pe.wait_ge(kv_block, 1)
            for t in range(T):
                for k in range(KB):
                    at = (t % 2) * D + k * P
                    mm = nc.tensor.matmul(aux[t // 2][0:R, at:at + P], g.xT[:, k, t * R:(t + 1) * R], kv[:, k], start=True, stop=True)
                mm.then_inc(out_mm, 1)
            count_group(4)


def attend(nc, inp, g):
    with ExitStack() as ctx:
        a = Scope(nc, ctx, "gat")
        mask = a.sb("mask", [R, T, NF])
        diag = a.sb("diag", [R, 3, NF])
        junk = a.sb("junk", [R, 2, NF])
        top = a.sb("top", [R, T, GH])
        above, below, src_leak = a.sb("above", [R, T, GH]), a.sb("below", [R, T, GH]), a.sb("src_leak", [R, T, GH])
        e_pos, e_neg = a.sb("e_pos", [R, 2, T, NF]), a.sb("e_neg", [R, 2, T, NF])
        sumsT = a.sb("sumsT", [GO + 1, NF])
        den = a.sb("den", [R, 2, T])
        agg = a.sb("agg", [R, 2, T, GO])
        par = a.sb("par", [E0, 2, len(BATCH_NORM), D])
        exponent = a.sb("exponent", [P, 2, KB * E0])
        slot = [a.ps(f"slot{i}", [P, 2, BANK]) for i in range(3)]
        out = a.ps("agg_ps", [P, 2, BANK])
        SRC, ABOVE, BELOW = range(3)
        ORDER = ((SRC, 0), (SRC, 1), (ABOVE, 0), (BELOW, 0), (SRC, 2), (ABOVE, 1), (BELOW, 1), (SRC, 3),
                 (ABOVE, 2), (BELOW, 2), (ABOVE, 3), (BELOW, 3))
        assert GH == 4
        SUMS = (out, out, out, slot[SRC])
        TURN = (slot[ABOVE], slot[BELOW], out)
        (turned, copied, degrees, diag_made, row_mm, above_used, below_used, weights, agg_mm, sums_copied, back_mm, agg_used, vec, maxed,
         leaked, level_ready, par_in, par_mm, par_ready, pool) = (a.sem(n) for n in ("turned", "copied", "degrees", "diag_made", "row_mm", "above_used", "below_used", "weights",
                                       "agg_mm", "sums_copied", "back_mm", "agg_used", "vec", "maxed", "leaked", "level_ready", "par_in", "par_mm", "par_ready", "pool"))
        block = ctx.enter_context(nc.Block())

        @block.sync
        def _(sp):
            load_first_weights(sp, inp, g, 0)
            for layer in range(2):
                for i, name in enumerate(BATCH_NORM):
                    sp.dma_start(par[:, layer, i], inp[f"L0_ffn_{name}{layer + 1}"]).then_inc(par_in, 16)

        @block.gpsimd
        def _(pool_eng):
            own = Own(pool_eng, pool)
            nc.gpsimd.tensor_single_scalar(src_leak[:], g.score_src[:], LEAK, ALU.mult).then_inc(leaked, 1)
            for i in range(3):
                nc.gpsimd.memset(diag[:, i, N:NF], 0.0)
            for n, (kind, h) in enumerate(ORDER):
                if kind != SRC:
                    pool_eng.wait_ge(level_ready, h + 1)
                if n >= 3:
                    pool_eng.wait_ge(row_mm, n - 2)
                score = (g.score_src, above, below)[kind]
                nc.gpsimd.tensor_tensor(diag[:, n % 3, 0:N].rearrange("p (t j) -> p t j", t=T),
                                        g.ident[0:R, 0:R].unsqueeze(1).to_broadcast([R, T, R]),
                                        score[:, :, h:h + 1].to_broadcast([R, T, R]), ALU.mult).then_inc(diag_made, 1)
            own.add(nc.gpsimd.memset(exponent[:], -0.5))
            pool_eng.wait_ge(par_ready, 1)
            bias, scale, shift, mean, var = (g.affine[:, :, i] for i in range(len(BATCH_NORM)))
            own.add(nc.gpsimd.tensor_single_scalar(var, var, 1e-3, ALU.add))
            own.add(nc.gpsimd.tensor_tensor(bias, bias, mean, ALU.subtract))
            own.settle()
            own.add(nc.gpsimd.tensor_tensor(var, var, exponent[:], ALU.pow))
            own.settle()
            own.add(nc.gpsimd.tensor_tensor(scale, scale, var, ALU.mult))
            own.settle()
            own.add(nc.gpsimd.tensor_tensor(bias, bias, scale, ALU.mult))
            own.settle()
            nc.gpsimd.tensor_tensor(bias, bias, shift, ALU.add)
            pool_eng.wait_ge(degrees, T)
            nc.gpsimd.tensor_single_scalar(g.deg[:], g.deg[:], 1.0, ALU.add).then_inc(degrees, 1)
            pool_eng.wait_ge(degrees, T + 1)
            nc.gpsimd.tensor_tensor(g.deg[:], g.deg[:], g.minus_half[:], ALU.pow)
            deviation(nc, own, g, 1, 1e-5)

        @block.tensor
        def _(pe):
            def turn_edges():
                for s in range(T):
                    if s >= 3:
                        pe.wait_ge(copied, s - 2)
                    for t in range(T):
                        to = TURN[s % 3][0:R, t // 4, (t % 4) * R:(t % 4 + 1) * R]
                        mm = nc.tensor.transpose(to, g.edges[:, t, s * R:(s + 1) * R], g.ident[0:R, 0:R])
                    mm.then_inc(turned, 1)

            def row(kind, h):
                n = ORDER.index((kind, h))
                pe.wait_ge(diag_made, n + 1)
                if kind == SRC:
                    if h:
                        pe.wait_ge(maxed, T * h)
                elif h == 0:
                    pe.wait_ge(copied, T)
                else:
                    pe.wait_ge(above_used if kind == ABOVE else below_used, T * h)
                for c in range(2):
                    mm = nc.tensor.matmul(slot[kind][0:R, c, 0:CH], g.ones[0:R, 0:R], diag[:, n % 3, c * CH:(c + 1) * CH],
                                          start=True, stop=True)
                mm.then_inc(row_mm, 1)

            def aggregate(h):
                if h == GH - 1:
                    pe.wait_ge(maxed, T * GH)
                elif h:
                    pe.wait_ge(agg_used, h)
                for s in range(T):
                    pe.wait_ge(weights, T * h + s + 1)
                    for c in range(2):
                        mm = nc.tensor.matmul(SUMS[h][0:GO + 1, c, 0:CH], g.h[:, s, h, :], e_pos[:, h % 2, s, c * CH:(c + 1) * CH],
                                              start=s == 0, stop=s == T - 1)
                mm.then_inc(agg_mm, 1)

            def turn_back(h):
                pe.wait_ge(sums_copied, h + 1)
                for t in range(T):
                    mm = nc.tensor.transpose(SUMS[h][0:R, 0, t * (GO + 1):(t + 1) * (GO + 1)], sumsT[:, t * R:(t + 1) * R],
                                             g.ident[0:GO + 1, 0:GO + 1])
                mm.then_inc(back_mm, 1)

            row(*ORDER[0])
            turn_edges()
            for kind, h in ORDER[1:4]:
                row(kind, h)
            pe.wait_ge(par_in, 16 * 2 * len(BATCH_NORM))
            for layer in range(2):
                for i in range(len(BATCH_NORM)):
                    for k in range(KB):
                        at = ((layer * len(BATCH_NORM) + i) * KB + k) * E0
                        mm = nc.tensor.transpose(out[:, 0, at:at + E0], par[:, layer, i, k * P:(k + 1) * P], g.ident[0:E0, 0:E0])
            mm.then_inc(par_mm, 1)
            for kind, h in ORDER[4:7]:
                row(kind, h)
            pe.wait_ge(par_ready, 1)
            aggregate(0)
            for kind, h in ORDER[7:10]:
                row(kind, h)
            turn_back(0)
            aggregate(1)
            for kind, h in ORDER[10:]:
                row(kind, h)
            turn_back(1)
            aggregate(2)
            turn_back(2)
            aggregate(3)
            turn_back(3)

        @block.scalar
        def _(act):
            for s in range(T):
                act.wait_ge(turned, s + 1)
                nc.scalar.copy(g.edgesT[:, s, 0:4 * R], TURN[s % 3][0:R, 0, 0:4 * R])
                nc.scalar.copy(g.edgesT[:, s, 4 * R:N], TURN[s % 3][0:R, 1, 0:R]).then_inc(copied, 1)

            def exponentials(h):
                if h >= 2:
                    act.wait_ge(agg_mm, h - 1)
                for kind, e, score, done in ((ABOVE, e_pos, g.score_src, above_used), (BELOW, e_neg, src_leak, below_used)):
                    act.wait_ge(row_mm, ORDER.index((kind, h)) + 1)
                    for s in range(T):
                        nc.scalar.activation(halves(e[:, h % 2, s]), slot[kind][0:R, :, 0:CH], ACT.Exp,
                                             bias=score[:, s, h:h + 1]).then_inc(done, 1)

            def copy_sums(h):
                act.wait_ge(agg_mm, h + 1)
                if h:
                    act.wait_ge(back_mm, h)
                nc.scalar.copy(halves(sumsT[:]), SUMS[h][0:GO + 1, :, 0:CH]).then_inc(sums_copied, 1)

            act.wait_ge(leaked, 1)
            exponentials(0)
            act.wait_ge(par_mm, 1)
            nc.scalar.copy(g.affine[:].rearrange("p l i e -> p (l i e)"), out[:, 0, 0:2 * len(BATCH_NORM) * KB * E0]).then_inc(par_ready, 1)
            exponentials(1)
            copy_sums(0)
            exponentials(2)
            copy_sums(1)
            exponentials(3)
            act.wait_ge(maxed, T * GH)
            for s in range(T):
                nc.scalar.activation(mask[:, s], g.edgesT[:, s], ACT.Identity, accum_out=g.deg[:, s:s + 1]).then_inc(degrees, 1)
            copy_sums(2)
            copy_sums(3)

        @block.vector
        def _(dve):
            own = Own(dve, vec)
            own.add(nc.vector.tensor_scalar(mask[:], g.edges[:], 0.0, NONE, ALU.is_equal, ALU.mult))
            own.settle()

            def levels(h):
                dve.wait_ge(row_mm, ORDER.index((SRC, h)) + 1)
                for t in range(T):
                    n = T * h + t
                    if n >= 2:
                        dve.wait_ge(maxed, n - 1)
                    nc.vector.tensor_tensor_reduce(halves(junk[:, n % 2]), halves(mask[:, t]), slot[SRC][0:R, :, 0:CH],
                                                   1.0, NONE, ALU.add, ALU.max, top[:, t, h:h + 1]).then_inc(maxed, 1)
                dve.wait_ge(maxed, T * (h + 1))
                best, score = top[:, :, h], g.score_dst[:, :, h]
                own.add(nc.vector.scalar_tensor_tensor(best, best, 0.1 * NONE, best, ALU.is_gt, ALU.mult))
                own.settle()
                own.add(nc.vector.tensor_tensor(best, best, score, ALU.add))
                own.settle()
                own.add(nc.vector.scalar_tensor_tensor(best, best, LEAK, best, ALU.mult, ALU.max))
                own.settle()
                nc.vector.tensor_tensor(above[:, :, h], score, best, ALU.subtract)
                nc.vector.scalar_tensor_tensor(below[:, :, h], score, LEAK, best, ALU.mult, ALU.subtract).then_inc(level_ready, 1)

            def weigh(h):
                dve.wait_ge(copied, T)
                for s in range(T):
                    dve.wait_ge(above_used, T * h + s + 1)
                    dve.wait_ge(below_used, T * h + s + 1)
                    b = h % 2
                    own.add(nc.vector.tensor_tensor(e_pos[:, b, s], e_pos[:, b, s], e_neg[:, b, s], ALU.max))
                    own.settle()
                    nc.vector.scalar_tensor_tensor(e_pos[:, b, s], e_pos[:, b, s], 1.0, g.edgesT[:, s], ALU.min, ALU.mult).then_inc(weights, 1)

            def finish(h):
                dve.wait_ge(back_mm, h + 1)
                b = h % 2
                sums = SUMS[h][0:R, 0, 0:T * (GO + 1)].rearrange("p (t o) -> p t o", t=T)
                own.add(nc.vector.tensor_single_scalar(den[:, b], sums[:, :, GO], 1e-9, ALU.max))
                own.settle()
                own.add(nc.vector.reciprocal(den[:, b], den[:, b]))
                own.settle()
                nc.vector.tensor_tensor(agg[:, b], sums[:, :, 0:GO], den[:, b].unsqueeze(2).to_broadcast([R, T, GO]), ALU.mult).then_inc(agg_used, 1)
                dve.wait_ge(agg_used, h + 1)
                to = g.x1[:, :, h * GO:(h + 1) * GO]
                own.add(nc.vector.scalar_tensor_tensor(to, agg[:, b], 0.0, to, ALU.max, ALU.add))

            levels(0)
            levels(1)
            weigh(0)
            levels(2)
            weigh(1)
            finish(0)
            levels(3)
            weigh(2)
            finish(1)
            weigh(3)
            finish(2)
            finish(3)
            own.settle()
            moments(nc, own, g, g.x1)


class Shared:

    def __init__(self, a):
        self.ident, self.ones = a.sb("ident", [P, P]), a.sb("ones", [P, P])
        self.xn, self.x1 = a.sb("xn", [R, T, D]), a.sb("x1", [R, T, D])
        self.xT = a.sb("xT", [P, KB, NF])
        self.edges = a.sb("edges", [R, T, NF])
        self.deg = a.sb("deg", [R, T])
        self.affine = a.sb("affine", [P, 2, len(BATCH_NORM), KB * E0])
        self.stats, self.mv = a.sb("stats", [R, T, 6]), a.sb("mv", [R, T, 2])
        self.rstd, self.minus_half = a.sb("rstd", [R, T]), a.sb("minus_half", [R, T])
        self.var_ready, self.rstd_ready = a.sem("var_ready"), a.sem("rstd_ready")


def share_attention(g, a):
    g.x = a.sb("x", [R, T, D])
    g.edgesT = a.sb("edgesT", [R, T, NF])
    g.h = a.sb("h", [R, T, GH, GO + 1])
    g.score_src, g.score_dst = a.sb("score_src", [R, T, GH]), a.sb("score_dst", [R, T, GH])


def share_first_weights(g, a):
    g.first_w = [a.sb(f"w{m}", [P, KB, D]) for m in range(3)]
    g.first_w_in = a.sem("w_in")


def load_first_weights(sp, inp, g, layer):
    for m, name in enumerate(EXPERT_WEIGHTS[layer]):
        sp.dma_start(g.first_w[m][:], inp[f"L{layer}_ffn_{name}"][0].rearrange("(k p) h -> p k h", p=P)).then_inc(g.first_w_in, 16)


def share_heads(g, a, H, KD):
    g.head_raw = [a.sb(f"raw{m}", [P, KB, D]) for m in range(4)]
    g.proj = a.sb("proj", [P, KB, KD])
    g.hb = a.sb("hb", [H, 3, KD])
    g.bo = a.sb("bo", [R, D])
    g.proj_in, g.bias_in, g.head_w_in = a.sem("proj_in"), a.sem("bias_in"), [a.sem(f"w_in{m}") for m in range(4)]


def load_head_weights(sp, inp, g, h, m):
    if m == WO:
        src = inp["L1_mix_Wo"][bass.ds(h, 1)].rearrange("a (k p) d -> p (a k) d", p=P)
    else:
        src = inp["L1_mix_" + ("Wq", "Wk", "Wv")[m]][:, bass.ds(h, 1)].rearrange("(k p) a m -> p k (a m)", p=P)
    sp.dma_start(g.head_raw[m][:], src).then_inc(g.head_w_in[m], 16)


def load_heads(sp, inp, g):
    load_head_weights(sp, inp, g, 0, WK)
    load_head_weights(sp, inp, g, 0, WQ)
    sp.dma_start(g.proj[:], inp["L1_mix_proj"].rearrange("(k p) d -> p k d", p=P)).then_inc(g.proj_in, 16)
    for i, n in enumerate(("bq", "bk", "bv")):
        sp.dma_start(g.hb[:, i], inp["L1_mix_" + n]).then_inc(g.bias_in, 16)
    sp.dma_start(g.bo[:], spread(inp["L1_mix_bo"], R)).then_inc(g.bias_in, 16)
    load_head_weights(sp, inp, g, 0, WV)
    load_head_weights(sp, inp, g, 0, WO)


def share_layer1(g, a):
    g.xn_parts = a.parts("xn", [R, T, D])
    g.adj = a.parts("adj", [R, T, NF])
    g.att = a.sb("att", [R, T, D])


def run_experts(nc, inp, g, layer, nth):
    pre = f"L{layer}_ffn_"
    top2 = layer == 1
    W = [inp[pre + n] for n in EXPERT_WEIGHTS[layer]]
    E = W[0].shape[0]
    BEFORE = (E0 // 2 * 48 if top2 else 0, 0)
    PAIRS = E // 2
    BANKS = (T + 1) // 2
    with ExitStack() as ctx:
        a = Scope(nc, ctx, f"ffn{layer}")
        raw = [g.first_w, [a.sb(f"raw1_{m}", [P, KB, D]) for m in range(3)]]
        w = [[a.parts(f"w{s}_{m}", [P, KB, D]) for m in range(3)] for s in range(2)]
        hid = [a.sb(f"hid{m}", [P, KB, NF]) for m in range(2)]
        hid_parts = [a.parts(f"hid{m}", [P, KB, NF]) for m in range(2)]
        xT_parts = a.parts("xT", [P, KB, NF])
        gate_w = a.sb("gate_w", [P, KB, P if top2 else E])
        gate_w2 = a.sb("gate_w2", [P, E])
        gate_b1 = a.sb("gate_b1", [P, 1])
        gate_b = a.sb("gate_b", [R, E])
        logit, prob, gate = (a.sb(n, [R, T, E]) for n in ("logit", "prob", "gate"))
        one1, one2, cand = (a.sb(n, [R, T, E]) for n in ("one1", "one2", "cand"))
        order = a.sb("order", [R, E])
        big, sums, best, second = (a.sb(n, [R, T]) for n in ("big", "sums", "best", "second"))
        gateT = a.sb("gateT", [E, N])
        b3 = a.sb("b3", [E, D])
        par = a.sb("par", [E, 2, D])
        par_col = a.sb("par_col", [P, 2, KB * E])
        rh = a.sb("rh", [P, NF])

        fm = [a.ps(f"fm{i}", [P, 2, BANK]) for i in range(2)]
        rt = [a.ps(f"rt{i}", [P, BANK]) for i in range(BANKS)]
        aux = a.ps("aux", [P, BANK])

        par_in, gate_in, w_in = a.sem("par_in"), a.sem("gate_in"), [g.first_w_in, a.sem("w_in1")]
        xn_ready, xt_mm, xt_ready, xt_hi = (a.sem(n) for n in ("xn_ready", "xt_mm", "xt_ready", "xt_hi"))
        order_ready, par_mm, par_ready, rh_mm, rh_ready = (
            a.sem(n) for n in ("order_ready", "par_mm", "par_ready", "rh_mm", "rh_ready"))
        logit_mm, shifted, exped, gt_mm, gt_ready = (
            a.sem(n) for n in ("logit_mm", "shifted", "exped", "gt_mm", "gt_ready"))
        fm_done, fm_free, rt_done, rt_free = (a.sem(n) for n in ("fm_done", "fm_free", "rt_done", "rt_free"))
        w_hi, w_lo, hid_hi, hid_lo, xt_lo, pads = (a.sem(n) for n in ("w_hi", "w_lo", "hid_hi", "hid_lo", "xt_lo", "pads"))
        vec, pool = a.sem("vec"), a.sem("pool")
        block = ctx.enter_context(nc.Block())

        @block.sync
        def _(sp):
            if top2:
                for m in range(2):
                    sp.dma_start(par[:, m], inp[pre + f"expert_b{m + 1}"]).then_inc(par_in, 16)
                sp.dma_start(gate_w[:], inp[pre + "router_w1"].rearrange("(k p) h -> p k h", p=P)).then_inc(gate_in, 16)
                sp.dma_start(gate_w2[:], inp[pre + "router_w2"]).then_inc(gate_in, 16)
                sp.dma_start(gate_b1[:], inp[pre + "router_b1"].rearrange("(p a) -> p a", a=1)).then_inc(gate_in, 16)
                sp.dma_start(gate_b[:], spread(inp[pre + "router_b2"], R)).then_inc(gate_in, 16)
                sp.dma_start(b3[:], inp[pre + "expert_b3"]).then_inc(gate_in, 16)
            else:
                sp.dma_start(gate_w[:], inp[pre + "Wr"].rearrange("(k p) e -> p k e", p=P)).then_inc(gate_in, 16)
                sp.dma_start(gate_b[:], spread(inp[pre + "br"], R)).then_inc(gate_in, 16)
                sp.dma_start(b3[:], inp[pre + "bo"]).then_inc(gate_in, 16)
            for m in range(3):
                sp.dma_start(raw[1][m][:], W[m][1].rearrange("(k p) h -> p k h", p=P)).then_inc(w_in[1], 16)
            if not top2:
                load_heads(sp, inp, g)
            with sp.Fori(0, PAIRS - 1) as i:
                for s in range(2):
                    for m in range(3):
                        sp.wait_ge(w_lo, i * 6 + (3 * s + m + 1))
                        sp.dma_start(raw[s][m][:], W[m][bass.ds(i * 2 + (2 + s), 1)].rearrange("e (k p) h -> p (e k) h", p=P)).then_inc(w_in[s], 16)

        GATE_IN = 80 if top2 else 48

        @block.gpsimd
        def _(pool_eng):
            own = Own(pool_eng, pool)
            for part in range(2):
                nc.gpsimd.memset(xT_parts[part][:, :, N:NF].bitcast(F32), 0.0).then_inc(pads, 1)
            pool_eng.wait_ge(pads, 2)
            for m in range(3):
                pool_eng.wait_ge(w_hi, m + 1)
                rest(nc.gpsimd, w[0][m], raw[0][m]).then_inc(w_lo, 1)
            for k in range(KB):
                pool_eng.wait_ge(xt_lo, k + 1)
                nc.gpsimd.tensor_tensor(g.xT[:, k], xT_parts[0][:, k].bitcast(F32), xT_parts[1][:, k].bitcast(F32), ALU.add).then_inc(xt_ready, 1)
            if top2:
                nc.gpsimd.iota(order[:], [[-1, E]], base=E, channel_multiplier=0,
                               allow_small_or_imprecise_dtypes=True).then_inc(order_ready, 1)

            def split_weights(e, s):
                for m in range(3):
                    pool_eng.wait_ge(w_hi, e * 3 + (m + 1))
                    rest(nc.gpsimd, w[s][m], raw[s][m]).then_inc(w_lo, 1)

            split_weights(1, 1)
            with pool_eng.Fori(0, PAIRS - 1) as i:
                split_weights(i * 2 + 2, 0)
                split_weights(i * 2 + 3, 1)
            if not top2:
                deviation(nc, own, g, nth + 1, 1e-5)

        @block.vector
        def _(dve):
            own = Own(dve, vec)
            standardize(nc, own, g, nth, g.x1, g.xn, xn_ready)
            for k in range(KB):
                dve.wait_ge(xt_hi, k + 1)
                for c, at in ((0, slice(0, 4 * R)), (1, slice(4 * R, N))):
                    ins = nc.vector.tensor_tensor(xT_parts[1][:, k, at], fm[k][:, c, 0:at.stop - at.start],
                                                  xT_parts[0][:, k, at].bitcast(F32), ALU.subtract)
                ins.then_inc(xt_lo, 1)

            def split_weights(e, s, m, first=False):
                if not first:
                    dve.wait_ge(*((fm_done, e * 4 + (2 * m - 6)) if m < 2 else (rt_done, e * BANKS - BANKS)))
                dve.wait_ge(w_in[s], (e - s) * 24 + (48 + BEFORE[s]) if not first else 48 + BEFORE[s])
                nc.vector.tensor_copy(w[s][m][0][:], raw[s][m][:]).then_inc(w_hi, 1)

            def hidden_rest(e, m):
                for k in range(KB):
                    dve.wait_ge(fm_free, e * 4 + (2 * m + k + 1))
                    rest(nc.vector, hid_parts[m], hid[m], (slice(None), k)).then_inc(hid_lo, 1)

            hidden_rest(0, 0)
            for m in range(3):
                split_weights(1, 1, m, first=True)
            dve.wait_ge(gate_in, GATE_IN)
            dve.wait_ge(logit_mm, 1)
            own.add(nc.vector.tensor_tensor(logit[:], aux[0:R, 0:T * E].rearrange("p (t e) -> p t e", t=T),
                                            gate_b[:].unsqueeze(1).to_broadcast([R, T, E]), ALU.add))
            own.settle()
            own.add(nc.vector.tensor_reduce(big[:], logit[:], AX.X, ALU.max))
            own.settle()
            nc.vector.tensor_tensor(logit[:], logit[:], big[:].unsqueeze(2).to_broadcast([R, T, E]), ALU.subtract).then_inc(shifted, 1)
            dve.wait_ge(exped, 1)
            own.add(nc.vector.tensor_reduce(sums[:], prob[:], AX.X, ALU.add))
            own.settle()
            own.add(nc.vector.reciprocal(sums[:], sums[:]))
            own.settle()

            def over_experts(x):
                return x[:].unsqueeze(2).to_broadcast([R, T, E])

            def make_gates(source):
                for b in range(BANKS):
                    at = slice(2 * b, min(2 * b + 2, T))
                    nc.vector.tensor_tensor(gate[:, at], source[:, at], sums[:, at].unsqueeze(2).to_broadcast([R, at.stop - at.start, E]),
                                            ALU.mult).then_inc(rt_free, 1)

            if not top2:
                make_gates(prob)
            else:
                own.add(nc.vector.tensor_tensor(prob[:], prob[:], over_experts(sums), ALU.mult))
                own.settle()

                def pick(one, value):
                    own.add(nc.vector.tensor_reduce(value[:], prob[:], AX.X, ALU.max))
                    own.settle()
                    own.add(nc.vector.tensor_tensor(cand[:], prob[:], over_experts(value), ALU.is_equal))
                    own.settle()
                    own.add(nc.vector.tensor_tensor(cand[:], cand[:], order[:].unsqueeze(1).to_broadcast([R, T, E]), ALU.mult))
                    own.settle()
                    own.add(nc.vector.tensor_reduce(big[:], cand[:], AX.X, ALU.max))
                    own.settle()
                    own.add(nc.vector.tensor_tensor(one[:], cand[:], over_experts(big), ALU.is_equal))
                    own.settle()

                dve.wait_ge(order_ready, 1)
                pick(one1, best)
                own.add(nc.vector.scalar_tensor_tensor(prob[:], one1[:], -2.0, prob[:], ALU.mult, ALU.add))
                own.settle()
                pick(one2, second)
                nc.vector.tensor_tensor(second[:], second[:], best[:], ALU.subtract).then_inc(shifted, 1)
                dve.wait_ge(exped, 2)
                own.add(nc.vector.tensor_single_scalar(sums[:], second[:], 1.0, ALU.add))
                own.settle()
                own.add(nc.vector.reciprocal(sums[:], sums[:]))
                own.add(nc.vector.tensor_tensor(one2[:], one2[:], over_experts(second), ALU.mult))
                own.settle()
                own.add(nc.vector.tensor_tensor(one1[:], one1[:], one2[:], ALU.add))
                own.settle()
                make_gates(one1)

            def add_expert(e, first_use=0):
                for b in range(BANKS):
                    dve.wait_ge(rt_done, e * BANKS + (first_use + b + 1))
                    dve.wait_ge(rt_free, e * BANKS + (first_use + b + 1))
                    for t in range(2 * b, min(2 * b + 2, T)):
                        at = t % 2 * D
                        ins = nc.vector.scalar_tensor_tensor(g.x1[:, t], rt[b][0:R, at:at + D], gate[:, t, bass.ds(e, 1)], g.x1[:, t],
                                                             ALU.mult, ALU.add)
                    ins.then_inc(rt_free, 1)
                    if first_use and not top2:
                        dve.wait_ge(rt_free, (E + 1) * BANKS + b + 1)
                        for t in range(2 * b, min(2 * b + 2, T)):
                            tile_moments(nc, own, g, g.x1, t)

            def expert(e, s, more=True, last=False):
                hidden_rest(e, 1)
                if more:
                    split_weights(e + 2, s, 0)
                if not last:
                    hidden_rest(e + 1, 0)
                if more:
                    split_weights(e + 2, s, 1)
                if last:
                    for b in range(BANKS):
                        n = min(2, T - 2 * b)
                        dve.wait_ge(rt_done, e * BANKS + b + 1)
                        dve.wait_ge(rt_free, e * BANKS + b + 1)
                        to = g.x1[:, 2 * b:2 * b + n]
                        nc.vector.tensor_tensor(to, to, rt[b][0:R, 0:n * D].rearrange("p (t d) -> p t d", t=n), ALU.add).then_inc(rt_free, 1)
                add_expert(e, BANKS if last else 0)
                if more:
                    split_weights(e + 2, s, 2)

            with dve.Fori(0, PAIRS - 1) as i:
                expert(i * 2, 0)
                expert(i * 2 + 1, 1)
            expert(E - 2, 0, more=False)
            expert(E - 1, 1, more=False, last=True)
            if not top2:
                all_moments(nc, own, g)

        @block.scalar
        def _(act):
            act.wait_ge(w_in[0], 48 + BEFORE[0])
            for m in range(3):
                nc.scalar.copy(w[0][m][0][:], raw[0][m][:]).then_inc(w_hi, 1)
            for k in range(KB):
                act.wait_ge(xt_mm, k + 1)
                nc.scalar.copy(xT_parts[0][:, k, 0:4 * R], fm[k][:, 0, 0:4 * R])
                nc.scalar.copy(xT_parts[0][:, k, 4 * R:N], fm[k][:, 1, 0:R]).then_inc(xt_hi, 1)
            if top2:
                act.wait_ge(par_mm, 1)
                nc.scalar.copy(par_col[:].rearrange("p m e -> p (m e)"), rt[0][:, 0:2 * KB * E]).then_inc(par_ready, 1)
                act.wait_ge(par_ready, 1)

            def unload(e, m):
                for k in range(KB):
                    act.wait_ge(fm_done, e * 4 + (2 * m + k + 1))
                    at = bass.ds(e + k * E, 1)
                    bias, scale = (par_col[:, m, at], 1.0) if top2 else (g.affine[:, m, 0, at], g.affine[:, m, 1, at])
                    for to, done in ((hid_parts[m][0], hid_hi), (hid[m], fm_free)):
                        nc.scalar.activation(halves(to[:, k]), fm[k][:, :, 0:CH], ACT.Relu,
                                             bias=bias, scale=scale).then_inc(done, 1)

            unload(0, 0)
            act.wait_ge(gate_in, GATE_IN)
            if top2:
                act.wait_ge(rh_mm, 1)
                for c in range(2):
                    ins = nc.scalar.activation(rh[:, c * CH:(c + 1) * CH], rt[c][:, 0:CH], ACT.Relu, bias=gate_b1[:])
                ins.then_inc(rh_ready, 1)
            act.wait_ge(shifted, 1)
            nc.scalar.activation(prob[:], logit[:], ACT.Exp).then_inc(exped, 1)
            if top2:
                act.wait_ge(shifted, 2)
                nc.scalar.activation(second[:], second[:], ACT.Exp).then_inc(exped, 1)
            with act.Fori(0, E - 2) as e:
                unload(e, 1)
                unload(e + 1, 0)
            act.wait_ge(gt_mm, 1)
            nc.scalar.copy(gateT[:, 0:4 * R], aux[0:E, 0:4 * R]).then_inc(gt_ready, 1)
            unload(E - 2, 1)
            unload(E - 1, 0)
            act.wait_ge(gt_mm, 2)
            nc.scalar.copy(gateT[:, 4 * R:N], aux[0:E, 0:R]).then_inc(gt_ready, 1)
            unload(E - 1, 1)

        @block.tensor
        def _(pe):
            for k in range(KB):
                for t in range(T):
                    pe.wait_ge(xn_ready, t + 1)
                    mm = nc.tensor.transpose(fm[k][:, t // 4, t % 4 * R:(t % 4 + 1) * R], g.xn[:, t, k * P:(k + 1) * P], g.ident[0:R, 0:R])
                mm.then_inc(xt_mm, 1)
            if top2:
                pe.wait_ge(par_in, 32)
                for m in range(2):
                    for k in range(KB):
                        at = (m * KB + k) * E
                        mm = nc.tensor.transpose(rt[0][:, at:at + E], par[:, m, k * P:(k + 1) * P], g.ident[0:E, 0:E])
                mm.then_inc(par_mm, 1)

            def hidden(e, m, s, first=False):
                src, src_lo = (xT_parts, xt_lo) if m == 0 else (hid_parts[0], hid_lo)
                for f in range(KB):
                    if first:
                        pe.wait_ge(xt_hi, KB)
                        pe.wait_ge(xt_lo, f + 1)
                    if not first:
                        pe.wait_ge(fm_free, e * 4 + (2 * m + f - 1))
                    for n, (i, j) in enumerate(PASSES):
                        if f == 0 and n == 0:
                            pe.wait_ge(w_hi, e * 3 + (m + 1))
                        elif f == 0 and i:
                            pe.wait_ge(w_lo, e * 3 + (m + 1))
                        for k in range(KB):
                            if f == 0 and m == 1 and n == 0:
                                pe.wait_ge(hid_hi, e * 4 + (k + 1))
                            elif f == 0 and j:
                                pe.wait_ge(src_lo, e * 4 + (k + 1) if m else k + 1)
                            for c in range(2):
                                mm = nc.tensor.matmul(fm[f][:, c, 0:CH], w[s][m][i][:, k, f * P:(f + 1) * P], src[j][:, k, c * CH:(c + 1) * CH],
                                                      start=n == 0 and k == 0, stop=n == 2 and k == KB - 1)
                    mm.then_inc(fm_done, 1)

            def last_layer(e, s, first_use=0):
                pe.wait_ge(hid_lo, e * 4 + 4)
                pe.wait_ge(w_lo, e * 3 + 3)
                for t in range(T):
                    b, at = t // 2, t % 2 * D
                    if t % 2 == 0:
                        pe.wait_ge(rt_free, e * BANKS + (first_use + b + 1))
                    for n, (i, j) in enumerate(PASSES):
                        for k in range(KB):
                            mm = nc.tensor.matmul(rt[b][0:R, at:at + D], hid_parts[1][j][:, k, t * R:(t + 1) * R], w[s][2][i][:, k],
                                                  start=n == 0 and k == 0, stop=n == 2 and k == KB - 1)
                    if t % 2 or t == T - 1:
                        mm.then_inc(rt_done, 1)

            pe.wait_ge(pads, 2)
            hidden(0, 0, 0, first=True)
            pe.wait_ge(gate_in, GATE_IN)
            pe.wait_ge(xt_ready, KB)
            if top2:
                pe.wait_ge(par_ready, 1)
                for k in range(KB):
                    for c in range(2):
                        mm = nc.tensor.matmul(rt[c][:, 0:CH], gate_w[:, k], g.xT[:, k, c * CH:(c + 1) * CH], start=k == 0, stop=k == KB - 1)
                mm.then_inc(rh_mm, 1)
                pe.wait_ge(rh_ready, 1)
                for t in range(T):
                    mm = nc.tensor.matmul(aux[0:R, t * E:(t + 1) * E], rh[:, t * R:(t + 1) * R], gate_w2[:], start=True, stop=True)
            else:
                for t in range(T):
                    for k in range(KB):
                        mm = nc.tensor.matmul(aux[0:R, t * E:(t + 1) * E], g.xT[:, k, t * R:(t + 1) * R], gate_w[:, k], start=k == 0, stop=k == KB - 1)
            mm.then_inc(logit_mm, 1)

            def pair(e):
                hidden(e, 1, 0)
                hidden(e + 1, 0, 1)
                last_layer(e, 0)
                hidden(e + 1, 1, 1)
                hidden(e + 2, 0, 0)
                last_layer(e + 1, 1)

            with pe.Fori(0, PAIRS - 1) as i:
                pair(i * 2)
            for t in range(4):
                mm = nc.tensor.transpose(aux[0:E, t * R:(t + 1) * R], gate[:, t], g.ident[0:R, 0:R])
            mm.then_inc(gt_mm, 1)
            hidden(E - 2, 1, 0)
            hidden(E - 1, 0, 1)
            last_layer(E - 2, 0)
            pe.wait_ge(gt_ready, 1)
            nc.tensor.transpose(aux[0:E, 0:R], gate[:, 4], g.ident[0:R, 0:R]).then_inc(gt_mm, 1)
            hidden(E - 1, 1, 1)
            pe.wait_ge(gt_ready, 2)
            for t in range(T):
                if t % 2 == 0:
                    pe.wait_ge(rt_free, (E - 1) * BANKS + t // 2 + 1)
                mm = nc.tensor.matmul(rt[t // 2][0:R, t % 2 * D:(t % 2 + 1) * D], gateT[:, t * R:(t + 1) * R], b3[:], start=True, stop=True)
                if t % 2 or t == T - 1:
                    mm.then_inc(rt_done, 1)
            last_layer(E - 1, 1, BANKS)


def run_heads(nc, inp, g, nth):
    H, KD = inp["L1_mix_bq"].shape
    SCALE = float(KD) ** -0.25
    EPS = 1e-6 * float(inp["L1_mix_proj"].shape[0]) ** 0.5
    OUT_BANK = (0, 1, 2, 0, 1)
    ROW = D + 2
    UQ, K0, Q0 = 4, 6, 8
    Z0 = BANK - KD
    with ExitStack() as ctx:
        a = Scope(nc, ctx, "heads")
        raw, proj, hb, bo = g.head_raw, g.proj, g.hb, g.bo
        wgt = [a.parts(f"w{m}", [P, KB, D]) for m in range(4)]
        projT = a.parts("projT", [P, KB, KD])
        hb_col = a.sb("hb_col", [P, 3, KB, H])
        minus = a.sb("minus", [P, 1])
        minus_all, ones_all = a.sb("minus_all", [P, P], F32R), a.sb("ones_all", [P, P], F32R)
        xT = a.parts("xT", [P, KB, NF])
        qT, kT = a.sb("qT", [P, KB, NF]), a.sb("kT", [P, KB, NF])
        qT_parts, kT_parts = a.parts("qT", [P, KB, NF]), a.parts("kT", [P, KB, NF])
        q_sq, k_sq = a.sb("q_sq", [P, KB, NF]), a.sb("k_sq", [P, KB, NF])
        q_sum, k_sum, q_sum_parts = a.sb("q_sum", [P, NF]), a.sb("k_sum", [P, NF]), a.parts("q_sum", [P, NF])
        exp_k, exp_q = g.xn, g.xT
        phi_q, phi_k = a.parts("phi_q", [P, KB, NF]), a.parts("phi_k", [R, T, KD])
        sqk = a.sb("sqk", [R, T])
        pxT, kvT = a.parts("pxT", [P, KB, KD]), a.parts("kvT", [P, KB, KD])
        kvT_whole, kvo = a.sb("kvT_whole", [P, KB, KD]), a.parts("kvo", [P, KB, ROW])
        z, z_bias = a.sb("z", [P, KB]), a.sb("z_bias", [P, KB, KD])
        junk = proj[:, 0].rearrange("p (m j) -> p m j", m=KB)
        rec = a.sb("rec", [R, T])
        dinv_diag, dinv_row = k_sum[0:R], a.sb("dinv_row", [R, NF])

        fm = [a.ps(f"fm{i}", [P, 2, BANK]) for i in range(2)]
        rt = [a.ps(f"rt{i}", [P, BANK]) for i in range(3)]
        aux = a.ps("aux", [P, BANK])

        proj_in, bias_in, w_in = g.proj_in, g.bias_in, g.head_w_in
        w_hi, w_lo = [a.sem(f"w_hi{m}") for m in range(4)], [a.sem(f"w_lo{m}") for m in range(4)]
        (xn_ready, xt_mm, xt_hi, xt_lo, consts, proj_mm, proj_hi, proj_lo, hb_mm, hb_ready, fm_done, fm_free, squared, qk_lo,
         summed, aux_done, sqk_ready, uk_done, uk_exp, pk_ready, pq_ready, px_done, px_hi, px_lo, kvt_done,
         kvt_whole, kvt_hi, kvt_lo, z_ready, z_bias_ready, q_sum_ready, kvo_done, kvo_hi, kvo_lo, out_done, out_free, rec_ready, vec, pool, diag_ready, dinv_mm,
         loops_added, adj_ready, adj_hi) = (a.sem(n) for n in (
             "xn_ready", "xt_mm", "xt_hi", "xt_lo", "consts", "proj_mm", "proj_hi", "proj_lo", "hb_mm", "hb_ready",
             "fm_done", "fm_free", "squared", "qk_lo", "summed", "aux_done", "sqk_ready", "uk_done", "uk_exp",
             "pk_ready", "pq_ready", "px_done", "px_hi", "px_lo", "kvt_done", "kvt_whole", "kvt_hi", "kvt_lo", "z_ready", "z_bias_ready", "q_sum_ready", "kvo_done", "kvo_hi",
             "kvo_lo", "out_done", "out_free", "rec_ready", "vec", "pool", "diag_ready", "dinv_mm", "loops_added", "adj_ready", "adj_hi"))
        block = ctx.enter_context(nc.Block())

        @block.sync
        def _(sp):
            with sp.Fori(0, H - 1) as h:
                for m in (WK, WQ, WV, WO):
                    sp.wait_ge(w_lo[m], h + 1)
                    load_head_weights(sp, inp, g, h + 1, m)

        @block.gpsimd
        def _(pool_eng):
            own = Own(pool_eng, pool)
            nc.gpsimd.memset(dinv_diag[:, N:NF], 0.0).then_inc(consts, 1)
            nc.gpsimd.memset(minus[:], -0.5).then_inc(consts, 1)
            nc.gpsimd.memset(minus_all[:].bitcast(F32), -0.5).then_inc(consts, 1)
            nc.gpsimd.memset(ones_all[:].bitcast(F32), 1.0).then_inc(consts, 1)
            for part in range(2):
                nc.gpsimd.memset(xT[part][:, :, N:NF].bitcast(F32), 0.0).then_inc(consts, 1)
                nc.gpsimd.memset(kvo[part][:, :, D + 1:ROW].bitcast(F32), 0.0).then_inc(consts, 1)
            for t in range(T):
                at = slice(t * R, (t + 1) * R)
                nc.gpsimd.tensor_tensor(g.edges[:, t, at], g.edges[:, t, at], g.ident[0:R, 0:R], ALU.add).then_inc(loops_added, 1)

            def weights_low(h, m):
                pool_eng.wait_ge(w_hi[m], h + 1)
                rest(nc.gpsimd, wgt[m], raw[m]).then_inc(w_lo[m], 1)

            def qk_low(h, what, f):
                pool_eng.wait_ge(fm_free, h * 6 + (2 * what + f + 1))
                parts, whole = ((kT_parts, kT), (qT_parts, qT))[what]
                rest(nc.gpsimd, parts, whole, (slice(None), f)).then_inc(qk_lo, 1)

            def next_head(h):
                weights_low(h, WK)
                weights_low(h, WQ)
                weights_low(h, WV)
                qk_low(h, 0, 0)
                qk_low(h, 0, 1)
                weights_low(h, WO)
                qk_low(h, 1, 0)
                qk_low(h, 1, 1)

            weights_low(0, WK)
            weights_low(0, WQ)
            for what in range(2):
                for f in range(KB):
                    qk_low(0, what, f)
            weights_low(0, WV)
            weights_low(0, WO)
            with pool_eng.Fori(0, H - 1) as h:
                next_head(h + 1)
            for t in range(T):
                pool_eng.wait_ge(adj_hi, t + 1)
                rest(nc.gpsimd, g.adj, g.edges, (slice(None), t))

        @block.vector
        def _(dve):
            own = Own(dve, vec)
            standardize(nc, own, g, nth, g.x1, g.xn, xn_ready)
            dve.wait_ge(consts, 8)
            nc.vector.tensor_tensor(dinv_diag[:, 0:N].rearrange("p (t j) -> p t j", t=T),
                                    g.ident[0:R, 0:R].unsqueeze(1).to_broadcast([R, T, R]),
                                    g.deg[:].unsqueeze(2).to_broadcast([R, T, R]), ALU.mult).then_inc(diag_ready, 1)
            for k in range(KB):
                dve.wait_ge(xt_hi, k + 1)
                for c, at in ((0, slice(0, 4 * R)), (1, slice(4 * R, N))):
                    ins = nc.vector.tensor_tensor(xT[1][:, k, at], fm[k][:, c, 0:at.stop - at.start], xT[0][:, k, at].bitcast(F32), ALU.subtract)
                ins.then_inc(xt_lo, 1)
            dve.wait_ge(proj_hi, 1)
            nc.vector.tensor_tensor(projT[1][:].rearrange("p k m -> p (k m)"), rt[0][:],
                                    projT[0][:].rearrange("p k m -> p (k m)").bitcast(F32), ALU.subtract).then_inc(proj_lo, 1)
            dve.wait_ge(dinv_mm, 1)
            for c in range(2):
                nc.vector.tensor_copy(dinv_row[:, c * CH:(c + 1) * CH], rt[1 + c][0:R, 0:CH]).then_inc(dinv_mm, 1)

            def sum_squares(h, what):
                dve.wait_ge(squared, h * 4 + (2 * what + 2))
                sq, to = (k_sq, k_sum) if what == 0 else (q_sq, q_sum)
                nc.vector.tensor_tensor(to[:], sq[:, 0], sq[:, 1], ALU.add).then_inc(summed, 1)
                if what:
                    dve.wait_ge(summed, h * 2 + 2)
                    nc.vector.tensor_copy(q_sum_parts[0][:], q_sum[:]).then_inc(q_sum_ready, 1)
                    dve.wait_ge(q_sum_ready, h * 2 + 1)
                    rest(nc.vector, q_sum_parts, q_sum).then_inc(q_sum_ready, 1)

            sum_squares(0, 0)
            dve.wait_ge(bias_in, 64)
            dve.wait_ge(xn_ready, T)
            for t in range(T):
                nc.vector.tensor_tensor(g.att[:, t], g.xn[:, t], bo[:], ALU.add).then_inc(out_free, 1)
            own.add(nc.vector.tensor_copy(g.xn_parts[0][:], g.xn[:]))
            sum_squares(0, 1)
            own.settle()
            own.add(rest(nc.vector, g.xn_parts, g.xn))
            own.settle()

            def adjacency(t):
                nc.vector.scalar_tensor_tensor(g.edges[:, t], g.edges[:, t], g.deg[:, t:t + 1], dinv_row[:], ALU.mult, ALU.mult).then_inc(adj_ready, 1)

            def head(h, last=False):
                dve.wait_ge(aux_done, h * 2 + 1)
                nc.vector.tensor_copy(sqk[:], aux[0:R, 0:T]).then_inc(sqk_ready, 1)
                dve.wait_ge(uk_exp, h + 1)
                nc.vector.tensor_single_scalar(phi_k[0][:], exp_k[:], EPS, ALU.add).then_inc(pk_ready, 1)
                dve.wait_ge(pk_ready, h * 2 + 1)
                nc.vector.scalar_tensor_tensor(phi_k[1][:], exp_k[:], EPS, phi_k[0][:].bitcast(F32), ALU.add, ALU.subtract).then_inc(pk_ready, 1)
                if last:
                    dve.wait_ge(dinv_mm, 3)
                    dve.wait_ge(loops_added, T)
                    for t in range(3):
                        adjacency(t)
                dve.wait_ge(px_hi, h + 1)
                nc.vector.tensor_tensor(pxT[1][:].rearrange("p k m -> p (k m)"), rt[0][:],
                                        pxT[0][:].rearrange("p k m -> p (k m)").bitcast(F32), ALU.subtract).then_inc(px_lo, 1)
                dve.wait_ge(z_bias_ready, h + 1)
                for m in range(KB):
                    nc.vector.tensor_tensor_reduce(junk[:, m], g.ident[:], aux[:, Z0 + m * P:Z0 + (m + 1) * P], 1.0, 0.0,
                                                   ALU.mult, ALU.add, z[:, m:m + 1]).then_inc(z_ready, 1)
                dve.wait_ge(z_ready, h * 3 + 2)
                nc.vector.tensor_copy(kvo[0][:, :, D], z[:]).then_inc(z_ready, 1)
                dve.wait_ge(z_ready, h * 3 + 3)
                nc.vector.tensor_tensor(kvo[1][:, :, D], z[:], kvo[0][:, :, D].bitcast(F32), ALU.subtract)
                if last:
                    for t in range(3, T):
                        adjacency(t)
                dve.wait_ge(kvt_done, h + 1)
                nc.vector.tensor_tensor(kvT_whole[:], rt[1][:].rearrange("p (k m) -> p k m", k=KB), z_bias[:], ALU.add).then_inc(kvt_whole, 1)
                dve.wait_ge(kvt_whole, h + 1)
                nc.vector.tensor_copy(kvT[0][:], kvT_whole[:]).then_inc(kvt_hi, 1)
                dve.wait_ge(kvt_hi, h + 1)
                rest(nc.vector, kvT, kvT_whole).then_inc(kvt_lo, 1)
                dve.wait_ge(fm_free, h * 6 + (UQ + 2))
                nc.vector.tensor_single_scalar(phi_q[0][:], exp_q[:], EPS, ALU.add).then_inc(pq_ready, 1)
                dve.wait_ge(pq_ready, h * 2 + 1)
                nc.vector.scalar_tensor_tensor(phi_q[1][:], exp_q[:], EPS, phi_q[0][:].bitcast(F32), ALU.add, ALU.subtract).then_inc(pq_ready, 1)
                dve.wait_ge(kvo_done, h + 1)
                nc.vector.tensor_copy(kvo[0][:, :, 0:D], rt[2][:].rearrange("p (k m) -> p k m", k=KB)).then_inc(kvo_hi, 1)
                dve.wait_ge(kvo_hi, h + 1)
                nc.vector.tensor_tensor(kvo[1][:, :, 0:D], rt[2][:].rearrange("p (k m) -> p k m", k=KB),
                                        kvo[0][:, :, 0:D].bitcast(F32), ALU.subtract).then_inc(kvo_lo, 1)
                if not last:
                    sum_squares(h + 1, 0)
                for t in range(T):
                    dve.wait_ge(out_done, h * T + (t + 1))
                    bank = rt[OUT_BANK[t]]
                    nc.vector.reciprocal(rec[:, t:t + 1], bank[0:R, D:D + 1]).then_inc(rec_ready, 1)
                    dve.wait_ge(rec_ready, h * T + (t + 1))
                    dve.wait_ge(out_free, h * T + (t + 1))
                    nc.vector.scalar_tensor_tensor(g.att[:, t], bank[0:R, 0:D], rec[:, t:t + 1], g.att[:, t], ALU.mult, ALU.add).then_inc(out_free, 1)
                if not last:
                    sum_squares(h + 1, 1)

            with dve.Fori(0, H - 1) as h:
                head(h)
            head(H - 1, last=True)

        @block.scalar
        def _(act):
            def weights_high(h, m):
                act.wait_ge(w_in[m], h * 16 + 16)
                nc.scalar.copy(wgt[m][0][:], raw[m][:]).then_inc(w_hi[m], 1)

            weights_high(0, WK)
            weights_high(0, WQ)
            act.wait_ge(proj_mm, 1)
            nc.scalar.copy(projT[0][:].rearrange("p k m -> p (k m)"), rt[0][:]).then_inc(proj_hi, 1)
            act.wait_ge(hb_mm, 1)
            n = 2 * KB * H
            nc.scalar.mul(hb_col[:, 0:2].rearrange("p a k h -> p (a k h)"), aux[:, 0:n], SCALE)
            nc.scalar.copy(hb_col[:, 2].rearrange("p k h -> p (k h)"), aux[:, n:n + KB * H]).then_inc(hb_ready, 1)
            for k in range(KB):
                act.wait_ge(xt_mm, k + 1)
                nc.scalar.copy(xT[0][:, k, 0:4 * R], fm[k][:, 0, 0:4 * R])
                nc.scalar.copy(xT[0][:, k, 4 * R:N], fm[k][:, 1, 0:R]).then_inc(xt_hi, 1)
            act.wait_ge(hb_ready, 1)

            def unload_qk(h, f, what, bf):
                act.wait_ge(fm_done, h * 6 + (2 * what + f + 1))
                sq, parts, whole = ((k_sq, kT_parts, kT), (q_sq, qT_parts, qT))[what]
                bias = hb_col[:, 1 - what, f, bass.ds(bf, 1)]
                for to, fun, done in ((sq, ACT.Square, squared), (parts[0], ACT.Identity, None), (whole, ACT.Identity, fm_free)):
                    ins = nc.scalar.activation(halves(to[:, f]), fm[f][:, :, 0:CH], fun, bias=bias, scale=SCALE)
                    if done:
                        ins.then_inc(done, 1)

            for what in range(2):
                for f in range(KB):
                    unload_qk(0, f, what, 0)
            weights_high(0, WV)
            weights_high(0, WO)

            def features(h, f):
                act.wait_ge(fm_done, h * 6 + (UQ + f + 1))
                nc.scalar.activation(halves(exp_q[:, f]), fm[f][:, :, 0:CH], ACT.Exp).then_inc(fm_free, 1)

            def head(h, last=False):
                if not last:
                    weights_high(h + 1, WK)
                act.wait_ge(sqk_ready, h + 1)
                for b in range(3):
                    act.wait_ge(uk_done, h * 3 + (b + 1))
                    for t in range(2 * b, min(2 * b + 2, T)):
                        ins = nc.scalar.activation(exp_k[:, t], rt[b][0:R, t % 2 * KD:(t % 2 + 1) * KD], ACT.Exp, bias=sqk[:, t:t + 1])
                ins.then_inc(uk_exp, 1)
                features(h, 0)
                if not last:
                    weights_high(h + 1, WQ)
                act.wait_ge(px_done, h + 1)
                nc.scalar.copy(pxT[0][:].rearrange("p k m -> p (k m)"), rt[0][:]).then_inc(px_hi, 1)
                act.wait_ge(aux_done, h * 2 + 2)
                for f in range(KB):
                    ins = nc.scalar.activation(z_bias[:, f], aux[:, Z0:Z0 + KD], ACT.Identity, scale=hb_col[:, 2, f, bass.ds(h, 1)])
                ins.then_inc(z_bias_ready, 1)
                features(h, 1)
                if not last:
                    act.wait_ge(kvt_done, h + 1)
                    weights_high(h + 1, WV)
                    unload_qk(h + 1, 0, 0, h + 1)
                    unload_qk(h + 1, 1, 0, h + 1)
                    act.wait_ge(kvo_done, h + 1)
                    weights_high(h + 1, WO)
                    unload_qk(h + 1, 0, 1, h + 1)
                    unload_qk(h + 1, 1, 1, h + 1)

            with act.Fori(0, H - 1) as h:
                head(h)
            head(H - 1, last=True)
            for t in range(T):
                act.wait_ge(adj_ready, t + 1)
                nc.scalar.copy(g.adj[0][:, t], g.edges[:, t]).then_inc(adj_hi, 1)

        @block.tensor
        def _(pe):
            pe.wait_ge(proj_in, 16)
            for m in range(KB):
                for k in range(KB):
                    mm = nc.tensor.transpose(rt[0][:, k * KD + m * P:k * KD + (m + 1) * P], proj[:, m, k * P:(k + 1) * P], g.ident[:])
            mm.then_inc(proj_mm, 1)
            pe.wait_ge(bias_in, 64)
            for i in range(3):
                for k in range(KB):
                    at = (i * KB + k) * H
                    mm = nc.tensor.transpose(aux[:, at:at + H], hb[:, i, k * P:(k + 1) * P], g.ident[0:H, 0:H])
            mm.then_inc(hb_mm, 1)
            for k in range(KB):
                for t in range(T):
                    pe.wait_ge(xn_ready, t + 1)
                    mm = nc.tensor.transpose(fm[k][:, t // 4, t % 4 * R:(t % 4 + 1) * R], g.xn[:, t, k * P:(k + 1) * P], g.ident[0:R, 0:R])
                mm.then_inc(xt_mm, 1)
            pe.wait_ge(diag_ready, 1)
            for c in range(2):
                mm = nc.tensor.matmul(rt[1 + c][0:R, 0:CH], g.ones[0:R, 0:R], dinv_diag[:, c * CH:(c + 1) * CH], start=True, stop=True)
            mm.then_inc(dinv_mm, 1)

            def project(h, f, m, first=False):
                if not first:
                    pe.wait_ge(fm_free, h * 6 + ((2 if m == WQ else 0) + f - 1))
                if f == 0:
                    pe.wait_ge(w_hi[m], h + 1)
                product(pe, nc, both_halves(fm[f]), KB, lambda i, k: wgt[m][i][:, k, f * P:(f + 1) * P], lambda j, k: xT[j][:, k],
                        left_low=(w_lo[m], h + 1)).then_inc(fm_done, 1)

            def query_features(h, f):
                pe.wait_ge(fm_free, h * 6 + UQ)
                if f:
                    pe.wait_ge(fm_free, h * 6 + (UQ + f - 1))
                product(pe, nc, both_halves(fm[f]), KB, lambda i, k: projT[i][:, k, f * P:(f + 1) * P], lambda j, k: qT_parts[j][:, k],
                        right_low=(qk_lo, h * 4 + 4), more=True)
                pe.wait_ge(q_sum_ready, h * 2 + 2)
                for j in range(2):
                    for to, at in both_halves(fm[f]):
                        mm = nc.tensor.matmul(to, minus_all[:], q_sum_parts[j][:, at], start=False, stop=j == 1)
                mm.then_inc(fm_done, 1)

            whole = slice(0, D)

            def head(h, last=False):
                pe.wait_ge(summed, h * 2 + 1)
                for t in range(T):
                    mm = nc.tensor.matmul(aux[0:R, t:t + 1], k_sum[:, t * R:(t + 1) * R], minus[:, 0:1], start=True, stop=True)
                mm.then_inc(aux_done, 1)
                pe.wait_ge(qk_lo, h * 4 + 2)
                for t in range(T):
                    if t % 2 == 0:
                        pe.wait_ge(out_free, h * T + (4, 5, 3)[t // 2])
                    mm = product(pe, nc, [(rt[t // 2][0:R, t % 2 * KD:(t % 2 + 1) * KD], whole)], KB,
                                 lambda i, k: kT_parts[i][:, k, t * R:(t + 1) * R], lambda j, k: projT[j][:, k])
                    if t % 2 or t == T - 1:
                        mm.then_inc(uk_done, 1)
                query_features(h, 0)
                pe.wait_ge(pk_ready, h * 2 + 1)
                for k in range(KB):
                    mm = product(pe, nc, [(rt[0][:, k * KD:(k + 1) * KD], whole)], T,
                                 lambda i, t: g.xn_parts[i][:, t, k * P:(k + 1) * P], lambda j, t: phi_k[j][:, t],
                                 right_low=(pk_ready, h * 2 + 2))
                mm.then_inc(px_done, 1)
                for j in range(2):
                    for t in range(T):
                        mm = nc.tensor.matmul(aux[:, Z0:Z0 + KD], ones_all[0:R], phi_k[j][:, t], start=j == 0 and t == 0, stop=j == 1 and t == T - 1)
                mm.then_inc(aux_done, 1)
                query_features(h, 1)
                pe.wait_ge(px_lo, h + 1)
                pe.wait_ge(w_lo[WV], h + 1)
                for f in range(KB):
                    mm = product(pe, nc, [(rt[1][:, f * KD:(f + 1) * KD], whole)], KB,
                                 lambda i, k: wgt[WV][i][:, k, f * P:(f + 1) * P], lambda j, k: pxT[j][:, k])
                mm.then_inc(kvt_done, 1)
                if not last:
                    project(h + 1, 0, WK)
                    project(h + 1, 1, WK)
                pe.wait_ge(kvt_lo, h + 1)
                pe.wait_ge(w_lo[WO], h + 1)
                for m in range(KB):
                    mm = product(pe, nc, [(rt[2][:, m * D:(m + 1) * D], whole)], KB,
                                 lambda i, k: kvT[i][:, k, m * P:(m + 1) * P], lambda j, k: wgt[WO][j][:, k])
                mm.then_inc(kvo_done, 1)
                if not last:
                    project(h + 1, 0, WQ)
                pe.wait_ge(kvo_lo, h + 1)
                pe.wait_ge(pq_ready, h * 2 + 2)
                for t in range(T):
                    if t >= 3:
                        pe.wait_ge(out_free, h * T + (T + t - 2))
                    product(pe, nc, [(rt[OUT_BANK[t]][0:R, 0:ROW], slice(0, ROW))], KB,
                            lambda i, k: phi_q[i][:, k, t * R:(t + 1) * R], lambda j, k: kvo[j][:, k]).then_inc(out_done, 1)
                if not last:
                    project(h + 1, 1, WQ)

            pe.wait_ge(xt_lo, KB)
            for m in (WK, WQ):
                for f in range(KB):
                    project(0, f, m, first=m == WK)
            pe.wait_ge(hb_ready, 1)
            pe.wait_ge(proj_lo, 1)
            pe.wait_ge(dinv_mm, 3)
            with pe.Fori(0, H - 1) as h:
                head(h)
            head(H - 1, last=True)


def convolve(nc, inp, g, nth):
    DH = inp["L1_gnn_W2"].shape[0]
    HB = DH // P
    AGG0, AGG1, FF, AGG2, H3 = 0, KB, KB + HB, 2 * KB + HB, 2 * KB + 2 * HB
    WIDE = max(T * DH, HB * NF)
    with ExitStack() as ctx:
        a = Scope(nc, ctx, "conv")
        vecs = a.sb("vecs", [R, 6, D])
        w_ff = [a.sb(f"w_ff{i}", [P, KB, D]) for i in range(2)]
        b_ff = a.sb("b_ff", [P, KB])
        bg, bg3 = a.sb("bg", [R, 2, DH]), a.sb("bg3", [P, HB])
        raw_a, raw_b = a.sb("raw_a", [P, HB, DH]), a.sb("raw_b", [P, HB, D])
        raw = [raw_b[:].rearrange("p (k a) d -> p k (a d)", k=KB), raw_a[:], raw_a[:], raw_b[:]]
        wg = [a.parts("wg1", [P, KB, DH]), a.parts("wg2", [P, HB, DH]), a.parts("wg3", [P, HB, DH]), a.parts("wfc", [P, HB, D])]
        nrm, attT, ffT = g.xn, a.sb("attT", [P, KB, NF]), a.sb("ffT", [P, KB, NF])
        aggT = a.parts("aggT", [P, HB, NF])
        row = a.sb("row", [R, 2, DH])
        hid_all = a.parts("hid", [P, WIDE])
        hid = [x[0:R, 0:T * DH].rearrange("p (t d) -> p t d", t=T) for x in hid_all]
        h3T = [x[:, 0:HB * NF].rearrange("p (k n) -> p k n", k=HB) for x in hid_all]
        h3_whole = g.xT

        fm = [a.ps(f"fm{i}", [P, 2, BANK]) for i in range(2)]
        rt = [a.ps(f"rt{i}", [P, BANK]) for i in range(3)]
        aux = a.ps("aux", [P, BANK])

        ff_in, w_in, bias_in = a.sem("ff_in"), [a.sem(f"w_in{i}") for i in range(4)], a.sem("bias_in")
        fm_done, fm_free = a.sem("fm_done"), [a.sem(f"fm_free{b}") for b in range(2)]
        (zeros, w_hi, w_lo, agg_hi, h3_whole_ready, norm_done, att_ready, at_mm, at_ready, ff_mm,
         row_mm, row_added, row_hi, row_lo, vec, pool) = (a.sem(n) for n in (
             "zeros", "w_hi", "w_lo", "agg_hi", "h3_whole_ready", "norm_done", "att_ready", "at_mm",
             "at_ready", "ff_mm", "row_mm", "row_added", "row_hi", "row_lo", "vec", "pool"))
        block = ctx.enter_context(nc.Block())

        @block.sync
        def _(sp):
            def load(i):
                sp.dma_start(raw[i], inp["L1_gnn_" + ("W1", "W2", "W3", "Wfc")[i]].rearrange("(k p) d -> p k d", p=P)).then_inc(w_in[i], 16)

            load(0)
            for i in range(2):
                sp.dma_start(bg[:, i], spread(inp[f"L1_gnn_b{i + 1}"], R)).then_inc(bias_in, 16)
            sp.dma_start(bg3[:], inp["L1_gnn_b3"].rearrange("(k p) -> p k", p=P), allow_slow_non_contiguous=True).then_inc(bias_in, 16)
            load(1)
            for i, n in enumerate(("mix_g1", "mix_beta1", "mix_bias2", "mix_g2", "mix_beta2", "gnn_bfc")):
                sp.dma_start(vecs[:, i], spread(inp["L1_" + n], R)).then_inc(ff_in, 16)
            sp.dma_start(b_ff[:], inp["L1_mix_bias1"].rearrange("(k p) -> p k", p=P), allow_slow_non_contiguous=True).then_inc(ff_in, 16)
            for i in range(2):
                sp.dma_start(w_ff[i][:], inp[f"L1_mix_W{i + 1}"].rearrange("(k p) d -> p k d", p=P)).then_inc(ff_in, 16)
            sp.wait_ge(w_lo, 1)
            load(3)
            sp.wait_ge(w_lo, 2)
            load(2)
            load_first_weights(sp, inp, g, 1)

        FF_IN, BIAS_IN = 16 * 9, 16 * 3

        @block.gpsimd
        def _(pool_eng):
            own = Own(pool_eng, pool)
            nc.gpsimd.memset(attT[:, :, N:NF], 0.0).then_inc(zeros, 1)
            for i in range(4):
                pool_eng.wait_ge(w_hi, i + 1)
                nc.gpsimd.tensor_tensor(wg[i][1][:], raw[i], wg[i][0][:].bitcast(F32), ALU.subtract).then_inc(w_lo, 1)
                if i == 1:
                    deviation(nc, own, g, nth, 1e-6)
            deviation(nc, own, g, nth + 1, 1e-6)
            deviation(nc, own, g, nth + 2, 1e-5)

        @block.vector
        def _(dve):
            own = Own(dve, vec)
            def agg_low(first, f):
                dve.wait_ge(agg_hi, (first if first < FF else first - KB) + f + 1)
                u = first + f
                nc.vector.tensor_tensor(halves(aggT[1][:, f]), fm[u % 2][:, :, 0:CH], halves(aggT[0][:, f].bitcast(F32)),
                                        ALU.subtract).then_inc(fm_free[u % 2], 1)

            def hidden_rows(layer):
                def low(t):
                    v = T * layer + t
                    dve.wait_ge(row_hi, v + 1)
                    nc.vector.scalar_tensor_tensor(hid[1][:, t], row[:, v % 2], 0.0, hid[0][:, t].bitcast(F32),
                                                   ALU.max, ALU.subtract).then_inc(row_lo, 1)

                for t in range(T):
                    v = T * layer + t
                    dve.wait_ge(row_mm, v + 1)
                    if v >= 2:
                        dve.wait_ge(row_lo, v - 1)
                    nc.vector.tensor_tensor(row[:, v % 2], rt[v % 3][0:R, 0:DH], bg[:, layer], ALU.add).then_inc(row_added, 1)
                    if t:
                        low(t - 1)
                low(T - 1)

            def everywhere(i):
                return vecs[:, i].unsqueeze(1).to_broadcast([R, T, D])

            def affine(n, scale, shift, out, done):
                dve.wait_ge(norm_done, T * (n + 1))
                own.add(nc.vector.tensor_tensor(nrm[:], nrm[:], everywhere(scale), ALU.mult))
                own.settle()
                nc.vector.tensor_tensor(out[:], nrm[:], everywhere(shift), ALU.add).then_inc(done, 1)

            agg_low(AGG0, 0)
            agg_low(AGG0, 1)
            dve.wait_ge(bias_in, BIAS_IN)
            hidden_rows(0)
            agg_low(AGG1, 0)
            moments(nc, own, g, g.att)
            agg_low(AGG1, 1)
            standardize(nc, own, g, nth, g.att, nrm, norm_done)
            agg_low(AGG1, 2)
            dve.wait_ge(ff_in, FF_IN)
            affine(0, 0, 1, g.att, att_ready)
            agg_low(AGG1, 3)
            own.add(nc.vector.tensor_tensor(g.x1[:], g.x1[:], everywhere(5), ALU.add))
            hidden_rows(1)
            dve.wait_ge(at_ready, 3)
            own.add(nc.vector.tensor_tensor(g.att[:], g.att[:], everywhere(2), ALU.add))
            own.settle()
            for f in range(HB):
                agg_low(AGG2, f)
            for b in range(3):
                n = min(2, T - 2 * b)
                dve.wait_ge(ff_mm, b + 1)
                to = g.att[:, 2 * b:2 * b + n]
                nc.vector.tensor_tensor(to, to, aux[0:R, 0:n * D].rearrange("p (t d) -> p t d", t=n), ALU.add).then_inc(att_ready, 1)

            def h3_low(f):
                u = H3 + f
                dve.wait_ge(fm_free[u % 2], u // 2 + 1)
                nc.vector.tensor_tensor(h3T[1][:, f], h3_whole[:, f % 2], h3T[0][:, f].bitcast(F32), ALU.subtract).then_inc(row_lo, 1)

            dve.wait_ge(att_ready, 4)
            moments(nc, own, g, g.att)
            h3_low(0)
            standardize(nc, own, g, nth + 1, g.att, nrm, norm_done)
            h3_low(1)
            affine(1, 3, 4, nrm, att_ready)
            h3_low(2)
            dve.wait_ge(att_ready, 5)
            own.add(nc.vector.tensor_tensor(g.x1[:], g.x1[:], nrm[:], ALU.add))
            h3_low(3)
            own.settle()
            for t in range(T):
                v = 2 * T + t
                dve.wait_ge(row_mm, v + 1)
                nc.vector.tensor_tensor(g.x1[:, t], g.x1[:, t], rt[v % 3][0:R, 0:D], ALU.add).then_inc(row_added, 1)
                dve.wait_ge(row_added, v + 1)
                tile_moments(nc, own, g, g.x1, t)
            all_moments(nc, own, g)

        @block.scalar
        def _(act):
            def weights_high(i):
                act.wait_ge(w_in[i], 16)
                nc.scalar.copy(wg[i][0][:], raw[i]).then_inc(w_hi, 1)

            def agg_high(first, f):
                u = first + f
                act.wait_ge(fm_done, u + 1)
                nc.scalar.copy(halves(aggT[0][:, f]), fm[u % 2][:, :, 0:CH]).then_inc(agg_hi, 1)

            def hidden_high(layer):
                for t in range(T):
                    v = T * layer + t
                    act.wait_ge(row_added, v + 1)
                    nc.scalar.activation(hid[0][:, t], row[:, v % 2], ACT.Relu).then_inc(row_hi, 1)

            agg_high(AGG0, 0)
            weights_high(0)
            agg_high(AGG0, 1)
            weights_high(1)
            hidden_high(0)
            for f in range(HB):
                agg_high(AGG1, f)
            for n in range(3):
                act.wait_ge(at_mm, n + 1)
                if n < 2:
                    nc.scalar.copy(attT[:, n, 0:4 * R], aux[:, 0:4 * R]).then_inc(at_ready, 1)
                else:
                    nc.scalar.copy(attT[:, :, 4 * R:N], aux[:, 0:KB * R].rearrange("p (k j) -> p k j", k=KB)).then_inc(at_ready, 1)
            weights_high(2)
            hidden_high(1)
            act.wait_ge(ff_in, FF_IN)
            for f in range(KB):
                u = FF + f
                act.wait_ge(fm_done, u + 1)
                nc.scalar.activation(halves(ffT[:, f]), fm[u % 2][:, :, 0:CH], ACT.Relu, bias=b_ff[:, f:f + 1]).then_inc(fm_free[u % 2], 1)
            for f in range(HB):
                agg_high(AGG2, f)
            weights_high(3)
            act.wait_ge(bias_in, BIAS_IN)
            for f in range(HB):
                u = H3 + f
                act.wait_ge(fm_done, u + 1)
                if f >= 2:
                    act.wait_ge(row_lo, 2 * T + f - 1)
                for to, done in ((h3_whole[:, f % 2], h3_whole_ready), (h3T[0][:, f], fm_free[u % 2])):
                    nc.scalar.activation(halves(to), fm[u % 2][:, :, 0:CH], ACT.Relu, bias=bg3[:, f:f + 1]).then_inc(done, 1)

        @block.tensor
        def _(pe):
            def next_fm(u):
                if u >= 2:
                    pe.wait_ge(fm_free[u % 2], u // 2)
                return both_halves(fm[u % 2])

            def spread_edges(first, n, src, src_low=()):
                for f in range(n):
                    outs = next_fm(first + f)
                    product(pe, nc, outs, T, lambda i, t: src[i][:, t, f * P:(f + 1) * P], lambda j, t: g.adj[j][:, t],
                            left_low=src_low).then_inc(fm_done, 1)

            def to_rows(layer, blocks, src, w, cols):
                for t in range(T):
                    v = T * layer + t
                    if v >= 3:
                        pe.wait_ge(row_added, v - 2)
                    product(pe, nc, [(rt[v % 3][0:R, 0:cols], slice(0, cols))], blocks,
                            lambda i, k: src[i][:, k, t * R:(t + 1) * R], lambda j, k: w[j][:, k]).then_inc(row_mm, 1)

            def agg_in_parts(end):
                pe.wait_ge(fm_free[(end - 1) % 2], (end + 1) // 2)
                pe.wait_ge(fm_free[end % 2], end // 2)

            spread_edges(AGG0, KB, g.xn_parts)
            agg_in_parts(AGG1)
            pe.wait_ge(w_lo, 1)
            to_rows(0, KB, aggT, wg[0], DH)
            pe.wait_ge(row_hi, T)
            spread_edges(AGG1, HB, hid, (row_lo, T))
            pe.wait_ge(att_ready, 1)
            for n in range(3):
                if n:
                    pe.wait_ge(at_ready, n)
                for j in range(4 if n < 2 else KB):
                    t, k = (j, n) if n < 2 else (4, j)
                    mm = nc.tensor.transpose(aux[:, j * R:(j + 1) * R], g.att[:, t, k * P:(k + 1) * P], g.ident[0:R, 0:R])
                mm.then_inc(at_mm, 1)
            agg_in_parts(FF)
            pe.wait_ge(w_lo, 2)
            to_rows(1, HB, aggT, wg[1], DH)
            pe.wait_ge(zeros, 1)
            pe.wait_ge(at_ready, 3)
            for f in range(KB):
                outs = next_fm(FF + f)
                for k in range(KB):
                    for to, at in outs:
                        mm = nc.tensor.matmul(to, w_ff[0][:, k, f * P:(f + 1) * P], attT[:, k, at], start=k == 0, stop=k == KB - 1)
                mm.then_inc(fm_done, 1)
            pe.wait_ge(row_hi, 2 * T)
            spread_edges(AGG2, HB, hid, (row_lo, 2 * T))
            for b in range(3):
                if b:
                    pe.wait_ge(att_ready, b + 1)
                for t in range(2 * b, min(2 * b + 2, T)):
                    for k in range(KB):
                        mm = nc.tensor.matmul(aux[0:R, t % 2 * D:(t % 2 + 1) * D], ffT[:, k, t * R:(t + 1) * R], w_ff[1][:, k], start=k == 0, stop=k == KB - 1)
                mm.then_inc(ff_mm, 1)
            agg_in_parts(H3)
            pe.wait_ge(w_lo, 3)
            for f in range(HB):
                outs = next_fm(H3 + f)
                product(pe, nc, outs, HB, lambda i, k: wg[2][i][:, k, f * P:(f + 1) * P], lambda j, k: aggT[j][:, k]).then_inc(fm_done, 1)
            pe.wait_ge(row_lo, 2 * T + HB)
            pe.wait_ge(w_lo, 4)
            to_rows(2, HB, h3T, wg[3], D)


def store(nc, g, out):
    with ExitStack() as ctx:
        a = Scope(nc, ctx, "store")
        stored = a.sem("stored")
        block = ctx.enter_context(nc.Block())

        @block.sync
        def _(sp):
            sp.dma_start(rows(out), g.x1[:]).then_inc(stored, 16)
            sp.wait_ge(stored, 16)


def gps_two_layers(nc, inp, out):
    with ExitStack() as ctx:
        g = Shared(Scope(nc, ctx, "g"))
        share_first_weights(g, Scope(nc, ctx, "first"))
        with nc.cleanup_on_exit():
            with ExitStack() as early:
                share_attention(g, Scope(nc, early, "early"))
                count_edges_and_mix(nc, inp, g)
                attend(nc, inp, g)
        with ExitStack() as layer1:
            share_layer1(g, Scope(nc, layer1, "layer1"))
            with ExitStack() as heads:
                share_heads(g, Scope(nc, heads, "first_head"), *inp["L1_mix_bq"].shape)
                run_experts(nc, inp, g, 0, 1)
                run_heads(nc, inp, g, 2)
            convolve(nc, inp, g, 3)
        run_experts(nc, inp, g, 1, 5)
        store(nc, g, out)


def kernel(**inputs):
    import concourse.bacc as bacc
    from concourse.bass_utils import run_bass_kernel_spmd

    nc = bacc.Bacc("TRN2", target_bir_lowering=False, num_devices=1)
    arrays, inp = {}, {}
    for name, value in inputs.items():
        value = np.ascontiguousarray(value)
        arrays[f"in_{name}"] = value
        inp[name] = nc.dram_tensor(f"in_{name}", value.shape, mybir.dt.from_np(value.dtype), kind="ExternalInput").ap()
    out = nc.dram_tensor("out", inputs["x"].shape, F32, kind="ExternalOutput").ap()
    gps_two_layers(nc, inp, out)
    return run_bass_kernel_spmd(nc, [arrays], core_ids=[0]).results[0]["out"]
```
